# Optimizing a Trainium2 kernel written in Bass

```python
import numpy as np
import jax
import jax.numpy as jnp

def _softmax(x, axis=-1):
    return jax.nn.softmax(x, axis=axis)

def _gelu(x):
    return jax.nn.gelu(x, approximate=True)

def _silu(x):
    return jax.nn.silu(x)

def _sigmoid(x):
    return jax.nn.sigmoid(x)

def _layernorm(x, axis=-1, eps=1e-05):
    m = jnp.mean(x, axis=axis, keepdims=True)
    v = jnp.var(x, axis=axis, keepdims=True)
    return (x - m) / jnp.sqrt(v + eps)

def _scatter_add(tgt, idx, src, axis=0):
    return tgt.at[idx].add(src)

def _segment_sum(src, seg, n):
    return jax.ops.segment_sum(src, seg, n)
kernel_name = 'mk_hybrid_d1_jaxref_r8_7beba3'

def setup_inputs(seed: int=0):
    np.random.seed(seed)
    _w = jnp.asarray

    def _L0_attn_a_setup():
        import jax, jax.numpy as jnp
        import numpy as np
        DIM = 128
        HEADS = 16
        DIM_HEAD = 64
        SOFTCAP = 50.0
        key = jax.random.key(seed)
        k1, k2, k3, k4 = jax.random.split(key, 4)
        b, n = (2, 256)
        dim_inner = HEADS * DIM_HEAD
        x = jax.random.normal(k1, (b, n, DIM), dtype=jnp.float32)
        w_qkv = jax.random.normal(k2, (DIM, 3 * dim_inner), dtype=jnp.float32) * 0.02
        w_gates = jax.random.normal(k3, (DIM, HEADS), dtype=jnp.float32) * 0.02
        w_out = jax.random.normal(k4, (dim_inner, DIM), dtype=jnp.float32) * 0.02
        return {'x': x, 'w_qkv': w_qkv, 'w_gates': w_gates, 'w_out': w_out}
    _L0_attn_a_in = _L0_attn_a_setup()

    def _L0_attn_b_setup():
        import jax, jax.numpy as jnp
        import numpy as np
        D_MODEL = 128
        N_HEADS = 16
        D_HEAD = D_MODEL // N_HEADS
        B, L = (2, 256)
        key = jax.random.key(seed)
        ks = jax.random.split(key, 9)
        s = 1.0 / np.sqrt(D_MODEL)
        inp = {'x': jax.random.normal(ks[0], (B, L, D_MODEL), dtype=jnp.float32)}
        for i, name in enumerate(['wq', 'wk', 'wv', 'wo']):
            inp[name + '_w'] = jax.random.normal(ks[1 + 2 * i], (D_MODEL, D_MODEL), dtype=jnp.float32) * s
            inp[name + '_b'] = jax.random.normal(ks[2 + 2 * i], (D_MODEL,), dtype=jnp.float32) * 0.01
        return inp
    _L0_attn_b_in = _L0_attn_b_setup()

    def _L0_ffn_setup():
        import jax, jax.numpy as jnp
        import numpy as np
        B, S, H, I, E_ROUTED, TOP_K = (8, 256, 128, 256, 8, 2)

        def _expert(x, Wg, Wu, Wd):
            return jax.nn.silu(x @ Wg.T) * (x @ Wu.T) @ Wd.T
        key = jax.random.key(seed)
        ks = jax.random.split(key, 9)
        s = 0.02
        return {'x': jax.random.normal(ks[0], (B, S, H), dtype=jnp.float32), 'Wg_s': jax.random.normal(ks[1], (I, H), dtype=jnp.float32) * s, 'Wu_s': jax.random.normal(ks[2], (I, H), dtype=jnp.float32) * s, 'Wd_s': jax.random.normal(ks[3], (H, I), dtype=jnp.float32) * s, 'Wg': jax.random.normal(ks[4], (E_ROUTED, I, H), dtype=jnp.float32) * s, 'Wu': jax.random.normal(ks[5], (E_ROUTED, I, H), dtype=jnp.float32) * s, 'Wd': jax.random.normal(ks[6], (E_ROUTED, H, I), dtype=jnp.float32) * s, 'Wr': jax.random.normal(ks[7], (E_ROUTED, H), dtype=jnp.float32) * s, 'rb': jnp.zeros((E_ROUTED,), dtype=jnp.float32)}
    _L0_ffn_in = _L0_ffn_setup()
    _d = {'L0_attn_a_x': _L0_attn_a_in['x'], 'L0_attn_a_w_qkv': _L0_attn_a_in['w_qkv'], 'L0_attn_a_w_gates': _L0_attn_a_in['w_gates'], 'L0_attn_a_w_out': _L0_attn_a_in['w_out'], 'L0_attn_b_wq_w': _L0_attn_b_in['wq_w'], 'L0_attn_b_wq_b': _L0_attn_b_in['wq_b'], 'L0_attn_b_wk_w': _L0_attn_b_in['wk_w'], 'L0_attn_b_wk_b': _L0_attn_b_in['wk_b'], 'L0_attn_b_wv_w': _L0_attn_b_in['wv_w'], 'L0_attn_b_wv_b': _L0_attn_b_in['wv_b'], 'L0_attn_b_wo_w': _L0_attn_b_in['wo_w'], 'L0_attn_b_wo_b': _L0_attn_b_in['wo_b'], 'L0_ffn_Wg_s': _L0_ffn_in['Wg_s'], 'L0_ffn_Wu_s': _L0_ffn_in['Wu_s'], 'L0_ffn_Wd_s': _L0_ffn_in['Wd_s'], 'L0_ffn_Wg': _L0_ffn_in['Wg'], 'L0_ffn_Wu': _L0_ffn_in['Wu'], 'L0_ffn_Wd': _L0_ffn_in['Wd'], 'L0_ffn_Wr': _L0_ffn_in['Wr'], 'L0_ffn_rb': _L0_ffn_in['rb']}
    _x0 = _d['L0_attn_a_x']
    _d['L0_attn_a_x'] = jax.random.normal(jax.random.fold_in(jax.random.key(seed), 1), (1, 2048, 128), dtype=_x0.dtype)
    del _x0
    return _d

def reference(L0_attn_a_x, L0_attn_a_w_qkv, L0_attn_a_w_gates, L0_attn_a_w_out, L0_attn_b_wq_w, L0_attn_b_wq_b, L0_attn_b_wk_w, L0_attn_b_wk_b, L0_attn_b_wv_w, L0_attn_b_wv_b, L0_attn_b_wo_w, L0_attn_b_wo_b, L0_ffn_Wg_s, L0_ffn_Wu_s, L0_ffn_Wd_s, L0_ffn_Wg, L0_ffn_Wu, L0_ffn_Wd, L0_ffn_Wr, L0_ffn_rb):

    def _L0_attn_a_ref(x, w_qkv, w_gates, w_out):
        import jax, jax.numpy as jnp
        import numpy as np
        DIM = 128
        HEADS = 16
        DIM_HEAD = 64
        SOFTCAP = 50.0
        b, n, _ = x.shape
        scale = DIM_HEAD ** (-0.5)
        qkv = jnp.einsum('bnf,fe->bne', x, w_qkv).reshape(b, n, 3, HEADS, DIM_HEAD)
        qkv = jnp.moveaxis(qkv, 2, 0)
        q, k, v = jnp.moveaxis(qkv, 3, 2)
        q = q * scale
        sim = jnp.einsum('bhid,bhjd->bhij', q, k)
        sim = SOFTCAP * jnp.tanh(sim / SOFTCAP)
        mask_value = -jnp.finfo(sim.dtype).max
        causal_mask = jnp.triu(jnp.ones((n, n), dtype=bool), 1)
        sim = jnp.where(causal_mask, mask_value, sim)
        attn = jax.nn.softmax(sim, axis=-1)
        out = jnp.einsum('bhij,bhjd->bhid', attn, v)
        gates = jax.nn.sigmoid(jnp.einsum('bnf,fh->bhn', x, w_gates))[..., None]
        out = out * gates
        out = jnp.transpose(out, (0, 2, 1, 3)).reshape(b, n, HEADS * DIM_HEAD)
        return jnp.einsum('bne,ef->bnf', out, w_out)

    def _L0_attn_b_ref(x, wq_w, wq_b, wk_w, wk_b, wv_w, wv_b, wo_w, wo_b):
        import jax, jax.numpy as jnp
        import numpy as np
        D_MODEL = 128
        N_HEADS = 16
        D_HEAD = D_MODEL // N_HEADS
        B, L = (2, 256)
        b, l, d = x.shape
        h, dh = (N_HEADS, D_HEAD)

        def proj(w, bias):
            return (jnp.einsum('bld,ed->ble', x, w) + bias).reshape(b, l, h, dh).transpose(0, 2, 1, 3)
        Q, K, V = (proj(wq_w, wq_b), proj(wk_w, wk_b), proj(wv_w, wv_b))
        scores = jnp.einsum('bhld,bhsd->bhls', Q, K)
        causal = jnp.tril(jnp.ones((l, l), dtype=scores.dtype))
        out = jnp.einsum('bhls,bhsd->bhld', scores * causal, V)
        out = out.transpose(0, 2, 1, 3).reshape(b, l, d)
        return jnp.einsum('bld,ed->ble', out, wo_w) + wo_b

    def _L0_ffn_ref(x, Wg_s, Wu_s, Wd_s, Wg, Wu, Wd, Wr, rb):
        import jax, jax.numpy as jnp
        import numpy as np
        B, S, H, I, E_ROUTED, TOP_K = (8, 256, 128, 256, 8, 2)

        def _expert(x, Wg, Wu, Wd):
            return jax.nn.silu(x @ Wg.T) * (x @ Wu.T) @ Wd.T
        shared = _expert(x, Wg_s, Wu_s, Wd_s)
        logits = jnp.einsum('bsh,eh->bse', x, Wr) + rb
        probs = jax.nn.sigmoid(logits)
        scores, idx = jax.lax.top_k(probs, TOP_K)
        cw = (jax.nn.one_hot(idx, E_ROUTED, dtype=x.dtype) * scores[..., None]).sum(-2)
        out = shared
        for e in range(E_ROUTED):
            out = out + cw[..., e:e + 1] * _expert(x, Wg[e], Wu[e], Wd[e])
        return out
    x = L0_attn_a_x
    x = x + _L0_attn_a_ref(_layernorm(x, axis=-1), L0_attn_a_w_qkv, L0_attn_a_w_gates, L0_attn_a_w_out)
    x = x + _L0_ffn_ref(_layernorm(x, axis=-1), L0_ffn_Wg_s, L0_ffn_Wu_s, L0_ffn_Wd_s, L0_ffn_Wg, L0_ffn_Wu, L0_ffn_Wd, L0_ffn_Wr, L0_ffn_rb)
    x = x + _L0_attn_b_ref(_layernorm(x, axis=-1), L0_attn_b_wq_w, L0_attn_b_wq_b, L0_attn_b_wk_w, L0_attn_b_wk_b, L0_attn_b_wv_w, L0_attn_b_wv_b, L0_attn_b_wo_w, L0_attn_b_wo_b)
    x = x + _L0_ffn_ref(_layernorm(x, axis=-1), L0_ffn_Wg_s, L0_ffn_Wu_s, L0_ffn_Wd_s, L0_ffn_Wg, L0_ffn_Wu, L0_ffn_Wd, L0_ffn_Wr, L0_ffn_rb)
    return x

_drawn_inputs = setup_inputs


def setup_inputs(seed=0):
    import zlib

    import numpy as np

    out = dict(_drawn_inputs(seed))
    spreads = {'L0_ffn_rb': (0.0, 0.8)}
    factors = {'L0_attn_a_w_qkv': 8.0,
     'L0_attn_a_w_gates': 8.0,
     'L0_attn_a_w_out': 8.0,
     'L0_attn_b_wq_b': 5.747,
     'L0_attn_b_wk_b': 8.0,
     'L0_attn_b_wv_b': 8.0,
     'L0_attn_b_wo_b': 8.0,
     'L0_ffn_Wg_s': 6.197,
     'L0_ffn_Wu_s': 5.984,
     'L0_ffn_Wd_s': 5.981,
     'L0_ffn_Wg': 7.893,
     'L0_ffn_Wu': 7.782,
     'L0_ffn_Wd': 7.804,
     'L0_ffn_Wr': 8.0}
    for name, (base, spread) in spreads.items():
        noise = np.random.default_rng([zlib.crc32(name.encode()), seed]).standard_normal(out[name].shape)
        drawn = base * np.exp(spread * noise) if base else spread * noise
        out[name] = jnp.asarray(drawn.astype(out[name].dtype))
    for name, factor in factors.items():
        out[name] = (out[name] * factor).astype(out[name].dtype)
    return out
```

```python
from contextlib import ExitStack

import concourse.bass as bass
from concourse import mybir

F32 = mybir.dt.float32
F32R = mybir.dt.float32r
ACT = mybir.ActivationFunctionType
ALU = mybir.AluOpType
AX = mybir.AxisListType

P = 128
T = 2048
BLK = 512
NB = T // BLK
NT = T // P
EPS = 1e-5

H = 16
DH = 64
PAIRS = H // 2
SOFTCAP = 50.0
KT_PER_BLK = BLK // P
STEPS = [(qb, j) for qb in range(NB) for j in range(KT_PER_BLK * (qb + 1))]
NS = len(STEPS)
DIAG = [j >= KT_PER_BLK * qb for qb, j in STEPS]
ND = sum(DIAG)
LAST = [max(n for n in range(NS) if STEPS[n][0] == qb) for qb in range(NB)]
UNITS = 4 * NB
RING = 4


def blk(b, n=BLK):
    return slice(b * n, (b + 1) * n)


class Semaphores:

    def __init__(self, nc, ctx):
        self.nc, self.ctx, self.of = nc, ctx, {}

    def __call__(self, part, name):
        if (part, name) not in self.of:
            self.of[part, name] = self.ctx.enter_context(self.nc.semaphore(f"{part}_{name}"))
        return self.of[part, name]

    def clear(self, *parts):
        with self.nc.Block() as block:
            @block.gpsimd
            def _(pool):
                for (part, _), semaphore in self.of.items():
                    if part in parts:
                        pool.sem_clear(semaphore)


def wait(eng, semaphore, value):
    if not isinstance(value, int) or value > 0:
        eng.wait_ge(semaphore, value)


def layer_norm(nc, sems, x, xn, x_hi, x_lo, name):
    with ExitStack() as ctx:
        sb = lambda n, s, d=F32: ctx.enter_context(nc.sbuf_tensor(f"{name}_{n}", s, d))
        sem = lambda n: sems("ln", n)
        mean_of = sb("mean_of", [P, P])
        eps = sb("eps", [P, 1])
        centred = sb("centred", [P, T])
        squared = sb("squared", [P, T])
        std = sb("std", [P, T])
        rstd = sb("rstd", [P, T])
        mean = ctx.enter_context(nc.psum_tensor(f"{name}_mean", [P, NB, BLK], F32))
        var = ctx.enter_context(nc.psum_tensor(f"{name}_var", [P, NB, BLK], F32))
        const_ready, mean_ready, centred_ready = sem("const_ready"), sem("mean_ready"), sem("centred_ready")
        squared_ready, var_ready, std_ready = sem("squared_ready"), sem("var_ready"), sem("std_ready")
        rstd_ready, xn_ready, hi_ready = sem("rstd_ready"), sem("xn_ready"), sem("hi_ready")
        block = ctx.enter_context(nc.Block())

        @block.gpsimd
        def _(pool):
            nc.gpsimd.memset(mean_of[:], 1.0 / P).then_inc(const_ready, 1)
            nc.gpsimd.memset(eps[:], EPS).then_inc(const_ready, 1)

        @block.tensor
        def _(pe):
            pe.wait_ge(const_ready, 2)
            for b in range(NB):
                nc.tensor.matmul(mean[:, b], mean_of[:], x[:, blk(b)], start=True, stop=True).then_inc(mean_ready, 1)
            for b in range(NB):
                pe.wait_ge(squared_ready, b + 1)
                nc.tensor.matmul(var[:, b], mean_of[:], squared[:, blk(b)], start=True, stop=True).then_inc(var_ready, 1)

        @block.scalar
        def _(act):
            act.wait_ge(const_ready, 2)
            for b in range(NB):
                act.wait_ge(centred_ready, b + 1)
                nc.scalar.activation(squared[:, blk(b)], centred[:, blk(b)], ACT.Square).then_inc(squared_ready, 1)
            for b in range(NB):
                act.wait_ge(var_ready, b + 1)
                nc.scalar.activation(std[:, blk(b)], var[:, b], ACT.Sqrt, bias=eps[:, 0:1]).then_inc(std_ready, 1)
            for b in range(NB):
                act.wait_ge(xn_ready, b + 1)
                nc.scalar.copy(x_hi[:, blk(b)], xn[:, blk(b)]).then_inc(hi_ready, 1)

        @block.vector
        def _(dve):
            for b in range(NB):
                dve.wait_ge(mean_ready, b + 1)
                nc.vector.tensor_tensor(centred[:, blk(b)], x[:, blk(b)], mean[:, b], ALU.subtract).then_inc(centred_ready, 1)
            for b in range(NB):
                dve.wait_ge(std_ready, b + 1)
                nc.vector.reciprocal(rstd[:, blk(b)], std[:, blk(b)]).then_inc(rstd_ready, 1)
                dve.wait_ge(rstd_ready, b + 1)
                nc.vector.tensor_tensor(xn[:, blk(b)], centred[:, blk(b)], rstd[:, blk(b)], ALU.mult).then_inc(xn_ready, 1)
                if b > 0:
                    dve.wait_ge(hi_ready, b)
                    nc.vector.tensor_tensor(x_lo[:, blk(b - 1)], xn[:, blk(b - 1)], x_hi[:, blk(b - 1)].bitcast(F32), ALU.subtract)
            dve.wait_ge(hi_ready, NB)
            nc.vector.tensor_tensor(x_lo[:, blk(NB - 1)], xn[:, blk(NB - 1)], x_hi[:, blk(NB - 1)].bitcast(F32), ALU.subtract)


def values_and_gates(nc, sems, xn, x_hi, x_lo, w_qkv, w_gates, v_dram, gate_dram):
    VD = H * DH
    HALF = VD // 2
    RV = 4
    NPS = 6
    with ExitStack() as ctx:
        sb = lambda n, s, d=F32: ctx.enter_context(nc.sbuf_tensor(f"vg_{n}", s, d))
        sem = lambda n: sems("vg", n)
        wv = sb("wv", [P, VD])
        wv_hi = sb("wv_hi", [P, VD], F32R)
        wv_lo = sb("wv_lo", [P, VD], F32R)
        wg = sb("wg", [P, H])
        v_tile = sb("v_tile", [P, RV, VD])
        gate = sb("gate", [H, T])
        v_ps = ctx.enter_context(nc.psum_tensor("vg_v_ps", [P, NPS, BLK], F32))
        g_ps = ctx.enter_context(nc.psum_tensor("vg_g_ps", [H, 2, BLK], F32))
        w_loaded, wg_loaded, hi_ready, split_ready = sem("w_loaded"), sem("wg_loaded"), sem("hi_ready"), sem("split_ready")
        v_computed, v_copied_act, v_copied_dve = sem("v_computed"), sem("v_copied_act"), sem("v_copied_dve")
        g_computed, g_ready, stored = sem("g_computed"), sem("g_ready"), sem("stored")
        v_stored = [sem(f"v_stored{i}") for i in range(RV)]
        block = ctx.enter_context(nc.Block())

        @block.sync
        def _(sp):
            sp.dma_start(wv[:], w_qkv[:, 2 * VD:3 * VD]).then_inc(w_loaded, 16)
            sp.dma_start(wg[:], w_gates).then_inc(wg_loaded, 16)
            for t in range(NT):
                sp.wait_ge(v_copied_act, t + 1)
                sp.wait_ge(v_copied_dve, t + 1)
                sp.dma_start(v_dram[:, :, t, :].rearrange("a p d -> p a d"),
                             v_tile[:, t % RV].rearrange("p (a d) -> p a d", a=PAIRS)).then_inc(v_stored[t % RV], 16)
            sp.wait_ge(g_ready, NB)
            sp.dma_start(gate_dram.rearrange("a h t -> (a h) t"), gate[:]).then_inc(stored, 16)
            for stored_of in v_stored:
                sp.wait_ge(stored_of, 16 * NT // RV)
            sp.wait_ge(stored, 16)

        @block.tensor
        def _(pe):
            pe.wait_ge(split_ready, 1)
            for t in range(NT):
                for half in range(2):
                    n = 2 * t + half
                    if n >= NPS:
                        pe.wait_ge(v_copied_act if half == 0 else v_copied_dve, (n - NPS) // 2 + 1)
                    out, cols = v_ps[:, n % NPS], blk(half, HALF)
                    nc.tensor.matmul(out, x_hi[:, blk(t, P)], wv_hi[:, cols], start=True, stop=False)
                    nc.tensor.matmul(out, x_hi[:, blk(t, P)], wv_lo[:, cols], start=False, stop=False)
                    nc.tensor.matmul(out, x_lo[:, blk(t, P)], wv_hi[:, cols], start=False, stop=True).then_inc(v_computed, 1)
            pe.wait_ge(wg_loaded, 16)
            for b in range(NB):
                if b >= 2:
                    pe.wait_ge(g_ready, b - 1)
                nc.tensor.matmul(g_ps[:, b % 2], wg[:], xn[:, blk(b)], start=True, stop=True).then_inc(g_computed, 1)

        @block.scalar
        def _(act):
            for t in range(NT):
                act.wait_ge(v_computed, 2 * t + 1)
                if t >= RV:
                    act.wait_ge(v_stored[t % RV], 16 * (t // RV))
                nc.scalar.copy(v_tile[:, t % RV, 0:HALF], v_ps[:, (2 * t) % NPS]).then_inc(v_copied_act, 1)
            for b in range(NB):
                act.wait_ge(g_computed, b + 1)
                nc.scalar.activation(gate[:, blk(b)], g_ps[:, b % 2], ACT.Sigmoid).then_inc(g_ready, 1)

        @block.vector
        def _(dve):
            dve.wait_ge(w_loaded, 16)
            nc.vector.tensor_copy(wv_hi[:], wv[:]).then_inc(hi_ready, 1)
            dve.wait_ge(hi_ready, 1)
            nc.vector.tensor_tensor(wv_lo[:], wv[:], wv_hi[:].bitcast(F32), ALU.subtract).then_inc(split_ready, 1)
            for t in range(NT):
                dve.wait_ge(v_computed, 2 * t + 2)
                if t >= RV:
                    dve.wait_ge(v_stored[t % RV], 16 * (t // RV))
                nc.vector.tensor_copy(v_tile[:, t % RV, HALF:VD], v_ps[:, (2 * t + 1) % NPS]).then_inc(v_copied_dve, 1)


def softcap_attention(nc, sems, x_hi, x_lo, w_qkv, v_dram, gate_dram, den_dram, factor_dram, o_dram):
    WQK = 4 * P
    PROJ_AT = {4 + 2 * u: u for u in range(UNITS)}
    DEN_AT = {LAST[qb] + 3: qb for qb in range(NB - 1)}
    OUT_AT = {LAST[qb] + 1: qb for qb in range(NB - 1)}
    SPLIT_AT, FACTOR_AT, NORM_AT = 2, 5, 12
    NW = 4
    with ExitStack() as ctx:
        sb = lambda n, s, d=F32: ctx.enter_context(nc.sbuf_tensor(f"at_{n}", s, d))
        psum = lambda n, s: ctx.enter_context(nc.psum_tensor(f"at_{n}", s, F32))
        sem = lambda n: sems("at", n)
        w_raw = sb("w_raw", [P, WQK])
        w_hi = sb("w_hi", [P, WQK], F32R)
        w_lo = sb("w_lo", [P, WQK], F32R)
        q_hi = [[sb(f"q_hi{a}{h}", [P, T], F32R) for h in range(2)] for a in range(2)]
        q_lo = [[sb(f"q_lo{a}{h}", [P, T], F32R) for h in range(2)] for a in range(2)]
        k_hl = [[sb(f"k_hl{a}{h}", [P, T], F32R) for h in range(2)] for a in range(2)]
        v = [sb(f"v{a}", [P, NT, P]) for a in range(2)]
        capped = sb("capped", [P, 2, 2, BLK])
        probs = sb("probs", [P, RING, 2, BLK])
        psums = [sb(f"psums{a}", [P, 2, BLK]) for a in range(2)]
        ones = sb("ones", [P, 32])
        causal = sb("causal", [P, 2, P])
        den_row = sb("den_row", [2 * 32, 2, BLK])
        out_t = [sb(f"out_t{a}", [P, T]) for a in range(2)]
        factor_b = sb("factor_b", [P, T])
        den_r = sb("den_r", [P, 2 * T // P])
        gate_r = sb("gate_r", [P, 2 * T // P])
        rden = sb("rden", [P, 2 * T // P])
        factor = sb("factor", [P, 2 * T // P])
        scores = psum("scores", [P, 2, 2, BLK])
        o_ps = psum("o_ps", [P, 2, BLK])
        proj_ps = psum("proj_ps", [P, BLK])
        den_ps = psum("den_ps", [2 * 32, BLK])

        init_ready = sem("init_ready")
        w_loaded, w_hi_ready, w_split = sem("w_loaded"), sem("w_hi_ready"), sem("w_split")
        proj_computed, proj_hi_ready, proj_ready = sem("proj_computed"), sem("proj_hi_ready"), sem("proj_ready")
        v_loaded = sem("v_loaded")
        scores_ready, tanh_done, exp_done, masked = sem("scores_ready"), sem("tanh_done"), sem("exp_done"), sem("masked")
        pv_done, summed, out_copied = sem("pv_done"), sem("summed"), sem("out_copied")
        den_computed, den_copied = sem("den_computed"), sem("den_copied")
        den_stored = [sem(f"den_stored{i}") for i in range(2)]
        den_loaded, rden_ready, factor_ready = sem("den_loaded"), sem("rden_ready"), sem("factor_ready")
        factor_stored, factor_loaded, normed, out_stored = sem("factor_stored"), sem("factor_loaded"), sem("normed"), sem("out_stored")
        block = ctx.enter_context(nc.Block())

        def run_pairs(eng, pair):
            pair(0, 0, False)
            pair(1, 1, False)
            with eng.Fori(1, PAIRS // 2 - 1) as i:
                pair(i * 2, 0, False)
                pair(i * 2 + 1, 1, False)
            pair(PAIRS - 2, 0, False)
            pair(PAIRS - 1, 1, True)

        def is_first(p):
            return isinstance(p, int) and p == 0

        def queries(n):
            qb, j = STEPS[n]
            first = max(qb * BLK, j * P)
            return first, (qb + 1) * BLK - first, first - qb * BLK

        @block.sync
        def _(sp):
            def load_weights(p):
                for which in range(2):
                    for twice in range(2):
                        dst = w_raw[:].rearrange("p (w h c d) -> p w h c d", w=2, h=2, c=2)[:, which, :, twice]
                        src = w_qkv[:, bass.ds(p * P + which * H * DH, P)].rearrange("p (h d) -> p h d", h=2)
                        sp.dma_start(dst, src).then_inc(w_loaded, 16)

            def load_values(p, a):
                sp.dma_start(v[a][:], v_dram[bass.ds(p, 1)].rearrange("a p t d -> (a p) t d")).then_inc(v_loaded, 16)

            def factors(p, before):
                for stored in den_stored:
                    sp.wait_ge(stored, p * (16 * NB // 2))
                shape = dict(c=2 * T // P)
                sp.dma_start(den_r[:], den_dram[bass.ds(before, 1)].rearrange("a h (p c) -> (a h p) c", **shape)).then_inc(den_loaded, 16)
                sp.dma_start(gate_r[:], gate_dram[bass.ds(before, 1)].rearrange("a h (p c) -> (a h p) c", **shape)).then_inc(den_loaded, 16)
                wait(sp, out_stored, (p - 1) * 16)
                sp.wait_ge(factor_ready, p)
                sp.dma_start(factor_dram.rearrange("h (p c) -> (h p) c", **shape), factor[:]).then_inc(factor_stored, 16)
                sp.wait_ge(factor_stored, p * 16)
                for h in range(2):
                    sp.dma_start(factor_b[h * DH:(h + 1) * DH, :], factor_dram[h:h + 1].broadcast_to([DH, T])).then_inc(factor_loaded, 16)

            def store_outputs(p, before):
                sp.wait_ge(normed, p)
                sp.dma_start(o_dram[bass.ds(before, 1)].rearrange("a p t -> (a p) t"), factor_b[:]).then_inc(out_stored, 16)

            def store_denominators(p, qb):
                sp.wait_ge(den_copied, p * NB + qb + 1)
                sp.dma_start(den_dram[bass.ds(p, 1), :, blk(qb)].rearrange("a h t -> (a h) t"),
                             den_row[0:33:32, qb % 2]).then_inc(den_stored[qb % 2], 16)

            def pair(p, a, last):
                before = p - 1
                if not last:
                    sp.wait_ge(w_split, p + 1)
                    load_weights(p + 1)
                    wait(sp, pv_done, p * NS)
                    sp.wait_ge(v_loaded, p * 16 + 16)
                    load_values(p + 1, 1 - a)
                if not is_first(p):
                    factors(p, before)
                store_denominators(p, 0)
                if not is_first(p):
                    store_outputs(p, before)
                for qb in range(1, NB):
                    store_denominators(p, qb)

            load_weights(0)
            load_values(0, 0)
            run_pairs(sp, pair)
            factors(PAIRS, PAIRS - 1)
            store_outputs(PAIRS, PAIRS - 1)
            sp.wait_ge(out_stored, 16 * PAIRS)
            sp.wait_ge(factor_stored, 16 * PAIRS)
            for stored in den_stored:
                sp.wait_ge(stored, 16 * NB // 2 * PAIRS)

        @block.tensor
        def _(pe):
            def scores_of(g, a, n):
                first, width, _ = queries(n)
                wait(pe, tanh_done, g - 1)
                for h in range(2):
                    keys = k_hl[a][h][:, blk(STEPS[n][1], P)]
                    out = scores[:, n % 2, h, 0:width]
                    nc.tensor.matmul(out, keys, q_hi[a][h][:, first:first + width], start=True, stop=False)
                    last = nc.tensor.matmul(out, keys, q_lo[a][h][:, first:first + width], start=False, stop=True)
                last.then_inc(scores_ready, 1)

            def outputs_of(p, g, a, n):
                qb, j = STEPS[n]
                _, width, at = queries(n)
                if DIAG[n]:
                    pe.wait_ge(masked, p * ND + sum(DIAG[:n]) + 1)
                else:
                    pe.wait_ge(exp_done, g + 1)
                if j == 0:
                    wait(pe, out_copied, p * NB + qb - 1)
                for h in range(2):
                    last = nc.tensor.matmul(o_ps[h * DH:(h + 1) * DH, qb % 2, at:BLK], v[a][:, j, h * DH:(h + 1) * DH],
                                            probs[:, n % RING, h, 0:width], start=(j == 0), stop=(n == LAST[qb]),
                                            skip_group_check=True)
                last.then_inc(pv_done, 1)

            def project(count, u):
                w, b = u // NB, u % NB
                wait(pe, proj_ready, count)
                cols, xs = blk(w, P), blk(b)
                nc.tensor.matmul(proj_ps[:], w_hi[:, cols], x_hi[:, xs], start=True, stop=False)
                nc.tensor.matmul(proj_ps[:], w_hi[:, cols], x_lo[:, xs], start=False, stop=False)
                nc.tensor.matmul(proj_ps[:], w_lo[:, cols], x_hi[:, xs], start=False, stop=True).then_inc(proj_computed, 1)

            def denominators(p, qb):
                pe.wait_ge(summed, p * NS + LAST[qb] + 1)
                wait(pe, den_copied, p * NB + qb)
                for h in range(2):
                    last = nc.tensor.matmul(den_ps[h * 32:(h + 1) * 32], ones[:], psums[qb % 2][:, h], start=True, stop=True)
                last.then_inc(den_computed, 1)

            def pair(p, a, last):
                for n in range(NS):
                    g = p * NS + n
                    if n + 2 < NS:
                        scores_of(g + 2, a, n + 2)
                    elif not last:
                        if n + 2 == NS:
                            pe.wait_ge(proj_ready, (p + 2) * UNITS)
                            pe.wait_ge(v_loaded, (p + 2) * 16)
                        scores_of(g + 2, 1 - a, n + 2 - NS)
                    if n in PROJ_AT and not last:
                        if n == min(PROJ_AT):
                            pe.wait_ge(w_split, p + 2)
                        project((p + 1) * UNITS + PROJ_AT[n], PROJ_AT[n])
                    if n in DEN_AT:
                        denominators(p, DEN_AT[n])
                    outputs_of(p, g, a, n)
                denominators(p, NB - 1)

            pe.wait_ge(init_ready, 2)
            pe.wait_ge(w_split, 1)
            for u in range(UNITS):
                project(u, u)
            pe.wait_ge(proj_ready, UNITS)
            pe.wait_ge(v_loaded, 16)
            scores_of(0, 0, 0)
            scores_of(1, 0, 1)
            run_pairs(pe, pair)

        @block.scalar
        def _(act):
            def tanh(g, n):
                width = queries(n)[1]
                act.wait_ge(scores_ready, g + 1)
                wait(act, exp_done, g - 1)
                nc.scalar.activation(capped[:, n % 2, :, 0:width], scores[:, n % 2, :, 0:width], ACT.Tanh,
                                     scale=DH ** -0.5 / SOFTCAP).then_inc(tanh_done, 1)

            def exp(g, n):
                width = queries(n)[1]
                act.wait_ge(tanh_done, g + 1)
                wait(act, pv_done, g + 1 - RING)
                wait(act, summed, g + 1 - RING)
                nc.scalar.activation(probs[:, n % RING, :, 0:width], capped[:, n % 2, :, 0:width], ACT.Exp,
                                     scale=SOFTCAP).then_inc(exp_done, 1)

            def pair(p, a, last):
                for n in range(NS):
                    g = p * NS + n
                    if not (last and n == NS - 1):
                        tanh(g + 1, (n + 1) % NS)
                    exp(g, n)

            act.wait_ge(scores_ready, 1)
            width = queries(0)[1]
            nc.scalar.activation(capped[:, 0, :, 0:width], scores[:, 0, :, 0:width], ACT.Tanh,
                                 scale=DH ** -0.5 / SOFTCAP).then_inc(tanh_done, 1)
            run_pairs(act, pair)

        @block.gpsimd
        def _(pool):
            def mask(p, g, n):
                pool.wait_ge(exp_done, g + 1)
                tile = probs[:, n % RING, :, 0:P]
                nc.gpsimd.tensor_tensor(tile, tile, causal[:], ALU.mult).then_inc(masked, 1)

            def normalise(p, a):
                pool.wait_ge(factor_loaded, p * 32)
                pool.wait_ge(out_copied, p * NB)
                nc.gpsimd.tensor_tensor(factor_b[:], out_t[1 - a][:], factor_b[:], ALU.mult).then_inc(normed, 1)

            def pair(p, a, last):
                for n in range(NS):
                    if DIAG[n]:
                        mask(p, p * NS + n, n)
                    if n == NORM_AT and not is_first(p):
                        normalise(p, a)

            nc.gpsimd.memset(ones[:], 1.0).then_inc(init_ready, 1)
            nc.gpsimd.memset(causal[:], 1.0).then_inc(init_ready, 1)
            pool.wait_ge(init_ready, 2)
            nc.gpsimd.affine_select(out=causal[:], in_=causal[:], pattern=[[0, 2], [1, P]], compare_op=ALU.is_ge, fill=0.0,
                                    base=0, channel_multiplier=-1).then_inc(init_ready, 1)
            pool.wait_ge(init_ready, 3)
            run_pairs(pool, pair)
            normalise(PAIRS, 0)

        @block.vector
        def _(dve):
            def sum_probs(p, g, n):
                qb, j = STEPS[n]
                _, width, at = queries(n)
                if DIAG[n]:
                    dve.wait_ge(masked, p * ND + sum(DIAG[:n]) + 1)
                else:
                    dve.wait_ge(exp_done, g + 1)
                new, total = probs[:, n % RING, :, 0:width], psums[qb % 2][:, :, at:BLK]
                if j == 0:
                    wait(dve, den_computed, p * NB + qb - 1)
                    nc.vector.tensor_copy(total, new).then_inc(summed, 1)
                else:
                    dve.wait_ge(summed, g)
                    nc.vector.tensor_tensor(total, total, new, ALU.add).then_inc(summed, 1)

            def split_weights(p):
                dve.wait_ge(w_loaded, p * (16 * NW) + 16 * NW)
                wait(dve, proj_computed, p * UNITS)
                nc.vector.tensor_copy(w_hi[:], w_raw[:]).then_inc(w_hi_ready, 1)
                dve.wait_ge(w_hi_ready, p + 1)
                nc.vector.tensor_tensor(w_lo[:], w_raw[:], w_hi[:].bitcast(F32), ALU.subtract).then_inc(w_split, 1)

            def split_projection(count, a, u):
                w, b = u // NB, u % NB
                h = w % 2
                dve.wait_ge(proj_computed, count + 1)
                hi = (q_hi if w < 2 else k_hl)[a][h][:, blk(b)]
                nc.vector.tensor_copy(hi, proj_ps[:]).then_inc(proj_hi_ready, 1)
                dve.wait_ge(proj_hi_ready, count + 1)
                if w < 2:
                    nc.vector.tensor_tensor(q_lo[a][h][:, blk(b)], proj_ps[:], hi.bitcast(F32), ALU.subtract).then_inc(proj_ready, 1)
                else:
                    rest = k_hl[a][h][DH:P, blk(b)]
                    nc.vector.tensor_tensor(rest, proj_ps[DH:P], rest.bitcast(F32), ALU.subtract).then_inc(proj_ready, 1)

            def copy_outputs(p, a, qb):
                dve.wait_ge(pv_done, p * NS + LAST[qb] + 1)
                if qb == 0:
                    wait(dve, normed, p - 1)
                nc.vector.tensor_copy(out_t[a][:, blk(qb)], o_ps[:, qb % 2]).then_inc(out_copied, 1)

            def copy_denominators(p, qb):
                dve.wait_ge(den_computed, p * NB + qb + 1)
                wait(dve, den_stored[qb % 2], (p * (NB // 2) + qb // 2) * 16)
                nc.vector.tensor_copy(den_row[:, qb % 2], den_ps[:]).then_inc(den_copied, 1)

            def factors(p):
                dve.wait_ge(den_loaded, p * 32)
                nc.vector.reciprocal(rden[:], den_r[:]).then_inc(rden_ready, 1)
                dve.wait_ge(rden_ready, p)
                wait(dve, factor_stored, (p - 1) * 16)
                nc.vector.tensor_tensor(factor[:], rden[:], gate_r[:], ALU.mult).then_inc(factor_ready, 1)

            def pair(p, a, last):
                for n in range(NS):
                    sum_probs(p, p * NS + n, n)
                    if not last:
                        if n == SPLIT_AT:
                            split_weights(p + 1)
                        if n in PROJ_AT:
                            if n == min(PROJ_AT):
                                wait(dve, scores_ready, p * NS)
                            split_projection((p + 1) * UNITS + PROJ_AT[n], 1 - a, PROJ_AT[n])
                    if n == FACTOR_AT and not is_first(p):
                        factors(p)
                    if n in OUT_AT:
                        copy_outputs(p, a, OUT_AT[n])
                    if n in DEN_AT:
                        copy_denominators(p, DEN_AT[n])
                copy_outputs(p, a, NB - 1)
                copy_denominators(p, NB - 1)

            split_weights(0)
            for u in range(UNITS):
                split_projection(u, 0, u)
            run_pairs(dve, pair)
            factors(PAIRS)


def output_projection(nc, sems, x, w_out, o_dram):
    with ExitStack() as ctx:
        w = ctx.enter_context(nc.sbuf_tensor("op_w", [P, PAIRS, P], F32))
        o = ctx.enter_context(nc.sbuf_tensor("op_o", [P, PAIRS, T], F32))
        y = ctx.enter_context(nc.psum_tensor("op_y", [P, NB, BLK], F32))
        w_loaded = sems("op", f"w_loaded")
        o_loaded = [sems("op", f"o_loaded{i}") for i in range(PAIRS)]
        y_ready = sems("op", f"y_ready")
        block = ctx.enter_context(nc.Block())

        @block.sync
        def _(sp):
            sp.dma_start(w[:], w_out.rearrange("(a c) f -> c a f", a=PAIRS)).then_inc(w_loaded, 16)
            for p in range(PAIRS):
                sp.dma_start(o[:, p], o_dram[p]).then_inc(o_loaded[p], 16)

        @block.tensor
        def _(pe):
            pe.wait_ge(w_loaded, 16)
            for p in range(PAIRS):
                pe.wait_ge(o_loaded[p], 16)
                for b in range(NB):
                    mm = nc.tensor.matmul(y[:, b], w[:, p], o[:, p, blk(b)], start=(p == 0), stop=(p == PAIRS - 1))
                    if p == PAIRS - 1:
                        mm.then_inc(y_ready, 1)

        @block.vector
        def _(dve):
            for b in range(NB):
                dve.wait_ge(y_ready, b + 1)
                nc.vector.tensor_tensor(x[:, blk(b)], x[:, blk(b)], y[:, b], ALU.add)


ROUTED = 8
EXPERTS = 1 + ROUTED
TOP_K = 2
HID = 256
CHUNKS = HID // P
UPB = EXPERTS * CHUNKS
RH = 6
RG = 3
LEAD = 3


def load_experts(nc, sems, wg_t, wu_t, wd_t, wgu_hi, wgu_lo, wd_hi, wd_lo):
    R = 3
    with ExitStack() as ctx:
        sem = lambda n: sems("le", n)
        wgu = ctx.enter_context(nc.sbuf_tensor("le_wgu", [P, R, 2, HID], F32))
        wd = ctx.enter_context(nc.sbuf_tensor("le_wd", [P, R, CHUNKS, P], F32))
        loaded = [sem(f"loaded{i}") for i in range(R)]
        hi_ready, split = sem("hi_ready"), sem("split")
        block = ctx.enter_context(nc.Block())

        @block.sync
        def _(sp):
            for e in range(EXPERTS):
                if e >= R:
                    sp.wait_ge(split, 2 * (e - R + 1))
                r = e % R
                sp.dma_start(wgu[:, r, 0], wg_t[e]).then_inc(loaded[r], 16)
                sp.dma_start(wgu[:, r, 1], wu_t[e]).then_inc(loaded[r], 16)
                sp.dma_start(wd[:, r], wd_t[e].rearrange("(c i) h -> i c h", c=CHUNKS)).then_inc(loaded[r], 16)

        @block.vector
        def _(dve):
            for e in range(EXPERTS):
                r = e % R
                dve.wait_ge(loaded[r], 48 * (e // R + 1))
                nc.vector.tensor_copy(wgu_hi[:, e], wgu[:, r]).then_inc(hi_ready, 1)
                nc.vector.tensor_copy(wd_hi[:, e], wd[:, r]).then_inc(hi_ready, 1)
                dve.wait_ge(hi_ready, 2 * e + 1)
                nc.vector.tensor_tensor(wgu_lo[:, e], wgu[:, r], wgu_hi[:, e].bitcast(F32), ALU.subtract).then_inc(split, 1)
                dve.wait_ge(hi_ready, 2 * e + 2)
                nc.vector.tensor_tensor(wd_lo[:, e], wd[:, r], wd_hi[:, e].bitcast(F32), ALU.subtract).then_inc(split, 1)


def route(nc, sems, xn, wr_t, rb, cw_dram, name):
    with ExitStack() as ctx:
        sb = lambda n, s, d=F32: ctx.enter_context(nc.sbuf_tensor(f"{name}_{n}", s, d))
        sem = lambda n: sems("rt", n)
        E = ROUTED
        wr = sb("wr", [P, E])
        bias = sb("bias", [P, E])
        ones = sb("ones", [P, P])
        ident = sb("ident", [P, P])
        before = sb("before", [P, E, E])
        logits = sb("logits", [P, NT, E])
        probs = sb("probs", [P, NT, E])
        above = sb("above", [P, NT, E, E])
        equal = sb("equal", [P, NT, E, E])
        rank = sb("rank", [P, NT, E])
        cw = sb("cw", [P, E, NT])
        cw_t = sb("cw_t", [E * NT, P])
        logits_ps = ctx.enter_context(nc.psum_tensor(f"{name}_logits_ps", [P, NT, E], F32))
        cw_ps = ctx.enter_context(nc.psum_tensor(f"{name}_cw_ps", [E * NT, P], F32))
        loaded, const_ready, before_ready, ident_ready = sem("loaded"), sem("const_ready"), sem("before_ready"), sem("ident_ready")
        logits_computed, logits_ready, probs_ready = sem("logits_computed"), sem("logits_ready"), sem("probs_ready")
        compared, step, cw_ready, cw_turned, cw_copied, stored = sem("compared"), sem("step"), sem("cw_ready"), sem("cw_turned"), sem("cw_copied"), sem("stored")
        block = ctx.enter_context(nc.Block())

        @block.sync
        def _(sp):
            sp.dma_start(wr[:], wr_t).then_inc(loaded, 16)
            sp.dma_start(bias[:], rb.unsqueeze(0).broadcast_to([P, E])).then_inc(loaded, 16)
            sp.wait_ge(const_ready, 2)
            sp.dma_start(cw_dram[0].rearrange("(p c) -> p c", p=NT), ones[0:NT, :]).then_inc(stored, 16)
            sp.wait_ge(cw_copied, 1)
            sp.dma_start(cw_dram[1:].rearrange("e (t k) -> (e t) k", k=P), cw_t[:]).then_inc(stored, 16)
            sp.wait_ge(stored, 32)

        @block.gpsimd
        def _(pool):
            nc.gpsimd.memset(before[:], 1.0).then_inc(const_ready, 1)
            nc.gpsimd.memset(ones[:], 1.0).then_inc(const_ready, 1)
            pool.wait_ge(const_ready, 2)
            nc.gpsimd.affine_select(out=before[:], in_=before[:], pattern=[[1, E], [-1, E]], compare_op=ALU.is_gt, fill=0.0,
                                    base=0, channel_multiplier=0).then_inc(before_ready, 1)
            nc.gpsimd.affine_select(out=ident[:], in_=ones[:], pattern=[[1, P]], compare_op=ALU.is_equal, fill=0.0,
                                    base=0, channel_multiplier=-1).then_inc(ident_ready, 1)

        @block.tensor
        def _(pe):
            pe.wait_ge(loaded, 32)
            for t in range(NT):
                mm = nc.tensor.matmul(logits_ps[:, t], xn[:, blk(t, P)], wr[:], start=True, stop=True)
            mm.then_inc(logits_computed, 1)
            pe.wait_ge(ident_ready, 1)
            pe.wait_ge(cw_ready, 1)
            nc.tensor.transpose(cw_ps[:], cw[:].rearrange("p e t -> p (e t)"), ident[:]).then_inc(cw_turned, 1)

        @block.scalar
        def _(act):
            act.wait_ge(logits_ready, 1)
            nc.scalar.activation(probs[:], logits[:], ACT.Sigmoid).then_inc(probs_ready, 1)

        @block.vector
        def _(dve):
            dve.wait_ge(logits_computed, 1)
            nc.vector.tensor_tensor(logits[:], logits_ps[:], bias[:].unsqueeze(1).broadcast_to([P, NT, E]), ALU.add).then_inc(logits_ready, 1)
            dve.wait_ge(probs_ready, 1)
            this = probs[:].unsqueeze(3).broadcast_to([P, NT, E, E])
            other = probs[:].unsqueeze(2).broadcast_to([P, NT, E, E])
            nc.vector.tensor_tensor(above[:], other, this, ALU.is_gt).then_inc(compared, 1)
            nc.vector.tensor_tensor(equal[:], other, this, ALU.is_equal).then_inc(compared, 1)
            dve.wait_ge(before_ready, 1)
            dve.wait_ge(compared, 2)
            nc.vector.tensor_tensor(equal[:], equal[:], before[:].unsqueeze(1).broadcast_to([P, NT, E, E]), ALU.mult).then_inc(step, 1)
            dve.wait_ge(step, 1)
            nc.vector.tensor_tensor(above[:], above[:], equal[:], ALU.add).then_inc(step, 1)
            dve.wait_ge(step, 2)
            nc.vector.tensor_reduce(rank[:], above[:], AX.X, ALU.add).then_inc(step, 1)
            dve.wait_ge(step, 3)
            nc.vector.scalar_tensor_tensor(out=cw[:].rearrange("p e t -> p t e"), in0=rank[:], scalar=float(TOP_K), in1=probs[:],
                                           op0=ALU.is_lt, op1=ALU.mult).then_inc(cw_ready, 1)
            dve.wait_ge(cw_turned, 1)
            nc.vector.tensor_copy(cw_t[:], cw_ps[:]).then_inc(cw_copied, 1)


def experts(nc, sems, x, x_hi, x_lo, wgu_hi, wgu_lo, wd_hi, wd_lo, cw_dram, name):
    with ExitStack() as ctx:
        sb = lambda n, s, d=F32: ctx.enter_context(nc.sbuf_tensor(f"{name}_{n}", s, d))
        sem = lambda n: sems("ex", n)
        silu = sb("silu", [P, RG, BLK])
        hid = sb("hid", [P, RG, BLK])
        hid_hi = sb("hid_hi", [P, RH, BLK], F32R)
        hid_lo = sb("hid_lo", [P, RH, BLK], F32R)
        weighted = sb("weighted", [P, RG, BLK])
        cw = sb("cw", [P, EXPERTS, BLK])
        gate_ps = ctx.enter_context(nc.psum_tensor(f"{name}_gate_ps", [P, RG, BLK], F32))
        up_ps = ctx.enter_context(nc.psum_tensor(f"{name}_up_ps", [P, RG, BLK], F32))
        down_ps = ctx.enter_context(nc.psum_tensor(f"{name}_down_ps", [P, 1, BLK], F32))
        cw_loaded = [sem(f"cw_loaded{e}") for e in range(EXPERTS)]
        gate_ready, up_ready, silu_ready, hid_ready = sem("gate_ready"), sem("up_ready"), sem("silu_ready"), sem("hid_ready")
        hi_ready, lo_ready, down_ready, scaled, added = sem("hi_ready"), sem("lo_ready"), sem("down_ready"), sem("scaled"), sem("added")
        block = ctx.enter_context(nc.Block())

        def run_blocks(eng, body):
            body(0, True, False)
            with eng.Fori(1, NB - 1) as b:
                body(b, False, False)
            body(NB - 1, False, True)

        @block.sync
        def _(sp):
            def load(b, e):
                sp.dma_start(cw[:, e], cw_dram[e:e + 1, bass.ds(b * BLK, BLK)].broadcast_to([P, BLK])).then_inc(cw_loaded[e], 16)

            for e in range(EXPERTS):
                load(0, e)
            with sp.Fori(0, NB - 1) as b:
                for e in range(EXPERTS):
                    sp.wait_ge(scaled, b * EXPERTS + e + 1)
                    load(b + 1, e)

        @block.tensor
        def _(pe):
            def gate_up(b, i):
                e, c = i // CHUNKS, i % CHUNKS
                wait(pe, hid_ready, b * UPB + i - RG + 1)
                xs_hi, xs_lo = x_hi[:, bass.ds(b * BLK, BLK)], x_lo[:, bass.ds(b * BLK, BLK)]
                for which, out, ready in ((0, gate_ps, gate_ready), (1, up_ps, up_ready)):
                    out = out[:, i % RG]
                    hi, lo = wgu_hi[:, e, which, blk(c, P)], wgu_lo[:, e, which, blk(c, P)]
                    nc.tensor.matmul(out, hi, xs_hi, start=True, stop=False)
                    nc.tensor.matmul(out, hi, xs_lo, start=False, stop=False)
                    nc.tensor.matmul(out, lo, xs_hi, start=False, stop=True).then_inc(ready, 1)

            def down(b, e):
                wait(pe, scaled, b * EXPERTS + e)
                for c in range(CHUNKS):
                    i = e * CHUNKS + c
                    hi, lo = wd_hi[:, e, c], wd_lo[:, e, c]
                    wait(pe, hi_ready, b * UPB + i + 1)
                    nc.tensor.matmul(down_ps[:, 0], hi, hid_hi[:, i % RH], start=(c == 0), stop=False)
                    nc.tensor.matmul(down_ps[:, 0], lo, hid_hi[:, i % RH], start=False, stop=False)
                    wait(pe, lo_ready, b * UPB + i + 1)
                    mm = nc.tensor.matmul(down_ps[:, 0], hi, hid_lo[:, i % RH], start=False, stop=(c == CHUNKS - 1))
                mm.then_inc(down_ready, 1)

            def body(b, first, last):
                for i in range(UPB):
                    if i + LEAD < UPB:
                        gate_up(b, i + LEAD)
                    elif not last:
                        gate_up(b + 1, i + LEAD - UPB)
                    if i % CHUNKS == CHUNKS - 1:
                        down(b, i // CHUNKS)

            for i in range(LEAD):
                gate_up(0, i)
            run_blocks(pe, body)

        @block.scalar
        def _(act):
            def silu_of(b, i):
                wait(act, gate_ready, b * UPB + i + 1)
                wait(act, hid_ready, b * UPB + i - RG + 1)
                nc.scalar.activation(silu[:, i % RG], gate_ps[:, i % RG], ACT.Silu).then_inc(silu_ready, 1)

            def body(b, first, last):
                for i in range(UPB):
                    if i + 1 < UPB:
                        silu_of(b, i + 1)
                    elif not last:
                        silu_of(b + 1, 0)
                    wait(act, hid_ready, b * UPB + i + 1)
                    wait(act, down_ready, b * EXPERTS + (i - RH) // CHUNKS + 1)
                    nc.scalar.copy(hid_hi[:, i % RH], hid[:, i % RG]).then_inc(hi_ready, 1)

            silu_of(0, 0)
            run_blocks(act, body)

        @block.vector
        def _(dve):
            def hidden(b, i):
                wait(dve, up_ready, b * UPB + i + 1)
                wait(dve, silu_ready, b * UPB + i + 1)
                wait(dve, hi_ready, b * UPB + i - RG + 1)
                wait(dve, lo_ready, b * UPB + i - RG + 1)
                nc.vector.tensor_tensor(hid[:, i % RG], silu[:, i % RG], up_ps[:, i % RG], ALU.mult).then_inc(hid_ready, 1)

            def scale(b, e):
                wait(dve, down_ready, b * EXPERTS + e + 1)
                wait(dve, added, b * EXPERTS + e - RG + 1)
                wait(dve, cw_loaded[e], b * 16 + 16)
                nc.vector.tensor_tensor(weighted[:, e % RG], cw[:, e], down_ps[:, 0], ALU.mult).then_inc(scaled, 1)

            def body(b, first, last):
                for i in range(UPB):
                    if i + 1 < UPB:
                        hidden(b, i + 1)
                    elif not last:
                        hidden(b + 1, 0)
                    wait(dve, hi_ready, b * UPB + i + 1)
                    wait(dve, down_ready, b * EXPERTS + (i - RH) // CHUNKS + 1)
                    nc.vector.tensor_tensor(hid_lo[:, i % RH], hid[:, i % RG], hid_hi[:, i % RH].bitcast(F32), ALU.subtract).then_inc(lo_ready, 1)
                    if i % CHUNKS == 0 and i:
                        scale(b, i // CHUNKS - 1)
                    elif i == 0 and not first:
                        scale(b - 1, EXPERTS - 1)
                if last:
                    scale(b, EXPERTS - 1)

            hidden(0, 0)
            run_blocks(dve, body)

        @block.gpsimd
        def _(pool):
            for b in range(NB):
                for e in range(EXPERTS):
                    xs = x[:, blk(b)]
                    pool.wait_ge(scaled, b * EXPERTS + e + 1)
                    wait(pool, added, b * EXPERTS + e)
                    nc.gpsimd.tensor_tensor(xs, xs, weighted[:, e % RG], ALU.add).then_inc(added, 1)


HB = 16
DB = P // HB
PAD = 32
GROUPS = HB * PAD // P
PER_G = HB // GROUPS


def linear_attention(nc, sems, x, xn, wq_t, wk_t, wv_t, wo_t, bq, bk, bv, bo):
    VP = HB * PAD
    with ExitStack() as ctx:
        sb = lambda n, s, d=F32: ctx.enter_context(nc.sbuf_tensor(f"la_{n}", s, d))
        psum = lambda c, n, s: c.enter_context(nc.psum_tensor(f"la_{n}", s, F32))
        sem = lambda n: sems("la", n)
        wq, wk = sb("wq", [P, P]), sb("wk", [P, P])
        wv_pad = sb("wv_pad", [P, HB, PAD])
        wo_pad = sb("wo_pad", [P, GROUPS, P])
        bq_c, bk_c, bo_c = sb("bq_c", [P, 1]), sb("bk_c", [P, 1]), sb("bo_c", [P, 1])
        bk_r = sb("bk_r", [P, P])
        bv_r = sb("bv_r", [P, HB, PAD])
        q_t, k_t = sb("q_t", [P, T]), sb("k_t", [P, T])
        k_n = sb("k_n", [P, NT, P])
        v_n = sb("v_n", [P, NT, HB, PAD])
        ones = sb("ones", [P, HB])
        own_lo, own = sb("own_lo", [P, HB]), sb("own", [P, HB])
        q_x = sb("q_x", [P, 2, HB, P])
        masked = sb("masked", [P, 2, HB, P])
        state = sb("state", [P, 2, HB, PAD])
        out_t = sb("out_t", [P, 2, GROUPS, BLK])

        const_ready, wv_loaded, small_loaded = sem("const_ready"), sem("wv_loaded"), sem("small_loaded")
        own_lo_ready, own_ready = sem("own_lo_ready"), sem("own_ready")
        qk_computed, qk_ready, kv_computed, k_ready, v_ready = sem("qk_computed"), sem("qk_ready"), sem("kv_computed"), sem("k_ready"), sem("v_ready")

        with ExitStack() as c:
            qk_ps = psum(c, "qk_ps", [P, 4, BLK])
            kn_ps = psum(c, "kn_ps", [P, 2, BLK])
            vn_ps = psum(c, "vn_ps", [P, 2, VP])
            block = c.enter_context(nc.Block())

            @block.gpsimd
            def _(pool):
                nc.gpsimd.memset(wv_pad[:], 0.0).then_inc(const_ready, 1)
                nc.gpsimd.memset(bv_r[:], 0.0).then_inc(const_ready, 1)
                nc.gpsimd.memset(wo_pad[:], 0.0).then_inc(const_ready, 1)
                nc.gpsimd.memset(ones[:], 1.0).then_inc(const_ready, 1)
                nc.gpsimd.memset(state[:, 0], 0.0).then_inc(const_ready, 1)
                pool.wait_ge(const_ready, 5)
                nc.gpsimd.affine_select(out=own_lo[:], in_=ones[:], pattern=[[-DB, HB]], compare_op=ALU.is_ge, fill=0.0,
                                        base=0, channel_multiplier=1).then_inc(own_lo_ready, 1)
                pool.wait_ge(own_lo_ready, 1)
                nc.gpsimd.affine_select(out=own[:], in_=own_lo[:], pattern=[[DB, HB]], compare_op=ALU.is_gt, fill=0.0,
                                        base=DB, channel_multiplier=-1).then_inc(own_ready, 1)

            @block.sync
            def _(sp):
                for dst, src in ((wq, wq_t), (wk, wk_t)):
                    sp.dma_start(dst[:], src).then_inc(small_loaded, 16)
                for dst, src in ((bq_c, bq), (bk_c, bk), (bo_c, bo)):
                    sp.dma_start(dst[:], src.unsqueeze(1)).then_inc(small_loaded, 16)
                sp.dma_start(bk_r[:], bk.unsqueeze(0).broadcast_to([P, P])).then_inc(small_loaded, 16)
                sp.wait_ge(const_ready, 5)
                sp.dma_start(wv_pad[:, :, 0:DB], wv_t.rearrange("c (h d) -> c h d", h=HB)).then_inc(wv_loaded, 16)
                sp.dma_start(bv_r[:, :, 0:DB], bv.rearrange("(h d) -> h d", h=HB).unsqueeze(0).broadcast_to([P, HB, DB])).then_inc(wv_loaded, 16)
                for j in range(PER_G):
                    sp.dma_start(wo_pad[j * PAD:j * PAD + DB], wo_t.rearrange("(g j d) e -> j d g e", g=GROUPS, j=PER_G)[j]).then_inc(wv_loaded, 16)
                sp.wait_ge(wv_loaded, 16 * (2 + PER_G))

            @block.tensor
            def _(pe):
                pe.wait_ge(small_loaded, 16 * 6)
                for b in range(NB):
                    for w, weights in enumerate((wq, wk)):
                        n = 2 * b + w
                        if n >= 4:
                            pe.wait_ge(qk_ready, n - 3)
                        nc.tensor.matmul(qk_ps[:, n % 4], weights[:], xn[:, blk(b)], start=True, stop=True).then_inc(qk_computed, 1)
                pe.wait_ge(wv_loaded, 16 * (2 + PER_G))
                for t in range(NT):
                    if t >= 2:
                        pe.wait_ge(k_ready, t - 1)
                        pe.wait_ge(v_ready, t - 1)
                    nc.tensor.matmul(kn_ps[:, t % 2, 0:P], xn[:, blk(t, P)], wk[:], start=True, stop=True)
                    nc.tensor.matmul(vn_ps[:, t % 2], xn[:, blk(t, P)], wv_pad[:].rearrange("p h d -> p (h d)"),
                                     start=True, stop=True).then_inc(kv_computed, 1)

            @block.scalar
            def _(act):
                act.wait_ge(small_loaded, 16 * 6)
                for b in range(NB):
                    for w, (out, bias) in enumerate(((q_t, bq_c), (k_t, bk_c))):
                        act.wait_ge(qk_computed, 2 * b + w + 1)
                        nc.scalar.activation(out[:, blk(b)], qk_ps[:, (2 * b + w) % 4], ACT.Identity, bias=bias[:, 0:1]).then_inc(qk_ready, 1)

            @block.vector
            def _(dve):
                dve.wait_ge(small_loaded, 16 * 6)
                dve.wait_ge(wv_loaded, 16 * (2 + PER_G))
                for t in range(NT):
                    dve.wait_ge(kv_computed, t + 1)
                    nc.vector.tensor_tensor(k_n[:, t], bk_r[:], kn_ps[:, t % 2, 0:P], ALU.add).then_inc(k_ready, 1)
                    nc.vector.tensor_tensor(v_n[:, t], bv_r[:], vn_ps[:, t % 2].rearrange("p (h d) -> p h d", h=HB),
                                            ALU.add).then_inc(v_ready, 1)

        SB = HB * P // BLK
        scores_ready, scores_copied, q_x_ready, masked_ready = sem("scores_ready"), sem("scores_copied"), sem("q_x_ready"), sem("masked_ready")
        sums_ready, state_ready, out_ready, out_copied, y_ready, y_added = sem("sums_ready"), sem("state_ready"), sem("out_ready"), sem("out_copied"), sem("y_ready"), sem("y_added")
        PER_Y = BLK // P
        with ExitStack() as c:
            scores = psum(c, "scores", [P, HB, P])
            out_ps = psum(c, "out_ps", [P, 2, GROUPS, P])
            sums = psum(c, "sums", [P, VP])
            y_ps = psum(c, "y_ps", [P, BLK])
            block = c.enter_context(nc.Block())
            hb = HB // SB

            @block.tensor
            def _(pe):
                def scores_of(t):
                    pe.wait_ge(q_x_ready, t + 1)
                    for s in range(SB):
                        if t > 0:
                            pe.wait_ge(scores_copied, (t - 1) * SB + s + 1)
                        nc.tensor.matmul(scores[:, s * hb:(s + 1) * hb], k_t[:, blk(t, P)], q_x[:, t % 2, s * hb:(s + 1) * hb],
                                         start=True, stop=True).then_inc(scores_ready, 1)

                def outputs_of(t):
                    if t >= 2:
                        pe.wait_ge(out_copied, t - 1)
                    if t > 0:
                        pe.wait_ge(state_ready, t)
                    for g in range(GROUPS):
                        for j in range(PER_G):
                            nc.tensor.matmul(out_ps[j * PAD:(j + 1) * PAD, t % 2, g], state[:, t % 2, g * PER_G + j], q_t[:, blk(t, P)],
                                             start=(g == 0), stop=False, skip_group_check=True)
                    pe.wait_ge(masked_ready, t + 1)
                    for g in range(GROUPS):
                        for j in range(PER_G):
                            h = g * PER_G + j
                            mm = nc.tensor.matmul(out_ps[j * PAD:(j + 1) * PAD, t % 2, g], v_n[:, t, h], masked[:, t % 2, h],
                                                  start=False, stop=True, skip_group_check=True)
                    mm.then_inc(out_ready, 1)

                def project(b):
                    pe.wait_ge(out_copied, (b + 1) * PER_Y)
                    if b > 0:
                        pe.wait_ge(y_added, b)
                    for g in range(GROUPS):
                        mm = nc.tensor.matmul(y_ps[:], wo_pad[:, g], out_t[:, b % 2, g], start=(g == 0), stop=(g == GROUPS - 1))
                    mm.then_inc(y_ready, 1)

                scores_of(0)
                for t in range(NT):
                    if t + 1 < NT:
                        scores_of(t + 1)
                    outputs_of(t)
                    if t + 1 < NT:
                        if t > 0:
                            pe.wait_ge(state_ready, t)
                        nc.tensor.matmul(sums[:], k_n[:, t], v_n[:, t].rearrange("p h d -> p (h d)"), start=(t == 0),
                                         stop=True, skip_group_check=True).then_inc(sums_ready, 1)
                    if t % PER_Y == 0 and t > 0:
                        project(t // PER_Y - 1)
                project(NB - 1)

            @block.scalar
            def _(act):
                for t in range(NT):
                    for s in range(SB):
                        act.wait_ge(scores_ready, t * SB + s + 1)
                        if t >= 2 and s == 0:
                            act.wait_ge(out_ready, t - 1)
                        nc.scalar.copy(masked[:, t % 2, s * hb:(s + 1) * hb], scores[:, s * hb:(s + 1) * hb]).then_inc(scores_copied, 1)

            @block.gpsimd
            def _(pool):
                for t in range(NT):
                    pool.wait_ge(scores_copied, (t + 1) * SB)
                    m = masked[:, t % 2]
                    nc.gpsimd.affine_select(out=m, in_=m, pattern=[[0, HB], [1, P]], compare_op=ALU.is_ge, fill=0.0, base=0,
                                            channel_multiplier=-1).then_inc(masked_ready, 1)

            @block.vector
            def _(dve):
                def spread(t):
                    if t >= 2:
                        dve.wait_ge(scores_ready, (t - 1) * SB)
                    nc.vector.tensor_tensor(q_x[:, t % 2], q_t[:, blk(t, P)].unsqueeze(1).broadcast_to([P, HB, P]),
                                            own[:].unsqueeze(2).broadcast_to([P, HB, P]), ALU.mult).then_inc(q_x_ready, 1)

                def add(b):
                    dve.wait_ge(y_ready, b + 1)
                    nc.vector.scalar_tensor_tensor(out=x[:, blk(b)], in0=y_ps[:], scalar=bo_c[:, 0:1], in1=x[:, blk(b)],
                                                   op0=ALU.add, op1=ALU.add).then_inc(y_added, 1)

                spread(0)
                spread(1)
                for t in range(NT):
                    dve.wait_ge(out_ready, t + 1)
                    b = t // PER_Y
                    if b >= 2:
                        dve.wait_ge(y_ready, b - 1)
                    nc.vector.tensor_copy(out_t[:, b % 2, :, blk(t % PER_Y, P)], out_ps[:, t % 2]).then_inc(out_copied, 1)
                    if t + 1 < NT:
                        dve.wait_ge(sums_ready, t + 1)
                        nc.vector.tensor_tensor(state[:, (t + 1) % 2], sums[:].rearrange("p (h d) -> p h d", h=HB),
                                                own[:].unsqueeze(2).broadcast_to([P, HB, PAD]), ALU.mult).then_inc(state_ready, 1)
                    if t + 2 < NT:
                        spread(t + 2)
                    if t % PER_Y == 0 and t > 0:
                        add(t // PER_Y - 1)
                add(NB - 1)


def program(nc, x_t, w_qkv, w_gates, w_out, wq_t, bq, wk_t, bk, wv_t, bv, wo_t, bo, wg_t, wu_t, wd_t, wr_t, rb, out_t):
    dram = lambda n, s: nc.dram_tensor(n, s, F32).ap()
    v_dram = dram("v_dram", [PAIRS, P, NT, P])
    gate_dram = dram("gate_dram", [PAIRS, 2, T])
    den_dram = dram("den_dram", [PAIRS, 2, T])
    factor_dram = dram("factor_dram", [2, T])
    o_dram = dram("o_dram", [PAIRS, P, T])
    cw_dram = [dram(f"cw_dram{i}", [EXPERTS, T]) for i in range(2)]
    with ExitStack() as ctx:
        sb = lambda n, s, d=F32: ctx.enter_context(nc.sbuf_tensor(n, s, d))
        x = sb("x", [P, T])
        x_hi, x_lo = sb("x_hi", [P, T], F32R), sb("x_lo", [P, T], F32R)
        sems = Semaphores(nc, ctx)
        x_loaded, out_stored = sems("io", "x_loaded"), sems("io", "out_stored")
        with nc.Block() as block:
            @block.sync
            def _(sp):
                sp.dma_start(x[:], x_t).then_inc(x_loaded, 16)
                sp.wait_ge(x_loaded, 16)
        with nc.sbuf_tensor("xn_a", [P, T], F32) as xn:
            layer_norm(nc, sems, x, xn, x_hi, x_lo, "ln_a")
            values_and_gates(nc, sems, xn, x_hi, x_lo, w_qkv, w_gates, v_dram, gate_dram)
        softcap_attention(nc, sems, x_hi, x_lo, w_qkv, v_dram, gate_dram, den_dram, factor_dram, o_dram)
        output_projection(nc, sems, x, w_out, o_dram)
        xn = sb("xn", [P, T])
        weights = (sb("wgu_hi", [P, EXPERTS, 2, HID], F32R), sb("wgu_lo", [P, EXPERTS, 2, HID], F32R),
                   sb("wd_hi", [P, EXPERTS, CHUNKS, P], F32R), sb("wd_lo", [P, EXPERTS, CHUNKS, P], F32R))
        load_experts(nc, sems, wg_t, wu_t, wd_t, *weights)
        sems.clear("ln")
        layer_norm(nc, sems, x, xn, x_hi, x_lo, "ln_f0")
        route(nc, sems, xn, wr_t, rb, cw_dram[0], "rt0")
        experts(nc, sems, x, x_hi, x_lo, *weights, cw_dram[0], "ex0")
        sems.clear("ln", "rt", "ex")
        layer_norm(nc, sems, x, xn, x_hi, x_lo, "ln_b")
        linear_attention(nc, sems, x, xn, wq_t, wk_t, wv_t, wo_t, bq, bk, bv, bo)
        sems.clear("ln")
        layer_norm(nc, sems, x, xn, x_hi, x_lo, "ln_f1")
        route(nc, sems, xn, wr_t, rb, cw_dram[1], "rt1")
        experts(nc, sems, x, x_hi, x_lo, *weights, cw_dram[1], "ex1")
        with nc.Block() as block:
            @block.sync
            def _(sp):
                sp.dma_start(out_t, x[:]).then_inc(out_stored, 16)
                sp.wait_ge(out_stored, 16)


def kernel(**inputs):
    import numpy as np
    import concourse.bacc as bacc
    from concourse.bass_utils import run_bass_kernel_spmd

    a = {n.removeprefix("L0_"): np.asarray(v) for n, v in inputs.items()}
    turn = lambda v: np.ascontiguousarray(np.swapaxes(v, -1, -2))
    both = lambda n: turn(np.concatenate([a[f"ffn_{n}_s"][None], a[f"ffn_{n}"]]))
    arrays = {"x_t": turn(a["attn_a_x"][0]), "w_qkv": a["attn_a_w_qkv"], "w_gates": a["attn_a_w_gates"], "w_out": a["attn_a_w_out"]}
    for n in "qkvo":
        arrays[f"w{n}_t"] = turn(a[f"attn_b_w{n}_w"])
        arrays[f"b{n}"] = a[f"attn_b_w{n}_b"]
    arrays |= {"wg_t": both("Wg"), "wu_t": both("Wu"), "wd_t": both("Wd"), "wr_t": turn(a["ffn_Wr"]), "rb": a["ffn_rb"]}
    arrays = {f"in_{n}": np.ascontiguousarray(v) for n, v in arrays.items()}

    nc = bacc.Bacc("TRN2", target_bir_lowering=False, num_devices=1)
    args = [nc.dram_tensor(n, v.shape, mybir.dt.from_np(v.dtype), kind="ExternalInput").ap() for n, v in arrays.items()]
    out = nc.dram_tensor("out_0", (P, T), F32, kind="ExternalOutput").ap()
    program(nc, *args, out)
    r = run_bass_kernel_spmd(nc, [arrays], core_ids=[0])
    return np.ascontiguousarray(r.results[0]["out_0"].T)[None]
```

```python
from contextlib import ExitStack

import concourse.bass as bass
from concourse import mybir

F32 = mybir.dt.float32
F32R = mybir.dt.float32r
ACT = mybir.ActivationFunctionType
ALU = mybir.AluOpType
AX = mybir.AxisListType

P = 128
T = 2048
BLK = 512
NB = T // BLK
NT = T // P
EPS = 1e-5

H = 16
DH = 64
PAIRS = H // 2
SOFTCAP = 50.0
KT_PER_BLK = BLK // P


def spread(full, diagonal):
    n, out = len(full) + len(diagonal), []
    ends = [-(-(i + 1) * n // len(diagonal)) - 1 for i in range(len(diagonal))]
    full, diagonal = iter(full), iter(diagonal)
    for i in range(n):
        out.append(next(diagonal) if i in ends else next(full))
    return out


def steps_of_a_pair():
    full = lambda qb: [(qb, j) for j in range(KT_PER_BLK * qb)]
    diagonal = lambda qb: [(qb, KT_PER_BLK * qb + i) for i in range(KT_PER_BLK)]
    steps = []
    for qb in range(1, NB - 1):
        steps += spread(full(qb), diagonal(qb))
    a, b = diagonal(NB - 1), diagonal(0)
    return steps + spread(full(NB - 1), [a[0], b[0], a[1], a[2], b[1], a[3]]) + b[2:]


STEPS = steps_of_a_pair()
NS = len(STEPS)
PLACE = {qb: (qb - 1) % NB for qb in range(NB)}
DIAG = [j >= KT_PER_BLK * qb for qb, j in STEPS]
ND = sum(DIAG)
LAST = [max(n for n in range(NS) if STEPS[n][0] == qb) for qb in range(NB)]
assert sorted(range(NB), key=lambda qb: LAST[qb]) == sorted(range(NB), key=lambda qb: PLACE[qb])
UNITS = 2 * NB
RING = 4


def blk(b, n=BLK):
    return slice(b * n, (b + 1) * n)


def rows_of(h):
    return slice(h * DH, (h + 1) * DH)


class Semaphores:

    def __init__(self, nc, ctx):
        self.nc, self.ctx, self.of = nc, ctx, {}

    def __call__(self, part, name):
        if (part, name) not in self.of:
            self.of[part, name] = self.ctx.enter_context(self.nc.semaphore(f"{part}_{name}"))
        return self.of[part, name]

    def clear(self, pool, *parts):
        for (part, _), semaphore in self.of.items():
            if part in parts:
                pool.sem_clear(semaphore)


def wait(eng, semaphore, value):
    if not isinstance(value, int) or value > 0:
        eng.wait_ge(semaphore, value)


def layer_norm(nc, sems, part, x, xn, x_hi, x_lo, name, x_loaded=None, beside=None, router=None):
    Q = P // NB
    R, HALF = 2, BLK // 2
    S = 2
    with ExitStack() as ctx:
        sb = lambda n, s, d=F32: ctx.enter_context(nc.sbuf_tensor(f"{name}_{n}", s, d))
        sem = lambda n: sems(part, n)
        beside = beside or {}
        mean_of = sb("mean_of", [P, P])
        mean_at = sb("mean_at", [P, R, Q])
        pick = sb("pick", [P, NB, R, P])
        pick_r = sb("pick_r", [P, NB, R, P], F32R)
        eps = sb("eps", [P, 1])
        centred = sb("centred", [P, T])
        squared = sb("squared", [P, T])
        std = sb("std", [P, HALF])
        rstd = sb("rstd", [P, HALF])
        rstd_hi, rstd_lo = sb("rstd_hi", [P, HALF], F32R), sb("rstd_lo", [P, HALF], F32R)
        mean = ctx.enter_context(nc.psum_tensor(f"{name}_mean", [P, NB, BLK], F32))
        var = ctx.enter_context(nc.psum_tensor(f"{name}_var", [P, HALF], F32))
        spread = ctx.enter_context(nc.psum_tensor(f"{name}_spread", [P, S, BLK], F32))
        mean_at_ready, table_loaded, pick_r_ready = sem("mean_at_ready"), sem("table_loaded"), sem("pick_r_ready")
        const_ready, zero_ready, pick_ready, mean_ready, centred_ready = sem("const_ready"), sem("zero_ready"), sem("pick_ready"), sem("mean_ready"), sem("centred_ready")
        squared_ready, var_ready, std_ready = sem("squared_ready"), sem("var_ready"), sem("std_ready")
        rstd_ready, rstd_hi_ready, rstd_split, spread_ready = sem("rstd_ready"), sem("rstd_hi_ready"), sem("rstd_split"), sem("spread_ready")
        xn_ready, hi_ready = sem("xn_ready"), sem("hi_ready")
        if router:
            weights, probs = router
            logits = sb("logits", [P, NT, ROUTED])
            logits_ps = ctx.enter_context(nc.psum_tensor(f"{name}_logits_ps", [P, NT, ROUTED], F32))
            logits_computed, logits_ready = sem("logits_computed"), sem("logits_ready")
        block = ctx.enter_context(nc.Block())

        @block.sync
        def _(sp):
            if "sync" in beside:
                beside["sync"](sp)

        @block.gpsimd
        def _(pool):
            nc.gpsimd.memset(mean_of[:], 1.0 / P).then_inc(const_ready, 1)
            nc.gpsimd.memset(eps[:], EPS).then_inc(const_ready, 1)
            nc.gpsimd.memset(mean_at[:], 0.0).then_inc(zero_ready, 1)
            nc.gpsimd.memset(pick[:], 1.0).then_inc(zero_ready, 1)
            pool.wait_ge(zero_ready, 2)
            for r in range(R):
                nc.gpsimd.memset(mean_at[:, r, r:r + 1], 1.0 / P).then_inc(mean_at_ready, 1)
            nc.gpsimd.affine_select(out=pick[:], in_=pick[:], pattern=[[-Q, NB], [-1, R], [0, P]], compare_op=ALU.is_equal, fill=0.0,
                                    base=0, channel_multiplier=1).then_inc(pick_ready, 1)
            if "gpsimd" in beside:
                pool.wait_ge(mean_at_ready, R)
                pool.wait_ge(pick_ready, 1)
                beside["gpsimd"](pool)

        @block.tensor
        def _(pe):
            pe.wait_ge(const_ready, 2)
            for b in range(NB):
                if x_loaded:
                    pe.wait_ge(x_loaded[b], 16)
                nc.tensor.matmul(mean[:, b], mean_of[:], x[:, blk(b)], start=True, stop=True).then_inc(mean_ready, 1)
            pe.wait_ge(squared_ready, NB)
            pe.wait_ge(mean_at_ready, R)
            for r in range(R):
                for b in range(NB):
                    nc.tensor.matmul(var[b * Q:(b + 1) * Q], mean_at[:, r], squared[:, blk(R * b + r, HALF)],
                                     start=(r == 0), stop=(r == R - 1), skip_group_check=True).then_inc(var_ready, 1)
            pe.wait_ge(pick_r_ready, 1)
            pe.wait_ge(rstd_split, 1)
            for b in range(NB):
                if b >= S:
                    pe.wait_ge(xn_ready, b - S + 1)
                for r in range(R):
                    out = spread[:, b % S, blk(r, HALF)]
                    nc.tensor.matmul(out, pick_r[:, b, r], rstd_hi[:], start=True, stop=False)
                    mm = nc.tensor.matmul(out, pick_r[:, b, r], rstd_lo[:], start=False, stop=True)
                mm.then_inc(spread_ready, 1)
            if router:
                pe.wait_ge(weights.router_loaded, 32)
                for t in range(NT):
                    pe.wait_ge(xn_ready, t * P // BLK + 1)
                    mm = nc.tensor.matmul(logits_ps[:, t], xn[:, blk(t, P)], weights.router[:], start=True, stop=True)
                mm.then_inc(logits_computed, 1)

        @block.scalar
        def _(act):
            act.wait_ge(const_ready, 2)
            nc.scalar.activation(std[:, 0:1], eps[:], ACT.Sqrt).then_inc(table_loaded, 1)
            for b in range(NB):
                act.wait_ge(centred_ready, b + 1)
                nc.scalar.activation(squared[:, blk(b)], centred[:, blk(b)], ACT.Square).then_inc(squared_ready, 1)
            act.wait_ge(pick_ready, 1)
            nc.scalar.copy(pick_r[:], pick[:]).then_inc(pick_r_ready, 1)
            act.wait_ge(table_loaded, 1)
            act.wait_ge(var_ready, NB * R)
            nc.scalar.activation(std[:], var[:], ACT.Sqrt, bias=eps[:, 0:1]).then_inc(std_ready, 1)
            if x_hi is not None:
                for b in range(NB):
                    act.wait_ge(xn_ready, b + 1)
                    nc.scalar.copy(x_hi[:, blk(b)], xn[:, blk(b)]).then_inc(hi_ready, 1)
            if router:
                act.wait_ge(logits_ready, 1)
                nc.scalar.activation(probs[:], logits[:], ACT.Sigmoid)

        @block.vector
        def _(dve):
            def rest(b):
                dve.wait_ge(hi_ready, b + 1)
                nc.vector.tensor_tensor(x_lo[:, blk(b)], xn[:, blk(b)], x_hi[:, blk(b)].bitcast(F32), ALU.subtract)

            for b in range(NB):
                dve.wait_ge(mean_ready, b + 1)
                nc.vector.tensor_tensor(centred[:, blk(b)], x[:, blk(b)], mean[:, b], ALU.subtract).then_inc(centred_ready, 1)
            if "vector" in beside:
                beside["vector"](dve)
            dve.wait_ge(std_ready, 1)
            nc.vector.reciprocal(rstd[:], std[:]).then_inc(rstd_ready, 1)
            dve.wait_ge(rstd_ready, 1)
            nc.vector.tensor_copy(rstd_hi[:], rstd[:]).then_inc(rstd_hi_ready, 1)
            dve.wait_ge(rstd_hi_ready, 1)
            nc.vector.tensor_tensor(rstd_lo[:], rstd[:], rstd_hi[:].bitcast(F32), ALU.subtract).then_inc(rstd_split, 1)
            for b in range(NB):
                dve.wait_ge(spread_ready, b + 1)
                nc.vector.tensor_tensor(xn[:, blk(b)], centred[:, blk(b)], spread[:, b % S], ALU.mult).then_inc(xn_ready, 1)
                if b > 0 and x_hi is not None:
                    rest(b - 1)
            if x_hi is not None:
                rest(NB - 1)
            if router:
                dve.wait_ge(logits_computed, 1)
                nc.vector.tensor_tensor(logits[:], logits_ps[:], weights.bias[:].unsqueeze(1).broadcast_to([P, NT, ROUTED]), ALU.add).then_inc(logits_ready, 1)


class AttentionWeights:

    def __init__(self, ctx, nc, sems, w_qkv):
        sb = lambda n, s, d=F32: ctx.enter_context(nc.sbuf_tensor(f"aw_{n}", s, d))
        self.nc, self.w_qkv = nc, w_qkv
        self.raw, self.hi, self.lo = sb("raw", [P, 2 * P]), sb("hi", [P, 2 * P], F32R), sb("lo", [P, 2 * P], F32R)
        self.loaded, self.hi_ready, self.split = sems("aw", "loaded"), sems("aw", "hi_ready"), sems("aw", "split")
        self.v_loaded, self.v_hi_ready = sems("aw", "v_loaded"), sems("aw", "v_hi_ready")

    def allocate_v(self, ctx):
        sb = lambda n, d=F32: ctx.enter_context(self.nc.sbuf_tensor(f"aw_{n}", [P, H * DH], d))
        self.v, self.v_hi, self.v_lo = sb("v"), sb("v_hi", F32R), sb("v_lo", F32R)

    def load_v(self, sp):
        sp.dma_start(self.v[:], self.w_qkv[:, 2 * H * DH:3 * H * DH]).then_inc(self.v_loaded, 16)

    def load_pair(self, sp, p):
        for which in range(2):
            sp.dma_start(self.raw[:, blk(which, P)], self.w_qkv[:, bass.ds(p * P + which * H * DH, P)]).then_inc(self.loaded, 16)

    def split_v(self, dve):
        dve.wait_ge(self.v_loaded, 16)
        self.nc.vector.tensor_copy(self.v_hi[:], self.v[:]).then_inc(self.v_hi_ready, 1)
        dve.wait_ge(self.v_hi_ready, 1)
        self.nc.vector.tensor_tensor(self.v_lo[:], self.v[:], self.v_hi[:].bitcast(F32), ALU.subtract)

    def split_pair(self, dve, p):
        dve.wait_ge(self.loaded, p * 32 + 32)
        self.nc.vector.tensor_copy(self.hi[:], self.raw[:]).then_inc(self.hi_ready, 1)
        dve.wait_ge(self.hi_ready, p + 1)
        self.nc.vector.tensor_tensor(self.lo[:], self.raw[:], self.hi[:].bitcast(F32), ALU.subtract).then_inc(self.split, 1)


class Pairs:

    def __init__(self, ctx, nc, sems):
        sb = lambda n, s, d=F32: ctx.enter_context(nc.sbuf_tensor(f"pr_{n}", s, d))
        sem = lambda n: sems("pr", n)
        self.nc = nc
        self.q_hi = [[sb(f"q_hi{a}{h}", [P, T], F32R) for h in range(2)] for a in range(2)]
        self.q_lo = [[sb(f"q_lo{a}{h}", [P, T], F32R) for h in range(2)] for a in range(2)]
        self.k_hl = [[sb(f"k_hl{a}{h}", [P, T], F32R) for h in range(2)] for a in range(2)]
        self.v = sb("v", [P, 2, NT, P])
        self.computed, self.hi_ready, self.ready, self.q_doubled = sem("computed"), sem("hi_ready"), sem("ready"), sem("q_doubled")

    def project(self, u, weights, x_hi, x_lo, out):
        cols, xs = blk(u // NB, P), blk(u % NB)
        self.nc.tensor.matmul(out, weights.hi[:, cols], x_hi[:, xs], start=True, stop=False)
        self.nc.tensor.matmul(out, weights.hi[:, cols], x_lo[:, xs], start=False, stop=False)
        self.nc.tensor.matmul(out, weights.lo[:, cols], x_hi[:, xs], start=False, stop=True).then_inc(self.computed, 1)

    def leading(self, a, u):
        return [(self.q_hi, self.k_hl)[u // NB][a][h][rows_of(h), blk(u % NB)] for h in range(2)]

    def subtract_leading(self, a, u, out):
        for h, hi in enumerate(self.leading(a, u)):
            lo = self.q_lo[a][h][rows_of(h), blk(u % NB)] if u < NB else self.k_hl[a][h][rows_of(1 - h), blk(u % NB)]
            rest = self.nc.vector.tensor_tensor(lo, out[rows_of(h)], hi.bitcast(F32), ALU.subtract)
        rest.then_inc(self.ready, 1)

    def double_queries(self, sp, a):
        for q in (self.q_hi[a], self.q_lo[a]):
            for h in range(2):
                sp.dma_start(q[h][rows_of(1 - h), :].bitcast(F32), q[h][rows_of(h), :].bitcast(F32)).then_inc(self.q_doubled, 16)


def values_and_gates(nc, sems, xn, x_hi, x_lo, w, pairs, w_gates, v_dram, gate_dram):
    VD = H * DH
    HALF = VD // 2
    RV = 8
    NPS = 4
    KEPT = 2 * P
    UNIT_AFTER = {2 * u + 1: u for u in range(UNITS)}
    with ExitStack() as ctx:
        sb = lambda n, s, d=F32: ctx.enter_context(nc.sbuf_tensor(f"vg_{n}", s, d))
        sem = lambda n: sems("vg", n)
        wg = sb("wg", [P, H])
        v_tile = sb("v_tile", [P, RV, VD - KEPT])
        gate = sb("gate", [H, T])
        v_ps = ctx.enter_context(nc.psum_tensor("vg_v_ps", [P, NPS, BLK], F32))
        g_ps = ctx.enter_context(nc.psum_tensor("vg_g_ps", [H, 2, BLK], F32))
        p_ps = ctx.enter_context(nc.psum_tensor("vg_p_ps", [P, 2, BLK], F32))
        wg_loaded = sem("wg_loaded")
        v_computed, v_copied_act, v_copied_dve = sem("v_computed"), sem("v_copied_act"), sem("v_copied_dve")
        g_computed, g_ready, stored = sem("g_computed"), sem("g_ready"), sem("stored")
        v_stored = [sem(f"v_stored{i}") for i in range(RV)]
        block = ctx.enter_context(nc.Block())

        @block.sync
        def _(sp):
            sp.dma_start(wg[:], w_gates).then_inc(wg_loaded, 16)
            for t in range(NT):
                sp.wait_ge(v_copied_act, t + 1)
                sp.wait_ge(v_copied_dve, t + 1)
                sp.dma_start(v_dram[2:, :, t, :].rearrange("a p d -> p a d"),
                             v_tile[:, t % RV].rearrange("p (a d) -> p a d", a=PAIRS - 2)).then_inc(v_stored[t % RV], 16)
                if t == 2 * NB:
                    sp.wait_ge(pairs.ready, NB)
                    pairs.double_queries(sp, 0)
            sp.wait_ge(g_ready, NB)
            sp.dma_start(gate_dram.rearrange("a h t -> (a h) t"), gate[:]).then_inc(stored, 16)
            for stored_of in v_stored:
                sp.wait_ge(stored_of, 16 * NT // RV)
            sp.wait_ge(stored, 16)

        @block.tensor
        def _(pe):
            for t in range(NT):
                for half in range(2):
                    n = 2 * t + half
                    if n >= NPS:
                        pe.wait_ge(v_copied_act if half == 0 else v_copied_dve, (n - NPS) // 2 + 1)
                    out, cols = v_ps[:, n % NPS], blk(half, HALF)
                    nc.tensor.matmul(out, x_hi[:, blk(t, P)], w.v_hi[:, cols], start=True, stop=False)
                    nc.tensor.matmul(out, x_hi[:, blk(t, P)], w.v_lo[:, cols], start=False, stop=False)
                    nc.tensor.matmul(out, x_lo[:, blk(t, P)], w.v_hi[:, cols], start=False, stop=True).then_inc(v_computed, 1)
                if t in UNIT_AFTER:
                    wait(pe, pairs.ready, UNIT_AFTER[t] - 1)
                    pairs.project(UNIT_AFTER[t], w, x_hi, x_lo, p_ps[:, UNIT_AFTER[t] % 2])
            pe.wait_ge(wg_loaded, 16)
            for b in range(NB):
                if b >= 2:
                    pe.wait_ge(g_ready, b - 1)
                nc.tensor.matmul(g_ps[:, b % 2], wg[:], xn[:, blk(b)], start=True, stop=True).then_inc(g_computed, 1)

        @block.scalar
        def _(act):
            for t in range(NT):
                act.wait_ge(v_computed, 2 * t + 1)
                if t >= RV:
                    act.wait_ge(v_stored[t % RV], 16 * (t // RV))
                first = v_ps[:, (2 * t) % NPS]
                nc.scalar.copy(pairs.v[:, :, t], first[:, 0:KEPT].rearrange("p (a d) -> p a d", a=2))
                nc.scalar.copy(v_tile[:, t % RV, 0:HALF - KEPT], first[:, KEPT:HALF]).then_inc(v_copied_act, 1)
                if t in UNIT_AFTER:
                    u = UNIT_AFTER[t]
                    act.wait_ge(pairs.computed, u + 1)
                    for h, hi in enumerate(pairs.leading(0, u)):
                        leading = nc.scalar.copy(hi, p_ps[rows_of(h), u % 2])
                    leading.then_inc(pairs.hi_ready, 1)
            for b in range(NB):
                act.wait_ge(g_computed, b + 1)
                nc.scalar.activation(gate[:, blk(b)], g_ps[:, b % 2], ACT.Sigmoid).then_inc(g_ready, 1)

        @block.vector
        def _(dve):
            for t in range(NT):
                dve.wait_ge(v_computed, 2 * t + 2)
                if t >= RV:
                    dve.wait_ge(v_stored[t % RV], 16 * (t // RV))
                nc.vector.tensor_copy(v_tile[:, t % RV, HALF - KEPT:], v_ps[:, (2 * t + 1) % NPS]).then_inc(v_copied_dve, 1)
                if t in UNIT_AFTER:
                    u = UNIT_AFTER[t]
                    dve.wait_ge(pairs.hi_ready, u + 1)
                    pairs.subtract_leading(0, u, p_ps[:, u % 2])


def softcap_attention(nc, sems, x, x_hi, x_lo, weights, pairs, w_out, v_dram, gate_dram, den_dram, factor_dram):
    PROJ_AT = {4 + 4 * u: u for u in range(UNITS)}
    OUT_LAG, DEN_LAG, DEN_COPY_LAG = 2, 2, 3
    SPLIT_AT, FACTOR_AT = 2, 9
    NORM_AT = {20 + 4 * b: b for b in range(NB)}
    Y_AT = {22 + 4 * b: b for b in range(NB)}
    with ExitStack() as ctx:
        sb = lambda n, s, d=F32: ctx.enter_context(nc.sbuf_tensor(f"at_{n}", s, d))
        psum = lambda n, s: ctx.enter_context(nc.psum_tensor(f"at_{n}", s, F32))
        sem = lambda n: sems("at", n)
        w_y = [sb(f"w_y{a}", [P, P]) for a in range(2)]
        q_hi, q_lo, k_hl = pairs.q_hi, pairs.q_lo, pairs.k_hl
        v = [pairs.v[:, a] for a in range(2)]
        capped = sb("capped", [P, 2, 2, BLK])
        probs = sb("probs", [P, RING, 2, BLK])
        psums = [sb(f"psums{a}", [P, 2, BLK]) for a in range(2)]
        ones = sb("ones", [P, DH])
        causal = sb("causal", [P, 2, P])
        den_row = sb("den_row", [P, 2, BLK])
        out_t = [sb(f"out_t{a}", [P, T]) for a in range(2)]
        factor_b = sb("factor_b", [P, T])
        den_r = sb("den_r", [P, 2 * T // P])
        gate_r = sb("gate_r", [P, 2 * T // P])
        rden = sb("rden", [P, 2 * T // P])
        factor = sb("factor", [P, 2 * T // P])
        scores = psum("scores", [P, 2, 2, BLK])
        o_ps = psum("o_ps", [P, 2, BLK])
        proj_ps = psum("proj_ps", [P, BLK])
        den_ps = psum("den_ps", [P, BLK])

        init_ready = sem("init_ready")
        proj_computed, proj_hi_ready, proj_ready, q_doubled = pairs.computed, pairs.hi_ready, pairs.ready, pairs.q_doubled
        v_loaded = sem("v_loaded")
        scores_ready, tanh_done, exp_done, masked = sem("scores_ready"), sem("tanh_done"), sem("exp_done"), sem("masked")
        pv_done, summed, out_copied = sem("pv_done"), sem("summed"), sem("out_copied")
        den_computed, den_copied = sem("den_computed"), sem("den_copied")
        den_stored = [sem(f"den_stored{i}") for i in range(2)]
        den_loaded, rden_ready, factor_ready = sem("den_loaded"), sem("rden_ready"), sem("factor_ready")
        factor_stored, factor_loaded, normed, y_computed = sem("factor_stored"), sem("factor_loaded"), sem("normed"), sem("y_computed")
        w_y_loaded, y_added = sem("w_y_loaded"), sem("y_added")
        gate_loaded, gated, divided = sem("gate_loaded"), sem("gated"), sem("divided")
        gate_b = v[0].rearrange("p t d -> p (t d)")
        block = ctx.enter_context(nc.Block())

        def run_pairs(eng, pair):
            pair(0, 0, False)
            pair(1, 1, False)
            with eng.Fori(1, PAIRS // 2 - 1) as i:
                pair(i * 2, 0, False)
                pair(i * 2 + 1, 1, False)
            pair(PAIRS - 2, 0, False)
            pair(PAIRS - 1, 1, True)

        def is_first(p):
            return isinstance(p, int) and p == 0

        def blocks_in_place():
            return sorted(range(NB), key=lambda qb: PLACE[qb])

        def due(p, a, n, lag):
            for qb in blocks_in_place():
                if LAST[qb] + lag == n and not (isinstance(p, int) and p == PAIRS):
                    yield p, a, qb
                if LAST[qb] + lag - NS == n and not is_first(p):
                    yield p - 1, 1 - a, qb

        def queries(n):
            qb, j = STEPS[n]
            first = max(qb * BLK, j * P)
            return first, (qb + 1) * BLK - first, first - qb * BLK

        @block.sync
        def _(sp):
            def load_values(p, a):
                sp.dma_start(v[a], v_dram[bass.ds(p, 1)].rearrange("a p t d -> (a p) t d")).then_inc(v_loaded, 16)

            def factors(p, a, before):
                for stored in den_stored:
                    sp.wait_ge(stored, p * (16 * NB // 2))
                shape = dict(c=2 * T // P)
                sp.dma_start(den_r[:], den_dram[bass.ds(before, 1), 1:3].rearrange("a h (p c) -> (a h p) c", **shape)).then_inc(den_loaded, 16)
                sp.dma_start(gate_r[:], gate_dram[bass.ds(before, 1)].rearrange("a h (p c) -> (a h p) c", **shape)).then_inc(den_loaded, 16)
                wait(sp, y_computed, (p - 1) * NB)
                sp.dma_start(w_y[1 - a][:], w_out[bass.ds(before * P, P)]).then_inc(w_y_loaded, 16)
                sp.wait_ge(factor_ready, p)
                sp.dma_start(factor_dram.rearrange("h (p c) -> (h p) c", **shape), factor[:]).then_inc(factor_stored, 16)
                sp.wait_ge(factor_stored, p * 16)
                for h in range(2):
                    sp.dma_start(factor_b[h * DH:(h + 1) * DH, :], factor_dram[h:h + 1].broadcast_to([DH, T])).then_inc(factor_loaded, 16)

            def store_denominators(p, qb):
                sp.wait_ge(den_copied, p * NB + PLACE[qb] + 1)
                buffer = PLACE[qb] % 2
                sp.dma_start(den_dram[bass.ds(p, 1), 1:3, blk(qb)].rearrange("a h t -> (a h) t"),
                             den_row[0:DH + 1:DH, buffer]).then_inc(den_stored[buffer], 16)

            def pair(p, a, last):
                before = p - 1
                if not last:
                    sp.wait_ge(weights.split, p + 1)
                    weights.load_pair(sp, p + 1)
                    if not is_first(p):
                        sp.wait_ge(pv_done, p * NS)
                        wait(sp, v_loaded, (p - 1) * 16)
                        load_values(p + 1, 1 - a)
                if not is_first(p):
                    store_denominators(before, 0)
                    factors(p, a, before)
                if last:
                    sp.wait_ge(pv_done, p * NS)
                    for h in range(2):
                        sp.dma_start(gate_b[rows_of(h), :], gate_dram[p, h:h + 1].broadcast_to([DH, T])).then_inc(gate_loaded, 16)
                    sp.wait_ge(w_y_loaded, p * 16)
                    sp.dma_start(w_y[a][:], w_out[p * P:(p + 1) * P]).then_inc(w_y_loaded, 16)
                    return
                sp.wait_ge(proj_ready, p * UNITS + UNITS + NB)
                pairs.double_queries(sp, 1 - a)
                for qb in range(1, NB):
                    store_denominators(p, qb)

            run_pairs(sp, pair)
            sp.wait_ge(factor_stored, 16 * (PAIRS - 1))
            for stored in den_stored:
                sp.wait_ge(stored, 16 * NB // 2 * (PAIRS - 1))

        @block.tensor
        def _(pe):
            def scores_of(g, a, n):
                first, width, _ = queries(n)
                wait(pe, tanh_done, g - 1)
                for h in range(2):
                    keys = k_hl[a][h][:, blk(STEPS[n][1], P)]
                    out = scores[:, n % 2, h, 0:width]
                    nc.tensor.matmul(out, keys, q_hi[a][h][:, first:first + width], start=True, stop=False)
                    last = nc.tensor.matmul(out, keys, q_lo[a][h][:, first:first + width], start=False, stop=True)
                last.then_inc(scores_ready, 1)

            def outputs_of(p, g, a, n):
                qb, j = STEPS[n]
                _, width, at = queries(n)
                if DIAG[n]:
                    pe.wait_ge(masked, p * ND + sum(DIAG[:n]) + 1)
                else:
                    pe.wait_ge(exp_done, g + 1)
                bank = PLACE[qb] % 2
                if j == 0:
                    wait(pe, out_copied, p * NB + PLACE[qb] - 1)
                for h in range(2):
                    last = nc.tensor.matmul(o_ps[h * DH:(h + 1) * DH, bank, at:BLK], v[a][:, j, h * DH:(h + 1) * DH],
                                            probs[:, n % RING, h, 0:width], start=(j == 0), stop=(n == LAST[qb]),
                                            skip_group_check=True)
                last.then_inc(pv_done, 1)

            def denominators(p, a, qb):
                pe.wait_ge(summed, p * NS + LAST[qb] + 1)
                wait(pe, den_copied, p * NB + PLACE[qb])
                for h in range(2):
                    last = nc.tensor.matmul(den_ps[rows_of(h)], ones[:], psums[PLACE[qb] % 2][:, h], start=True, stop=True)
                last.then_inc(den_computed, 1)

            def output_projection(p, a, b, last):
                if not last:
                    pe.wait_ge(proj_ready, (p + 1) * UNITS + sum(at <= n_of_y[b] for at in PROJ_AT))
                wait(pe, y_added, (p - 1) * NB + b)
                if b == 0:
                    pe.wait_ge(w_y_loaded, p * 16)
                pe.wait_ge(normed, (p - 1) * NB + b + 1)
                nc.tensor.matmul(proj_ps[:], w_y[1 - a][:], factor_b[:, blk(b)], start=True, stop=True).then_inc(y_computed, 1)

            n_of_y = {b: n for n, b in Y_AT.items()}

            def pair(p, a, last):
                for n in range(NS):
                    g = p * NS + n
                    if n + 2 < NS:
                        scores_of(g + 2, a, n + 2)
                    elif not last:
                        if n + 2 == NS:
                            pe.wait_ge(proj_ready, (p + 2) * UNITS)
                            pe.wait_ge(q_doubled, (p + 2) * 64)
                            wait(pe, v_loaded, p * 16)
                        scores_of(g + 2, 1 - a, n + 2 - NS)
                    if n in PROJ_AT and not last:
                        if n == min(PROJ_AT):
                            pe.wait_ge(weights.split, p + 2)
                        wait(pe, proj_ready, (p + 1) * UNITS + PROJ_AT[n])
                        wait(pe, y_added, (p - 1) * NB + sum(at < n for at in Y_AT))
                        pairs.project(PROJ_AT[n], weights, x_hi, x_lo, proj_ps[:])
                    if n in Y_AT and not is_first(p):
                        output_projection(p, a, Y_AT[n], last)
                    for block_done in due(p, a, n, DEN_LAG):
                        denominators(*block_done)
                    if n > 0:
                        outputs_of(p, g - 1, a, n - 1)
                    elif not is_first(p):
                        outputs_of(p - 1, g - 1, 1 - a, NS - 1)

            pe.wait_ge(q_doubled, 64)
            scores_of(0, 0, 0)
            scores_of(1, 0, 1)
            pe.wait_ge(init_ready, 2)
            run_pairs(pe, pair)
            outputs_of(PAIRS - 1, PAIRS * NS - 1, 1, NS - 1)
            for n in range(NS):
                for block_done in due(PAIRS, 0, n, DEN_LAG):
                    denominators(*block_done)
            pe.wait_ge(w_y_loaded, PAIRS * 16)
            for place, qb in enumerate(blocks_in_place()):
                pe.wait_ge(divided, place + 1)
                nc.tensor.matmul(scores[:, place // 2, place % 2], w_y[1][:], out_t[1][:, blk(qb)], start=True, stop=True).then_inc(y_computed, 1)

        @block.scalar
        def _(act):
            def tanh(g, n):
                width = queries(n)[1]
                act.wait_ge(scores_ready, g + 1)
                wait(act, exp_done, g - 1)
                nc.scalar.activation(capped[:, n % 2, :, 0:width], scores[:, n % 2, :, 0:width], ACT.Tanh,
                                     scale=DH ** -0.5 / SOFTCAP).then_inc(tanh_done, 1)

            def exp(g, n):
                width = queries(n)[1]
                act.wait_ge(tanh_done, g + 1)
                wait(act, pv_done, g + 1 - RING)
                wait(act, summed, g + 1 - RING)
                nc.scalar.activation(probs[:, n % RING, :, 0:width], capped[:, n % 2, :, 0:width], ACT.Exp,
                                     scale=SOFTCAP).then_inc(exp_done, 1)

            def pair(p, a, last):
                for n in range(NS):
                    g = p * NS + n
                    if not (last and n == NS - 1):
                        tanh(g + 1, (n + 1) % NS)
                    exp(g, n)

            act.wait_ge(scores_ready, 1)
            width = queries(0)[1]
            nc.scalar.activation(capped[:, 0, :, 0:width], scores[:, 0, :, 0:width], ACT.Tanh,
                                 scale=DH ** -0.5 / SOFTCAP).then_inc(tanh_done, 1)
            run_pairs(act, pair)

        @block.gpsimd
        def _(pool):
            def mask(p, g, n):
                pool.wait_ge(exp_done, g + 1)
                tile = probs[:, n % RING, :, 0:P]
                nc.gpsimd.tensor_tensor(tile, tile, causal[:], ALU.mult).then_inc(masked, 1)

            def normalise(p, a, b):
                if b == 0:
                    pool.wait_ge(factor_loaded, p * 32)
                    pool.wait_ge(out_copied, p * NB)
                part = factor_b[:, blk(b)]
                nc.gpsimd.tensor_tensor(part, out_t[1 - a][:, blk(b)], part, ALU.mult).then_inc(normed, 1)

            def pair(p, a, last):
                for n in range(NS):
                    if DIAG[n]:
                        mask(p, p * NS + n, n)
                    if n in NORM_AT and not is_first(p):
                        normalise(p, a, NORM_AT[n])

            nc.gpsimd.memset(ones[:], 1.0).then_inc(init_ready, 1)
            nc.gpsimd.memset(causal[:], 1.0).then_inc(init_ready, 1)
            pool.wait_ge(init_ready, 2)
            nc.gpsimd.affine_select(out=causal[:], in_=causal[:], pattern=[[0, 2], [1, P]], compare_op=ALU.is_ge, fill=0.0,
                                    base=0, channel_multiplier=-1).then_inc(init_ready, 1)
            pool.wait_ge(init_ready, 3)
            sems.clear(pool, "ln0")
            run_pairs(pool, pair)

        @block.vector
        def _(dve):
            def sum_probs(p, g, n):
                qb, j = STEPS[n]
                _, width, at = queries(n)
                if DIAG[n]:
                    dve.wait_ge(masked, p * ND + sum(DIAG[:n]) + 1)
                else:
                    dve.wait_ge(exp_done, g + 1)
                new, total = probs[:, n % RING, :, 0:width], psums[PLACE[qb] % 2][:, :, at:BLK]
                if j == 0:
                    wait(dve, den_computed, p * NB + PLACE[qb] - 1)
                    nc.vector.tensor_copy(total, new).then_inc(summed, 1)
                else:
                    dve.wait_ge(summed, g)
                    nc.vector.tensor_tensor(total, total, new, ALU.add).then_inc(summed, 1)

            def split_weights(p):
                wait(dve, proj_computed, p * UNITS)
                weights.split_pair(dve, p)

            def split_projection(count, a, u):
                dve.wait_ge(proj_computed, count + 1)
                for h, hi in enumerate(pairs.leading(a, u)):
                    leading = nc.vector.tensor_copy(hi, proj_ps[rows_of(h)])
                leading.then_inc(proj_hi_ready, 1)
                dve.wait_ge(proj_hi_ready, count + 1)
                pairs.subtract_leading(a, u, proj_ps)

            def copy_outputs(p, a, qb):
                dve.wait_ge(pv_done, p * NS + LAST[qb] + 1)
                if PLACE[qb] == 0:
                    wait(dve, normed, (p - 1) * NB)
                nc.vector.tensor_copy(out_t[a][:, blk(qb)], o_ps[:, PLACE[qb] % 2]).then_inc(out_copied, 1)

            def copy_denominators(p, a, qb):
                place = PLACE[qb]
                dve.wait_ge(den_computed, p * NB + place + 1)
                wait(dve, den_stored[place % 2], (p * (NB // 2) + place // 2) * 16)
                nc.vector.tensor_copy(den_row[:, place % 2], den_ps[:]).then_inc(den_copied, 1)

            def add_outputs(p, b):
                dve.wait_ge(y_computed, (p - 1) * NB + b + 1)
                nc.vector.tensor_tensor(x[:, blk(b)], x[:, blk(b)], proj_ps[:], ALU.add).then_inc(y_added, 1)

            def factors(p):
                dve.wait_ge(den_loaded, p * 32)
                nc.vector.reciprocal(rden[:], den_r[:]).then_inc(rden_ready, 1)
                dve.wait_ge(rden_ready, p)
                wait(dve, factor_stored, (p - 1) * 16)
                nc.vector.tensor_tensor(factor[:], rden[:], gate_r[:], ALU.mult).then_inc(factor_ready, 1)

            def pair(p, a, last):
                for n in range(NS):
                    sum_probs(p, p * NS + n, n)
                    if not last:
                        if n == SPLIT_AT:
                            split_weights(p + 1)
                        if n in PROJ_AT:
                            if n == min(PROJ_AT):
                                wait(dve, scores_ready, p * NS)
                            split_projection((p + 1) * UNITS + PROJ_AT[n], 1 - a, PROJ_AT[n])
                    if n == FACTOR_AT and not is_first(p):
                        factors(p)
                    if n in Y_AT and not is_first(p):
                        add_outputs(p, Y_AT[n])
                    finish(p, a, n)

            def divide(qb):
                place, done = PLACE[qb], (PAIRS - 1) * NB + PLACE[qb] + 1
                rden, outputs = den_row[:, place % 2], out_t[1][:, blk(qb)]
                dve.wait_ge(den_computed, done)
                dve.wait_ge(den_stored[place % 2], 16 * NB // 2 * (PAIRS - 1))
                nc.vector.reciprocal(rden, den_ps[:]).then_inc(den_copied, 1)
                dve.wait_ge(gate_loaded, 32)
                dve.wait_ge(den_copied, done)
                nc.vector.tensor_tensor(rden, rden, gate_b[:, blk(qb)], ALU.mult).then_inc(gated, 1)
                dve.wait_ge(gated, place + 1)
                dve.wait_ge(out_copied, done)
                nc.vector.tensor_tensor(outputs, outputs, rden, ALU.mult).then_inc(divided, 1)

            def finish(p, a, n):
                for block_done in due(p, a, n, OUT_LAG):
                    copy_outputs(*block_done)
                for of, parity, qb in due(p, a, n, DEN_COPY_LAG):
                    if isinstance(of, int) and of == PAIRS - 1:
                        divide(qb)
                    else:
                        copy_denominators(of, parity, qb)

            run_pairs(dve, pair)
            for n in range(NS):
                finish(PAIRS, 0, n)
            for place, qb in enumerate(blocks_in_place()):
                dve.wait_ge(y_computed, (PAIRS - 1) * NB + place + 1)
                nc.vector.tensor_tensor(x[:, blk(qb)], x[:, blk(qb)], scores[:, place // 2, place % 2], ALU.add)


ROUTED = 8
EXPERTS = 1 + ROUTED
TOP_K = 2
HID = 256
CHUNKS = HID // P
UPB = EXPERTS * CHUNKS
RH = 6
RG = 3
LEAD = 3


SPLIT_LEAD = 3


class MixtureWeights:

    def __init__(self, ctx, nc, sems):
        sb = lambda n, s, d=F32: ctx.enter_context(nc.sbuf_tensor(f"mw_{n}", s, d))
        self.nc = nc
        self.gu_hi, self.gu_lo = sb("gu_hi", [P, EXPERTS, 2, HID], F32R), sb("gu_lo", [P, EXPERTS, 2, HID], F32R)
        self.d_hi, self.d_lo = sb("d_hi", [P, EXPERTS, CHUNKS, P], F32R), sb("d_lo", [P, EXPERTS, CHUNKS, P], F32R)
        self.router = sb("router", [P, ROUTED])
        self.bias = sb("bias", [P, ROUTED])
        self.ident = sb("ident", [P, P])
        self.before = sb("before", [P, ROUTED, ROUTED])
        self.router_loaded, self.ones_ready = sems("mw", "router_loaded"), sems("mw", "ones_ready")
        self.ident_ready, self.before_ready = sems("mw", "ident_ready"), sems("mw", "before_ready")
        self.loaded = [sems("mw", f"loaded{e}") for e in range(EXPERTS)]

    def allocate_raw(self, ctx):
        self.gu = ctx.enter_context(self.nc.sbuf_tensor("mw_gu", [P, EXPERTS, 2, HID], F32))
        self.d = ctx.enter_context(self.nc.sbuf_tensor("mw_d", [P, EXPERTS, CHUNKS, P], F32))

    def load(self, sp, wg_t, wu_t, wd_t, wr_t, rb):
        sp.dma_start(self.router[:], wr_t).then_inc(self.router_loaded, 16)
        sp.dma_start(self.bias[:], rb.unsqueeze(0).broadcast_to([P, ROUTED])).then_inc(self.router_loaded, 16)
        for e in range(EXPERTS):
            sp.dma_start(self.gu[:, e, 0], wg_t[e]).then_inc(self.loaded[e], 16)
            sp.dma_start(self.gu[:, e, 1], wu_t[e]).then_inc(self.loaded[e], 16)
            sp.dma_start(self.d[:, e], wd_t[e].rearrange("(c i) h -> i c h", c=CHUNKS)).then_inc(self.loaded[e], 16)

    def make_constants(self, pool):
        self.nc.gpsimd.memset(self.before[:], 1.0).then_inc(self.ones_ready, 1)
        self.nc.gpsimd.memset(self.ident[:], 1.0).then_inc(self.ones_ready, 1)
        pool.wait_ge(self.ones_ready, 2)
        self.nc.gpsimd.affine_select(out=self.before[:], in_=self.before[:], pattern=[[1, ROUTED], [-1, ROUTED]], compare_op=ALU.is_gt,
                                     fill=0.0, base=0, channel_multiplier=0).then_inc(self.before_ready, 1)
        self.nc.gpsimd.affine_select(out=self.ident[:], in_=self.ident[:], pattern=[[1, P]], compare_op=ALU.is_equal, fill=0.0,
                                     base=0, channel_multiplier=-1).then_inc(self.ident_ready, 1)


def experts(nc, sems, x, x_hi, x_lo, weights, probs, cw_dram, name, split):
    with ExitStack() as ctx:
        sb = lambda n, s, d=F32: ctx.enter_context(nc.sbuf_tensor(f"{name}_{n}", s, d))
        sem = lambda n: sems("ex", n)
        E = ROUTED
        above = sb("above", [P, NT, E, E])
        equal = sb("equal", [P, NT, E, E])
        rank = sb("rank", [P, NT, E])
        cw_n = sb("cw_n", [P, E, NT])
        cw_t = sb("cw_t", [E * NT, P])
        silu = sb("silu", [P, RG, BLK])
        hid = sb("hid", [P, RG, BLK])
        hid_hi = sb("hid_hi", [P, RH, BLK], F32R)
        hid_lo = sb("hid_lo", [P, RH, BLK], F32R)
        weighted = sb("weighted", [P, RG, BLK])
        cw = sb("cw", [P, E, BLK])
        gate_ps = ctx.enter_context(nc.psum_tensor(f"{name}_gate_ps", [P, RG, BLK], F32))
        up_ps = ctx.enter_context(nc.psum_tensor(f"{name}_up_ps", [P, RG, BLK], F32))
        down_ps = ctx.enter_context(nc.psum_tensor(f"{name}_down_ps", [P, 1, BLK], F32))
        route_ps = ctx.enter_context(nc.psum_tensor(f"{name}_route_ps", [E * NT, P], F32))
        compared, step, cw_ready, cw_turned, cw_copied, stored = sem("compared"), sem("step"), sem("cw_ready"), sem("cw_turned"), sem("cw_copied"), sem("stored")
        w_hi_ready, w_split = sem("w_hi_ready"), sem("w_split")
        cw_loaded = [sem(f"cw_loaded{e}") for e in range(1, EXPERTS)]
        gate_ready, up_ready, silu_ready, hid_ready = sem("gate_ready"), sem("up_ready"), sem("silu_ready"), sem("hid_ready")
        hi_ready, lo_ready, down_ready, scaled, added = sem("hi_ready"), sem("lo_ready"), sem("down_ready"), sem("scaled"), sem("added")
        block = ctx.enter_context(nc.Block())

        def run_blocks(eng, body):
            body(0, True, False)
            with eng.Fori(1, NB - 1) as b:
                body(b, False, False)
            body(NB - 1, False, True)

        @block.sync
        def _(sp):
            def load(b, e):
                sp.dma_start(cw[:, e - 1], cw_dram[e - 1:e, bass.ds(b * BLK, BLK)].broadcast_to([P, BLK])).then_inc(cw_loaded[e - 1], 16)

            sp.wait_ge(cw_copied, 1)
            sp.dma_start(cw_dram.rearrange("e (t k) -> (e t) k", k=P), cw_t[:]).then_inc(stored, 16)
            sp.wait_ge(stored, 16)
            for e in range(1, EXPERTS):
                load(0, e)
            with sp.Fori(0, NB - 1) as b:
                for e in range(1, EXPERTS):
                    sp.wait_ge(scaled, b * EXPERTS + e + 1)
                    load(b + 1, e)

        @block.tensor
        def _(pe):
            def gate_up(b, i):
                e, c = i // CHUNKS, i % CHUNKS
                wait(pe, hid_ready, b * UPB + i - RG + 1)
                if split and isinstance(b, int) and b == 0:
                    pe.wait_ge(w_split, 2 * e + 2)
                xs_hi, xs_lo = x_hi[:, bass.ds(b * BLK, BLK)], x_lo[:, bass.ds(b * BLK, BLK)]
                for which, out, ready in ((0, gate_ps, gate_ready), (1, up_ps, up_ready)):
                    out = out[:, i % RG]
                    hi, lo = weights.gu_hi[:, e, which, blk(c, P)], weights.gu_lo[:, e, which, blk(c, P)]
                    nc.tensor.matmul(out, hi, xs_hi, start=True, stop=False)
                    nc.tensor.matmul(out, hi, xs_lo, start=False, stop=False)
                    nc.tensor.matmul(out, lo, xs_hi, start=False, stop=True).then_inc(ready, 1)

            def down(b, e):
                wait(pe, scaled, b * EXPERTS + e)
                for c in range(CHUNKS):
                    i = e * CHUNKS + c
                    hi, lo = weights.d_hi[:, e, c], weights.d_lo[:, e, c]
                    wait(pe, hi_ready, b * UPB + i + 1)
                    nc.tensor.matmul(down_ps[:, 0], hi, hid_hi[:, i % RH], start=(c == 0), stop=False)
                    nc.tensor.matmul(down_ps[:, 0], lo, hid_hi[:, i % RH], start=False, stop=False)
                    wait(pe, lo_ready, b * UPB + i + 1)
                    mm = nc.tensor.matmul(down_ps[:, 0], hi, hid_lo[:, i % RH], start=False, stop=(c == CHUNKS - 1))
                mm.then_inc(down_ready, 1)

            def body(b, first, last):
                for i in range(UPB):
                    if i + LEAD < UPB:
                        gate_up(b, i + LEAD)
                    elif not last:
                        gate_up(b + 1, i + LEAD - UPB)
                    if i % CHUNKS == CHUNKS - 1:
                        down(b, i // CHUNKS)

            for i in range(LEAD):
                gate_up(0, i)
            pe.wait_ge(weights.ident_ready, 1)
            pe.wait_ge(cw_ready, 1)
            nc.tensor.transpose(route_ps[:], cw_n[:].rearrange("p e t -> p (e t)"), weights.ident[:]).then_inc(cw_turned, 1)
            run_blocks(pe, body)

        @block.scalar
        def _(act):
            def silu_of(b, i):
                wait(act, gate_ready, b * UPB + i + 1)
                wait(act, hid_ready, b * UPB + i - RG + 1)
                nc.scalar.activation(silu[:, i % RG], gate_ps[:, i % RG], ACT.Silu).then_inc(silu_ready, 1)

            def lead_weights(e):
                act.wait_ge(weights.loaded[e], 48)
                nc.scalar.copy(weights.gu_hi[:, e], weights.gu[:, e]).then_inc(w_hi_ready, 1)
                nc.scalar.copy(weights.d_hi[:, e], weights.d[:, e]).then_inc(w_hi_ready, 1)

            def body(b, first, last):
                for i in range(UPB):
                    if i + 1 < UPB:
                        silu_of(b, i + 1)
                    elif not last:
                        silu_of(b + 1, 0)
                    wait(act, hid_ready, b * UPB + i + 1)
                    wait(act, down_ready, b * EXPERTS + (i - RH) // CHUNKS + 1)
                    nc.scalar.copy(hid_hi[:, i % RH], hid[:, i % RG]).then_inc(hi_ready, 1)
                    if split and first and i % CHUNKS == 0 and i // CHUNKS + SPLIT_LEAD < EXPERTS:
                        lead_weights(i // CHUNKS + SPLIT_LEAD)

            if split:
                for e in range(SPLIT_LEAD):
                    lead_weights(e)
            silu_of(0, 0)
            run_blocks(act, body)

        @block.vector
        def _(dve):
            def rest_weights(e):
                dve.wait_ge(w_hi_ready, 2 * e + 2)
                nc.vector.tensor_tensor(weights.gu_lo[:, e], weights.gu[:, e], weights.gu_hi[:, e].bitcast(F32), ALU.subtract).then_inc(w_split, 1)
                nc.vector.tensor_tensor(weights.d_lo[:, e], weights.d[:, e], weights.d_hi[:, e].bitcast(F32), ALU.subtract).then_inc(w_split, 1)

            def hidden(b, i):
                wait(dve, up_ready, b * UPB + i + 1)
                wait(dve, silu_ready, b * UPB + i + 1)
                wait(dve, hi_ready, b * UPB + i - RG + 1)
                wait(dve, lo_ready, b * UPB + i - RG + 1)
                nc.vector.tensor_tensor(hid[:, i % RG], silu[:, i % RG], up_ps[:, i % RG], ALU.mult).then_inc(hid_ready, 1)

            def scale(b, e):
                wait(dve, down_ready, b * EXPERTS + e + 1)
                wait(dve, added, b * EXPERTS + e - RG + 1)
                if e == 0:
                    nc.vector.tensor_copy(weighted[:, e % RG], down_ps[:, 0]).then_inc(scaled, 1)
                else:
                    wait(dve, cw_loaded[e - 1], b * 16 + 16)
                    nc.vector.tensor_tensor(weighted[:, e % RG], cw[:, e - 1], down_ps[:, 0], ALU.mult).then_inc(scaled, 1)

            def body(b, first, last):
                for i in range(UPB):
                    if i + 1 < UPB:
                        hidden(b, i + 1)
                    elif not last:
                        hidden(b + 1, 0)
                    wait(dve, hi_ready, b * UPB + i + 1)
                    wait(dve, down_ready, b * EXPERTS + (i - RH) // CHUNKS + 1)
                    nc.vector.tensor_tensor(hid_lo[:, i % RH], hid[:, i % RG], hid_hi[:, i % RH].bitcast(F32), ALU.subtract).then_inc(lo_ready, 1)
                    if i % CHUNKS == 0 and i:
                        scale(b, i // CHUNKS - 1)
                    elif i == 0 and not first:
                        scale(b - 1, EXPERTS - 1)
                    if split and first and i % CHUNKS == 0 and i // CHUNKS + SPLIT_LEAD < EXPERTS:
                        rest_weights(i // CHUNKS + SPLIT_LEAD)
                if last:
                    scale(b, EXPERTS - 1)

            if split:
                for e in range(SPLIT_LEAD):
                    rest_weights(e)
            this = probs[:].unsqueeze(3).broadcast_to([P, NT, E, E])
            other = probs[:].unsqueeze(2).broadcast_to([P, NT, E, E])
            nc.vector.tensor_tensor(above[:], other, this, ALU.is_gt).then_inc(compared, 1)
            nc.vector.tensor_tensor(equal[:], other, this, ALU.is_equal).then_inc(compared, 1)
            dve.wait_ge(weights.before_ready, 1)
            dve.wait_ge(compared, 2)
            nc.vector.tensor_tensor(equal[:], equal[:], weights.before[:].unsqueeze(1).broadcast_to([P, NT, E, E]), ALU.mult).then_inc(step, 1)
            dve.wait_ge(step, 1)
            nc.vector.tensor_tensor(above[:], above[:], equal[:], ALU.add).then_inc(step, 1)
            dve.wait_ge(step, 2)
            nc.vector.tensor_reduce(rank[:], above[:], AX.X, ALU.add).then_inc(step, 1)
            dve.wait_ge(step, 3)
            nc.vector.scalar_tensor_tensor(out=cw_n[:].rearrange("p e t -> p t e"), in0=rank[:], scalar=float(TOP_K), in1=probs[:],
                                           op0=ALU.is_lt, op1=ALU.mult).then_inc(cw_ready, 1)
            dve.wait_ge(cw_turned, 1)
            nc.vector.tensor_copy(cw_t[:], route_ps[:]).then_inc(cw_copied, 1)
            hidden(0, 0)
            run_blocks(dve, body)

        @block.gpsimd
        def _(pool):
            for b in range(NB):
                for e in range(EXPERTS):
                    xs = x[:, blk(b)]
                    pool.wait_ge(scaled, b * EXPERTS + e + 1)
                    wait(pool, added, b * EXPERTS + e)
                    nc.gpsimd.tensor_tensor(xs, xs, weighted[:, e % RG], ALU.add).then_inc(added, 1)


HB = 16
DB = P // HB
PAD = 32
GROUPS = HB * PAD // P
PER_G = HB // GROUPS
STACK = 4


class LinearWeights:

    def __init__(self, ctx, nc, sems):
        sb = lambda n, s: ctx.enter_context(nc.sbuf_tensor(f"lw_{n}", s, F32))
        self.nat = sb("nat", [P, 3, P])
        self.bias_rep = sb("bias_rep", [P, 2, GROUPS])
        self.bq_c = sb("bq_c", [P, 1])
        self.bo_c = sb("bo_c", [P, 1])
        self.bkv_r = sb("bkv_r", [P, 2, P])
        self.loaded = sems("lw", "loaded")

    def load(self, sp, wq_t, wk_t, wv_t, bq, bq_groups, bk, bk_groups, bv, bo):
        for i, src in enumerate((wq_t, wk_t, wv_t)):
            sp.dma_start(self.nat[:, i], src).then_inc(self.loaded, 16)
        sp.dma_start(self.bq_c[:], bq.unsqueeze(1)).then_inc(self.loaded, 16)
        sp.dma_start(self.bo_c[:], bo.unsqueeze(1)).then_inc(self.loaded, 16)
        for i, src in enumerate((bq_groups, bk_groups)):
            for r in range(STACK):
                sp.dma_start(self.bias_rep[r * PAD:(r + 1) * PAD, i], src).then_inc(self.loaded, 16)
        for i, src in enumerate((bk, bv)):
            sp.dma_start(self.bkv_r[:, i], src.unsqueeze(0).broadcast_to([P, P])).then_inc(self.loaded, 16)
        sp.wait_ge(self.loaded, 16 * (7 + 2 * STACK))


def linear_attention(nc, sems, x, xn, w, wo_t):
    with ExitStack() as ctx:
        sb_in = lambda c, n, s, d=F32: c.enter_context(nc.sbuf_tensor(f"la_{n}", s, d))
        sb = lambda n, s, d=F32: sb_in(ctx, n, s, d)
        psum = lambda c, n, s: c.enter_context(nc.psum_tensor(f"la_{n}", s, F32))
        sem = lambda n: sems("la", n)
        wo = sb("wo", [P, P])
        q_t = sb("q_t", [P, T])
        q_st = sb("q_st", [P, GROUPS, T], F32R)
        k_st = sb("k_st", [P, GROUPS, T], F32R)
        kv_n = sb("kv_n", [P, NT, 2, P])
        ones = sb("ones", [P, HB])
        own_lo, own = sb("own_lo", [P, HB]), sb("own", [P, HB])
        own_st = sb("own_st", [P, PER_G])
        out_t = sb("out_t", [P, 2, BLK])

        const_ready, w_rep_ready = sem("const_ready"), sem("w_rep_ready")
        wo_loaded, own_lo_ready, own_ready, own_st_ready = sem("wo_loaded"), sem("own_lo_ready"), sem("own_ready"), sem("own_st_ready")
        qk_computed, qk_hi_ready, lo_ready, kv_computed, kv_ready = sem("qk_computed"), sem("qk_hi_ready"), sem("lo_ready"), sem("kv_computed"), sem("kv_ready")

        units = [(b, kind, g) for b in range(NB) for kind, g in [("q_t", 0)] + [(kind, g) for g in range(GROUPS) for kind in "qk"]]
        NU = len(units)
        lo_steps = [sum({"q_t": 0, "q": 1, "k": 2}[kind] for _, kind, _ in units[:n + 1]) for n in range(NU)]
        KV_AFTER = {2 * t + 2: t for t in range(NT)}
        BANKS = 6

        with ExitStack() as c:
            w_rep = sb_in(c, "w_rep", [P, 2, GROUPS, STACK, PAD])
            qk_ps = psum(c, "qk_ps", [P, BANKS, BLK])
            kv_ps = psum(c, "kv_ps", [P, 2, BLK])
            block = c.enter_context(nc.Block())

            @block.gpsimd
            def _(pool):
                sems.clear(pool, "ln1", "ex")
                nc.gpsimd.memset(ones[:], 1.0).then_inc(const_ready, 1)
                pool.wait_ge(const_ready, 1)
                nc.gpsimd.affine_select(out=own_lo[:], in_=ones[:], pattern=[[-DB, HB]], compare_op=ALU.is_ge, fill=0.0,
                                        base=0, channel_multiplier=1).then_inc(own_lo_ready, 1)
                pool.wait_ge(own_lo_ready, 1)
                nc.gpsimd.affine_select(out=own[:], in_=own_lo[:], pattern=[[DB, HB]], compare_op=ALU.is_gt, fill=0.0,
                                        base=DB, channel_multiplier=-1).then_inc(own_ready, 1)

            @block.sync
            def _(sp):
                for j in range(PER_G):
                    for g in range(GROUPS):
                        at, head = j * PAD + g * DB, g * PER_G + j
                        sp.dma_start(wo[at:at + DB], wo_t[head * DB:(head + 1) * DB]).then_inc(wo_loaded, 16)
                sp.wait_ge(wo_loaded, 16 * HB)

            @block.tensor
            def _(pe):
                def keys_and_values(t):
                    if t >= 2:
                        pe.wait_ge(kv_ready, t - 1)
                    nc.tensor.matmul(kv_ps[:, t % 2, 0:2 * P], xn[:, blk(t, P)], w.nat[:, 1:3].rearrange("p w d -> p (w d)"),
                                     start=True, stop=True).then_inc(kv_computed, 1)

                for n, (b, kind, g) in enumerate(units):
                    if n == 1:
                        pe.wait_ge(w_rep_ready, 2)
                    if n >= BANKS:
                        pe.wait_ge(qk_hi_ready, n - BANKS + 1)
                        pe.wait_ge(lo_ready, max(1, lo_steps[n - BANKS]))
                    weight = w.nat[:, 0] if kind == "q_t" else w_rep[:, "qk".index(kind), g].rearrange("p r d -> p (r d)")
                    nc.tensor.matmul(qk_ps[:, n % BANKS], weight, xn[:, blk(b)], start=True, stop=True).then_inc(qk_computed, 1)
                    if n in KV_AFTER:
                        keys_and_values(KV_AFTER[n])

            @block.scalar
            def _(act):
                for n, (b, kind, g) in enumerate(units):
                    act.wait_ge(qk_computed, n + 1)
                    if kind == "q_t":
                        out, bias = q_t[:, blk(b)], w.bq_c[:, 0:1]
                    else:
                        out, bias = (q_st if kind == "q" else k_st)[:, g, blk(b)], w.bias_rep[:, "qk".index(kind), g:g + 1]
                    nc.scalar.activation(out, qk_ps[:, n % BANKS], ACT.Identity, bias=bias).then_inc(qk_hi_ready, 1)

            @block.vector
            def _(dve):
                for i in range(2):
                    nc.vector.tensor_copy(w_rep[:, i], w.nat[:, i].rearrange("p (g d) -> p g d", g=GROUPS).unsqueeze(2)
                                          .broadcast_to([P, GROUPS, STACK, PAD])).then_inc(w_rep_ready, 1)
                dve.wait_ge(own_ready, 1)
                nc.vector.tensor_reduce(own_st[:], own[:].rearrange("p (r j) -> p j r", j=PER_G), AX.X, ALU.add).then_inc(own_st_ready, 1)
                def add_bias(t):
                    dve.wait_ge(kv_computed, t + 1)
                    nc.vector.tensor_tensor(kv_n[:, t], w.bkv_r[:], kv_ps[:, t % 2, 0:2 * P].rearrange("p (w d) -> p w d", w=2), ALU.add).then_inc(kv_ready, 1)

                for n, (b, kind, g) in enumerate(units):
                    if n in KV_AFTER:
                        add_bias(KV_AFTER[n])
                    if kind == "q_t":
                        continue
                    dve.wait_ge(qk_hi_ready, n + 1)
                    rows = [slice(2 * PAD, P)] if kind == "q" else [slice(PAD, 2 * PAD), slice(3 * PAD, P)]
                    for r in rows:
                        part = (q_st if kind == "q" else k_st)[r, g, blk(b)]
                        nc.vector.scalar_tensor_tensor(out=part, in0=qk_ps[r, n % BANKS], scalar=w.bias_rep[r, "qk".index(kind), g:g + 1],
                                                       in1=part.bitcast(F32), op0=ALU.add, op1=ALU.subtract).then_inc(lo_ready, 1)

        SB = HB * P // BLK
        scores_ready, scores_copied, q_x_ready, masked_ready = sem("scores_ready"), sem("scores_copied"), sem("q_x_ready"), sem("masked_ready")
        sums_ready, state_ready, out_ready, out_copied, y_ready, y_added = sem("sums_ready"), sem("state_ready"), sem("out_ready"), sem("out_copied"), sem("y_ready"), sem("y_added")
        state_zeroed, v_wide_ready = sem("state_zeroed"), sem("v_wide_ready")
        PER_Y = BLK // P
        with ExitStack() as c:
            q_x = sb_in(c, "q_x", [P, 2, GROUPS, PER_G, P], F32R)
            masked = sb_in(c, "masked", [P, 2, HB, P])
            state = sb_in(c, "state", [P, 2, P])
            v_wide = sb_in(c, "v_wide", [P, 2, GROUPS * (P + DB)])
            scores = psum(c, "scores", [P, HB, P])
            out_ps = psum(c, "out_ps", [P, 2, BLK])
            sums = psum(c, "sums", [P, HB, DB])
            y_ps = psum(c, "y_ps", [P, BLK])
            block = c.enter_context(nc.Block())

            @block.tensor
            def _(pe):
                def scores_of(t):
                    for g in range(GROUPS):
                        if t == 0:
                            pe.wait_ge(q_x_ready, g + 1)
                        elif g == 0:
                            pe.wait_ge(q_x_ready, t + GROUPS)
                        if t > 0:
                            pe.wait_ge(scores_copied, (t - 1) * SB + g + 1)
                        nc.tensor.matmul(scores[:, g * PER_G:(g + 1) * PER_G], k_st[:, g, blk(t, P)], q_x[:, t % 2, g],
                                         start=True, stop=True).then_inc(scores_ready, 1)

                def outputs_of(t):
                    if t >= 2:
                        pe.wait_ge(out_copied, t - 1)
                    if t > 0:
                        pe.wait_ge(state_ready, t)
                    nc.tensor.matmul(out_ps[:, t % 2, 0:P], state[:, t % 2], q_t[:, blk(t, P)], start=True, stop=False, skip_group_check=True)
                    pe.wait_ge(v_wide_ready, t + 1)
                    for g in range(GROUPS):
                        pe.wait_ge(masked_ready, t * SB + g + 1)
                        for j in range(PER_G):
                            h = g * PER_G + j
                            mm = nc.tensor.matmul(out_ps[j * PAD:(j + 1) * PAD, t % 2, 0:P], v_wide[:, t % 2, blk(h, PAD)], masked[:, t % 2, h],
                                                  start=False, stop=(g == GROUPS - 1), skip_group_check=True)
                    mm.then_inc(out_ready, 1)

                def project(b):
                    pe.wait_ge(out_copied, (b + 1) * PER_Y)
                    if b > 0:
                        pe.wait_ge(y_added, b)
                    nc.tensor.matmul(y_ps[:], wo[:], out_t[:, b % 2], start=True, stop=True).then_inc(y_ready, 1)

                scores_of(0)
                pe.wait_ge(state_zeroed, 2)
                for t in range(NT):
                    if t + 1 < NT:
                        if t > 0:
                            pe.wait_ge(state_ready, t)
                        nc.tensor.matmul(sums[:].rearrange("p h d -> p (h d)"), kv_n[:, t, 0], kv_n[:, t, 1], start=(t == 0),
                                         stop=True, skip_group_check=True).then_inc(sums_ready, 1)
                        scores_of(t + 1)
                    outputs_of(t)
                    if t % PER_Y == 0 and t > 0:
                        project(t // PER_Y - 1)
                project(NB - 1)

            @block.scalar
            def _(act):
                act.wait_ge(state_zeroed, 2)
                for t in range(NT):
                    if t >= 2:
                        act.wait_ge(out_ready, t - 1)
                    wide = v_wide[:, t % 2].rearrange("p (g x) -> p g x", g=GROUPS)[:, :, 0:P].rearrange("p g (j m) -> p g j m", j=PER_G)
                    nc.scalar.copy(wide[:, :, :, 0:DB], kv_n[:, t, 1].rearrange("p (g j d) -> p g j d", g=GROUPS, j=PER_G)).then_inc(v_wide_ready, 1)
                    for g in range(GROUPS):
                        act.wait_ge(scores_ready, t * SB + g + 1)
                        if t >= 2 and g == 0:
                            act.wait_ge(out_ready, t - 1)
                        heads = slice(g * PER_G, (g + 1) * PER_G)
                        nc.scalar.copy(masked[:, t % 2, heads], scores[:, heads]).then_inc(scores_copied, 1)

            @block.gpsimd
            def _(pool):
                nc.gpsimd.memset(v_wide[:], 0.0).then_inc(state_zeroed, 1)
                nc.gpsimd.memset(state[:], 0.0).then_inc(state_zeroed, 1)
                for t in range(NT):
                    for g in range(GROUPS):
                        pool.wait_ge(scores_copied, t * SB + g + 1)
                        m = masked[:, t % 2, g * PER_G:(g + 1) * PER_G]
                        nc.gpsimd.affine_select(out=m, in_=m, pattern=[[0, PER_G], [1, P]], compare_op=ALU.is_ge, fill=0.0, base=0,
                                                channel_multiplier=-1).then_inc(masked_ready, 1)

            @block.vector
            def _(dve):
                def spread(t, groups=slice(0, GROUPS)):
                    if t >= 2:
                        dve.wait_ge(scores_ready, (t - 1) * SB)
                    shape = [P, groups.stop - groups.start, PER_G, P]
                    nc.vector.tensor_tensor(q_x[:, t % 2, groups], q_st[:, groups, blk(t, P)].bitcast(F32).unsqueeze(2).broadcast_to(shape),
                                            own_st[:].unsqueeze(1).unsqueeze(3).broadcast_to(shape), ALU.mult).then_inc(q_x_ready, 1)

                def add(b):
                    dve.wait_ge(y_ready, b + 1)
                    nc.vector.scalar_tensor_tensor(out=x[:, blk(b)], in0=y_ps[:], scalar=w.bo_c[:, 0:1], in1=x[:, blk(b)],
                                                   op0=ALU.add, op1=ALU.add).then_inc(y_added, 1)

                for g in range(GROUPS):
                    spread(0, slice(g, g + 1))
                spread(1)
                dve.wait_ge(state_zeroed, 2)
                for t in range(NT):
                    if t + 1 < NT:
                        dve.wait_ge(sums_ready, t + 1)
                        if t > 0:
                            dve.wait_ge(out_ready, t)
                        nc.vector.tensor_tensor(state[:, (t + 1) % 2].rearrange("p (j g d) -> p g j d", g=GROUPS, j=PER_G),
                                                sums[:].rearrange("p (g j) d -> p g j d", g=GROUPS),
                                                own[:].rearrange("p (g j) -> p g j", g=GROUPS).unsqueeze(3).broadcast_to([P, GROUPS, PER_G, DB]),
                                                ALU.mult).then_inc(state_ready, 1)
                    if t + 2 < NT:
                        spread(t + 2)
                    dve.wait_ge(out_ready, t + 1)
                    b = t // PER_Y
                    if b >= 2:
                        dve.wait_ge(y_ready, b - 1)
                    nc.vector.tensor_copy(out_t[:, b % 2, blk(t % PER_Y, P)], out_ps[:, t % 2, 0:P]).then_inc(out_copied, 1)
                    if t % PER_Y == 0 and t > 0:
                        add(t // PER_Y - 1)
                add(NB - 1)


def program(nc, x_t, w_qkv, w_gates, w_out, wq_t, bq, wk_t, bk, wv_t, bv, wo_t, bo, bq_groups, bk_groups, wg_t, wu_t, wd_t, wr_t, rb, out_t):
    dram = lambda n, s: nc.dram_tensor(n, s, F32).ap()
    v_dram = dram("v_dram", [PAIRS, P, NT, P])
    gate_dram = dram("gate_dram", [PAIRS, 2, T])
    den_dram = dram("den_dram", [PAIRS, 3, T])
    factor_dram = dram("factor_dram", [2, T])
    cw_dram = [dram(f"cw_dram{i}", [ROUTED, T]) for i in range(2)]
    with ExitStack() as ctx:
        sb_in = lambda c, n, s, d=F32: c.enter_context(nc.sbuf_tensor(n, s, d))
        parts_in = lambda c, n: (sb_in(c, f"{n}_hi", [P, T], F32R), sb_in(c, f"{n}_lo", [P, T], F32R))
        x = sb_in(ctx, "x", [P, T])
        sems = Semaphores(nc, ctx)
        x_loaded, out_stored = [sems("io", f"x_loaded{b}") for b in range(NB)], sems("io", "out_stored")
        with ExitStack() as c:
            x_hi, x_lo = parts_in(c, "a")
            aw = AttentionWeights(c, nc, sems, w_qkv)

            def load(sp):
                for b in range(NB):
                    sp.dma_start(x[:, blk(b)], x_t[:, blk(b)]).then_inc(x_loaded[b], 16)
                aw.load_v(sp)
                aw.load_pair(sp, 0)

            def split(dve):
                aw.split_v(dve)
                aw.split_pair(dve, 0)

            pairs = Pairs(c, nc, sems)
            with ExitStack() as cv:
                xn = sb_in(cv, "xn_a", [P, T])
                aw.allocate_v(cv)
                layer_norm(nc, sems, "ln0", x, xn, x_hi, x_lo, "ln_a", x_loaded=x_loaded, beside={"sync": load, "vector": split})
                values_and_gates(nc, sems, xn, x_hi, x_lo, aw, pairs, w_gates, v_dram, gate_dram)
            softcap_attention(nc, sems, x, x_hi, x_lo, aw, pairs, w_out, v_dram, gate_dram, den_dram, factor_dram)
        sb = lambda n, s, d: sb_in(ctx, n, s, d)
        xn = sb("xn", [P, T], F32)
        weights = MixtureWeights(ctx, nc, sems)

        def mixture(i, split):
            with ExitStack() as c:
                x_hi, x_lo = parts_in(c, f"f{i}")
                probs = sb_in(c, f"probs{i}", [P, NT, ROUTED])
                beside = None
                if split:
                    weights.allocate_raw(c)
                    beside = {"sync": lambda sp: weights.load(sp, wg_t, wu_t, wd_t, wr_t, rb), "gpsimd": weights.make_constants}
                layer_norm(nc, sems, "ln1", x, xn, x_hi, x_lo, f"ln_f{i}", beside=beside, router=(weights, probs))
                experts(nc, sems, x, x_hi, x_lo, weights, probs, cw_dram[i], f"ex{i}", split)

        mixture(0, True)
        with ExitStack() as c:
            lw = LinearWeights(c, nc, sems)
            layer_norm(nc, sems, "ln0", x, xn, None, None, "ln_b",
                       beside={"sync": lambda sp: lw.load(sp, wq_t, wk_t, wv_t, bq, bq_groups, bk, bk_groups, bv, bo)})
            linear_attention(nc, sems, x, xn, lw, wo_t)
        mixture(1, False)
        with nc.Block() as block:
            @block.sync
            def _(sp):
                sp.dma_start(out_t, x[:]).then_inc(out_stored, 16)
                sp.wait_ge(out_stored, 16)


def kernel(**inputs):
    import numpy as np
    import concourse.bacc as bacc
    from concourse.bass_utils import run_bass_kernel_spmd

    a = {n.removeprefix("L0_"): np.asarray(v) for n, v in inputs.items()}
    turn = lambda v: np.ascontiguousarray(np.swapaxes(v, -1, -2))
    both = lambda n: turn(np.concatenate([a[f"ffn_{n}_s"][None], a[f"ffn_{n}"]]))
    arrays = {"x_t": turn(a["attn_a_x"][0]), "w_qkv": a["attn_a_w_qkv"], "w_gates": a["attn_a_w_gates"], "w_out": a["attn_a_w_out"]}
    for n in "qkvo":
        arrays[f"w{n}_t"] = turn(a[f"attn_b_w{n}_w"])
        arrays[f"b{n}"] = a[f"attn_b_w{n}_b"]
    for n in "qk":
        arrays[f"b{n}_groups"] = turn(a[f"attn_b_w{n}_b"].reshape(GROUPS, PAD))
    arrays |= {"wg_t": both("Wg"), "wu_t": both("Wu"), "wd_t": both("Wd"), "wr_t": turn(a["ffn_Wr"]), "rb": a["ffn_rb"]}
    arrays = {f"in_{n}": np.ascontiguousarray(v) for n, v in arrays.items()}

    nc = bacc.Bacc("TRN2", target_bir_lowering=False, num_devices=1)
    args = [nc.dram_tensor(n, v.shape, mybir.dt.from_np(v.dtype), kind="ExternalInput").ap() for n, v in arrays.items()]
    out = nc.dram_tensor("out_0", (P, T), F32, kind="ExternalOutput").ap()
    program(nc, *args, out)
    r = run_bass_kernel_spmd(nc, [arrays], core_ids=[0])
    return np.ascontiguousarray(r.results[0]["out_0"].T)[None]
```

```python
from contextlib import ExitStack

import concourse.bass as bass
from concourse import mybir

F32 = mybir.dt.float32
F32R = mybir.dt.float32r
ACT = mybir.ActivationFunctionType
ALU = mybir.AluOpType
AX = mybir.AxisListType

P = 128
T = 2048
BLK = 512
NB = T // BLK
NT = T // P
EPS = 1e-5

H = 16
DH = 64
PAIRS = H // 2
SOFTCAP = 50.0
KT_PER_BLK = BLK // P


def spread_evenly(full, diagonal):
    n, out = len(full) + len(diagonal), []
    ends = [-(-(i + 1) * n // len(diagonal)) - 1 for i in range(len(diagonal))]
    full, diagonal = iter(full), iter(diagonal)
    for i in range(n):
        out.append(next(diagonal) if i in ends else next(full))
    return out


def steps_of_a_pair():
    full = lambda qb: [(qb, j) for j in range(KT_PER_BLK * qb)]
    diagonal = lambda qb: [(qb, KT_PER_BLK * qb + i) for i in range(KT_PER_BLK)]
    steps = []
    for qb in range(1, NB - 1):
        steps += spread_evenly(full(qb), diagonal(qb))
    a, b = diagonal(NB - 1), diagonal(0)
    return steps + spread_evenly(full(NB - 1), [a[0], b[0], a[1], a[2], b[1], a[3]]) + b[2:]


STEPS = steps_of_a_pair()
NS = len(STEPS)
PLACE = {qb: (qb - 1) % NB for qb in range(NB)}
DIAG = [j >= KT_PER_BLK * qb for qb, j in STEPS]
ND = sum(DIAG)
LAST = [max(n for n in range(NS) if STEPS[n][0] == qb) for qb in range(NB)]
assert sorted(range(NB), key=lambda qb: LAST[qb]) == sorted(range(NB), key=lambda qb: PLACE[qb])
UNITS = 2 * NB
RING = 4


def blk(b, n=BLK):
    return slice(b * n, (b + 1) * n)


def rows_of(h):
    return slice(h * DH, (h + 1) * DH)


class Semaphores:

    def __init__(self, nc, ctx):
        self.nc, self.ctx, self.of = nc, ctx, {}

    def __call__(self, part, name):
        if (part, name) not in self.of:
            self.of[part, name] = self.ctx.enter_context(self.nc.semaphore(f"{part}_{name}"))
        return self.of[part, name]

    def clear(self, pool, *parts):
        for (part, _), semaphore in self.of.items():
            if part in parts:
                pool.sem_clear(semaphore)


def wait(eng, semaphore, value):
    if not isinstance(value, int) or value > 0:
        eng.wait_ge(semaphore, value)


def layer_norm(nc, sems, part, x, xn, x_hi, x_lo, name, x_loaded=None, beside=None, router=None):
    Q = P // NB
    R, HALF = 2, BLK // 2
    S = 2
    with ExitStack() as ctx:
        sb = lambda n, s, d=F32: ctx.enter_context(nc.sbuf_tensor(f"{name}_{n}", s, d))
        sem = lambda n: sems(part, n)
        beside = beside or {}
        mean_of = sb("mean_of", [P, P])
        mean_at = sb("mean_at", [P, R, Q])
        pick = sb("pick", [P, NB, R, P])
        pick_r = sb("pick_r", [P, NB, R, P], F32R)
        eps = sb("eps", [P, 1])
        centred = sb("centred", [P, T])
        squared = sb("squared", [P, T])
        std = sb("std", [P, HALF])
        rstd = sb("rstd", [P, HALF])
        rstd_hi, rstd_lo = sb("rstd_hi", [P, HALF], F32R), sb("rstd_lo", [P, HALF], F32R)
        mean = ctx.enter_context(nc.psum_tensor(f"{name}_mean", [P, NB, BLK], F32))
        var = ctx.enter_context(nc.psum_tensor(f"{name}_var", [P, HALF], F32))
        spread = ctx.enter_context(nc.psum_tensor(f"{name}_spread", [P, S, BLK], F32))
        mean_at_ready, table_loaded, pick_r_ready = sem("mean_at_ready"), sem("table_loaded"), sem("pick_r_ready")
        const_ready, zero_ready, pick_ready, mean_ready, centred_ready = sem("const_ready"), sem("zero_ready"), sem("pick_ready"), sem("mean_ready"), sem("centred_ready")
        squared_ready, var_ready, std_ready = sem("squared_ready"), sem("var_ready"), sem("std_ready")
        rstd_ready, rstd_hi_ready, rstd_split, spread_ready = sem("rstd_ready"), sem("rstd_hi_ready"), sem("rstd_split"), sem("spread_ready")
        xn_ready, hi_ready = sem("xn_ready"), sem("hi_ready")
        if router:
            weights, probs = router
            logits = sb("logits", [P, NT, ROUTED])
            logits_ps = ctx.enter_context(nc.psum_tensor(f"{name}_logits_ps", [P, NT, ROUTED], F32))
            logits_computed, logits_ready = sem("logits_computed"), sem("logits_ready")
        block = ctx.enter_context(nc.Block())

        @block.sync
        def _(sp):
            if "sync" in beside:
                beside["sync"](sp)

        @block.gpsimd
        def _(pool):
            nc.gpsimd.memset(mean_of[:], 1.0 / P).then_inc(const_ready, 1)
            nc.gpsimd.memset(eps[:], EPS).then_inc(const_ready, 1)
            nc.gpsimd.memset(mean_at[:], 0.0).then_inc(zero_ready, 1)
            nc.gpsimd.memset(pick[:], 1.0).then_inc(zero_ready, 1)
            pool.wait_ge(zero_ready, 2)
            for r in range(R):
                nc.gpsimd.memset(mean_at[:, r, r:r + 1], 1.0 / P).then_inc(mean_at_ready, 1)
            nc.gpsimd.affine_select(out=pick[:], in_=pick[:], pattern=[[-Q, NB], [-1, R], [0, P]], compare_op=ALU.is_equal, fill=0.0,
                                    base=0, channel_multiplier=1).then_inc(pick_ready, 1)
            if "gpsimd" in beside:
                pool.wait_ge(mean_at_ready, R)
                pool.wait_ge(pick_ready, 1)
                beside["gpsimd"](pool)

        @block.tensor
        def _(pe):
            pe.wait_ge(const_ready, 2)
            for b in range(NB):
                if x_loaded:
                    pe.wait_ge(x_loaded[b], 16)
                nc.tensor.matmul(mean[:, b], mean_of[:], x[:, blk(b)], start=True, stop=True).then_inc(mean_ready, 1)
            pe.wait_ge(squared_ready, NB)
            pe.wait_ge(mean_at_ready, R)
            for r in range(R):
                for b in range(NB):
                    nc.tensor.matmul(var[b * Q:(b + 1) * Q], mean_at[:, r], squared[:, blk(R * b + r, HALF)],
                                     start=(r == 0), stop=(r == R - 1), skip_group_check=True).then_inc(var_ready, 1)
            pe.wait_ge(pick_r_ready, 1)
            pe.wait_ge(rstd_split, 1)
            for b in range(NB):
                if b >= S:
                    pe.wait_ge(xn_ready, b - S + 1)
                for r in range(R):
                    out = spread[:, b % S, blk(r, HALF)]
                    nc.tensor.matmul(out, pick_r[:, b, r], rstd_hi[:], start=True, stop=False)
                    mm = nc.tensor.matmul(out, pick_r[:, b, r], rstd_lo[:], start=False, stop=True)
                mm.then_inc(spread_ready, 1)
            if router:
                pe.wait_ge(weights.router_loaded, 32)
                for t in range(NT):
                    pe.wait_ge(xn_ready, t * P // BLK + 1)
                    mm = nc.tensor.matmul(logits_ps[:, t], xn[:, blk(t, P)], weights.router[:], start=True, stop=True)
                mm.then_inc(logits_computed, 1)

        @block.scalar
        def _(act):
            act.wait_ge(const_ready, 2)
            nc.scalar.activation(std[:, 0:1], eps[:], ACT.Sqrt).then_inc(table_loaded, 1)
            for b in range(NB):
                act.wait_ge(centred_ready, b + 1)
                nc.scalar.activation(squared[:, blk(b)], centred[:, blk(b)], ACT.Square).then_inc(squared_ready, 1)
            act.wait_ge(pick_ready, 1)
            nc.scalar.copy(pick_r[:], pick[:]).then_inc(pick_r_ready, 1)
            act.wait_ge(table_loaded, 1)
            act.wait_ge(var_ready, NB * R)
            nc.scalar.activation(std[:], var[:], ACT.Sqrt, bias=eps[:, 0:1]).then_inc(std_ready, 1)
            if "scalar" in beside:
                beside["scalar"](act)
            if x_hi is not None:
                for b in range(NB):
                    act.wait_ge(xn_ready, b + 1)
                    nc.scalar.copy(x_hi[:, blk(b)], xn[:, blk(b)]).then_inc(hi_ready, 1)
            if router:
                act.wait_ge(logits_ready, 1)
                nc.scalar.activation(probs[:], logits[:], ACT.Sigmoid)

        @block.vector
        def _(dve):
            def rest(b):
                dve.wait_ge(hi_ready, b + 1)
                nc.vector.tensor_tensor(x_lo[:, blk(b)], xn[:, blk(b)], x_hi[:, blk(b)].bitcast(F32), ALU.subtract)

            for b in range(NB):
                dve.wait_ge(mean_ready, b + 1)
                nc.vector.tensor_tensor(centred[:, blk(b)], x[:, blk(b)], mean[:, b], ALU.subtract).then_inc(centred_ready, 1)
            if "vector" in beside:
                beside["vector"](dve)
            dve.wait_ge(std_ready, 1)
            nc.vector.reciprocal(rstd[:], std[:]).then_inc(rstd_ready, 1)
            dve.wait_ge(rstd_ready, 1)
            nc.vector.tensor_copy(rstd_hi[:], rstd[:]).then_inc(rstd_hi_ready, 1)
            dve.wait_ge(rstd_hi_ready, 1)
            nc.vector.tensor_tensor(rstd_lo[:], rstd[:], rstd_hi[:].bitcast(F32), ALU.subtract).then_inc(rstd_split, 1)
            for b in range(NB):
                dve.wait_ge(spread_ready, b + 1)
                nc.vector.tensor_tensor(xn[:, blk(b)], centred[:, blk(b)], spread[:, b % S], ALU.mult).then_inc(xn_ready, 1)
                if b > 0 and x_hi is not None:
                    rest(b - 1)
            if x_hi is not None:
                rest(NB - 1)
            if "vector_end" in beside:
                beside["vector_end"](dve)
            if router:
                dve.wait_ge(logits_computed, 1)
                nc.vector.tensor_tensor(logits[:], logits_ps[:], weights.bias[:].unsqueeze(1).broadcast_to([P, NT, ROUTED]), ALU.add).then_inc(logits_ready, 1)


class AttentionWeights:

    def __init__(self, ctx, nc, sems, w_qkv):
        sb = lambda n, s, d=F32: ctx.enter_context(nc.sbuf_tensor(f"aw_{n}", s, d))
        self.nc, self.w_qkv = nc, w_qkv
        self.raw, self.hi, self.lo = sb("raw", [P, 2 * P]), sb("hi", [P, 2 * P], F32R), sb("lo", [P, 2 * P], F32R)
        self.loaded, self.hi_ready, self.split = sems("aw", "loaded"), sems("aw", "hi_ready"), sems("aw", "split")
        self.v_loaded, self.v_hi_ready = sems("aw", "v_loaded"), sems("aw", "v_hi_ready")

    def allocate_v(self, ctx):
        sb = lambda n, d=F32: ctx.enter_context(self.nc.sbuf_tensor(f"aw_{n}", [P, H * DH], d))
        self.v, self.v_hi, self.v_lo = sb("v"), sb("v_hi", F32R), sb("v_lo", F32R)

    def load_v(self, sp):
        sp.dma_start(self.v[:], self.w_qkv[:, 2 * H * DH:3 * H * DH]).then_inc(self.v_loaded, 16)

    def load_pair(self, sp, p):
        for which in range(2):
            sp.dma_start(self.raw[:, blk(which, P)], self.w_qkv[:, bass.ds(p * P + which * H * DH, P)]).then_inc(self.loaded, 16)

    def split_v(self, dve):
        dve.wait_ge(self.v_loaded, 16)
        self.nc.vector.tensor_copy(self.v_hi[:], self.v[:]).then_inc(self.v_hi_ready, 1)
        dve.wait_ge(self.v_hi_ready, 1)
        self.nc.vector.tensor_tensor(self.v_lo[:], self.v[:], self.v_hi[:].bitcast(F32), ALU.subtract)

    def split_pair(self, dve, p):
        dve.wait_ge(self.loaded, p * 32 + 32)
        self.nc.vector.tensor_copy(self.hi[:], self.raw[:]).then_inc(self.hi_ready, 1)
        dve.wait_ge(self.hi_ready, p + 1)
        self.nc.vector.tensor_tensor(self.lo[:], self.raw[:], self.hi[:].bitcast(F32), ALU.subtract).then_inc(self.split, 1)


class Pairs:

    def __init__(self, ctx, nc, sems):
        sb = lambda n, s, d=F32: ctx.enter_context(nc.sbuf_tensor(f"pr_{n}", s, d))
        sem = lambda n: sems("pr", n)
        self.nc = nc
        self.q_hi = [[sb(f"q_hi{a}{h}", [P, T], F32R) for h in range(2)] for a in range(2)]
        self.q_lo = [[sb(f"q_lo{a}{h}", [P, T], F32R) for h in range(2)] for a in range(2)]
        self.k_hl = [[sb(f"k_hl{a}{h}", [P, T], F32R) for h in range(2)] for a in range(2)]
        self.v = sb("v", [P, 2, NT, P])
        self.computed, self.hi_ready, self.ready, self.q_doubled = sem("computed"), sem("hi_ready"), sem("ready"), sem("q_doubled")

    def project(self, u, weights, x_hi, x_lo, out):
        cols, xs = blk(u // NB, P), blk(u % NB)
        self.nc.tensor.matmul(out, weights.hi[:, cols], x_hi[:, xs], start=True, stop=False)
        self.nc.tensor.matmul(out, weights.hi[:, cols], x_lo[:, xs], start=False, stop=False)
        self.nc.tensor.matmul(out, weights.lo[:, cols], x_hi[:, xs], start=False, stop=True).then_inc(self.computed, 1)

    def leading(self, a, u):
        return [(self.q_hi, self.k_hl)[u // NB][a][h][rows_of(h), blk(u % NB)] for h in range(2)]

    def subtract_leading(self, a, u, out):
        for h, hi in enumerate(self.leading(a, u)):
            lo = self.q_lo[a][h][rows_of(h), blk(u % NB)] if u < NB else self.k_hl[a][h][rows_of(1 - h), blk(u % NB)]
            rest = self.nc.vector.tensor_tensor(lo, out[rows_of(h)], hi.bitcast(F32), ALU.subtract)
        rest.then_inc(self.ready, 1)

    def double_queries(self, sp, a):
        for q in (self.q_hi[a], self.q_lo[a]):
            for h in range(2):
                sp.dma_start(q[h][rows_of(1 - h), :].bitcast(F32), q[h][rows_of(h), :].bitcast(F32)).then_inc(self.q_doubled, 16)


def values_and_gates(nc, sems, xn, x_hi, x_lo, w, pairs, w_gates, v_dram, gate_dram):
    VD = H * DH
    HALF = VD // 2
    RV = 8
    NPS = 4
    KEPT = 2 * P
    UNITS_AFTER = {2 * u + 1: [u] for u in range(NB)} | {NT - 1: range(NB, UNITS)}
    GATES_AFTER = {2 * NB + i: i for i in range(NB)}
    with ExitStack() as ctx:
        sb = lambda n, s, d=F32: ctx.enter_context(nc.sbuf_tensor(f"vg_{n}", s, d))
        sem = lambda n: sems("vg", n)
        wg = sb("wg", [P, H])
        v_tile = sb("v_tile", [P, RV, VD - KEPT])
        gate = sb("gate", [H, T])
        v_ps = ctx.enter_context(nc.psum_tensor("vg_v_ps", [P, NPS, BLK], F32))
        g_ps = ctx.enter_context(nc.psum_tensor("vg_g_ps", [H, 2, BLK], F32))
        p_ps = ctx.enter_context(nc.psum_tensor("vg_p_ps", [P, 2, BLK], F32))
        wg_loaded = sem("wg_loaded")
        v_computed, v_copied_act, v_copied_dve = sem("v_computed"), sem("v_copied_act"), sem("v_copied_dve")
        g_computed, g_ready, stored = sem("g_computed"), sem("g_ready"), sem("stored")
        v_stored = [sem(f"v_stored{i}") for i in range(RV)]
        block = ctx.enter_context(nc.Block())

        @block.sync
        def _(sp):
            sp.dma_start(wg[:], w_gates).then_inc(wg_loaded, 16)
            for t in range(NT):
                sp.wait_ge(v_copied_act, t + 1)
                sp.wait_ge(v_copied_dve, t + 1)
                sp.dma_start(v_dram[2:, :, t, :].rearrange("a p d -> p a d"),
                             v_tile[:, t % RV].rearrange("p (a d) -> p a d", a=PAIRS - 2)).then_inc(v_stored[t % RV], 16)
                if t == 2 * NB:
                    sp.wait_ge(pairs.ready, NB)
                    pairs.double_queries(sp, 0)
                if t == 3 * NB:
                    sp.wait_ge(g_ready, NB)
                    sp.dma_start(gate_dram.rearrange("a h t -> (a h) t"), gate[:]).then_inc(stored, 16)
            for stored_of in v_stored:
                sp.wait_ge(stored_of, 16 * NT // RV)
            sp.wait_ge(stored, 16)

        @block.tensor
        def _(pe):
            for t in range(NT):
                for half in range(2):
                    n = 2 * t + half
                    if n >= NPS:
                        pe.wait_ge(v_copied_act if half == 0 else v_copied_dve, (n - NPS) // 2 + 1)
                    out, cols = v_ps[:, n % NPS], blk(half, HALF)
                    nc.tensor.matmul(out, x_hi[:, blk(t, P)], w.v_hi[:, cols], start=True, stop=False)
                    nc.tensor.matmul(out, x_hi[:, blk(t, P)], w.v_lo[:, cols], start=False, stop=False)
                    nc.tensor.matmul(out, x_lo[:, blk(t, P)], w.v_hi[:, cols], start=False, stop=True).then_inc(v_computed, 1)
                for u in UNITS_AFTER.get(t, ()):
                    wait(pe, pairs.ready, u - 1)
                    pairs.project(u, w, x_hi, x_lo, p_ps[:, u % 2])
                if t in GATES_AFTER:
                    b = GATES_AFTER[t]
                    pe.wait_ge(wg_loaded, 16)
                    if b >= 2:
                        pe.wait_ge(g_ready, b - 1)
                    nc.tensor.matmul(g_ps[:, b % 2], wg[:], xn[:, blk(b)], start=True, stop=True).then_inc(g_computed, 1)

        @block.scalar
        def _(act):
            for t in range(NT):
                act.wait_ge(v_computed, 2 * t + 1)
                if t >= RV:
                    act.wait_ge(v_stored[t % RV], 16 * (t // RV))
                first = v_ps[:, (2 * t) % NPS]
                nc.scalar.copy(pairs.v[:, :, t], first[:, 0:KEPT].rearrange("p (a d) -> p a d", a=2))
                nc.scalar.copy(v_tile[:, t % RV, 0:HALF - KEPT], first[:, KEPT:HALF]).then_inc(v_copied_act, 1)
                for u in UNITS_AFTER.get(t, ()):
                    act.wait_ge(pairs.computed, u + 1)
                    for h, hi in enumerate(pairs.leading(0, u)):
                        leading = nc.scalar.copy(hi, p_ps[rows_of(h), u % 2])
                    leading.then_inc(pairs.hi_ready, 1)
                if t in GATES_AFTER:
                    b = GATES_AFTER[t]
                    act.wait_ge(g_computed, b + 1)
                    nc.scalar.activation(gate[:, blk(b)], g_ps[:, b % 2], ACT.Sigmoid).then_inc(g_ready, 1)

        @block.vector
        def _(dve):
            for t in range(NT):
                dve.wait_ge(v_computed, 2 * t + 2)
                if t >= RV:
                    dve.wait_ge(v_stored[t % RV], 16 * (t // RV))
                nc.vector.tensor_copy(v_tile[:, t % RV, HALF - KEPT:], v_ps[:, (2 * t + 1) % NPS]).then_inc(v_copied_dve, 1)
                for u in UNITS_AFTER.get(t, ()):
                    dve.wait_ge(pairs.hi_ready, u + 1)
                    pairs.subtract_leading(0, u, p_ps[:, u % 2])


def softcap_attention(nc, sems, x, x_hi, x_lo, weights, pairs, w_out, v_dram, gate_dram, den_dram, factor_dram):
    PROJ_AT = {4 + 4 * u: u for u in range(UNITS)}
    OUT_LAG, DEN_LAG, DEN_COPY_LAG = 2, 2, 2
    SPLIT_AT, FACTOR_AT = 2, 11
    NORM_AT = {20 + 4 * b: b for b in range(NB)}
    Y_AT = {22 + 4 * b: b for b in range(NB)}
    with ExitStack() as ctx:
        sb = lambda n, s, d=F32: ctx.enter_context(nc.sbuf_tensor(f"at_{n}", s, d))
        psum = lambda n, s: ctx.enter_context(nc.psum_tensor(f"at_{n}", s, F32))
        sem = lambda n: sems("at", n)
        w_y = [sb(f"w_y{a}", [P, P]) for a in range(2)]
        q_hi, q_lo, k_hl = pairs.q_hi, pairs.q_lo, pairs.k_hl
        v = [pairs.v[:, a] for a in range(2)]
        capped = sb("capped", [P, 2, 2, BLK])
        probs = sb("probs", [P, RING, 2, BLK])
        psums = [sb(f"psums{a}", [P, 2, BLK]) for a in range(2)]
        ones = sb("ones", [P, DH])
        causal = sb("causal", [P, 2, P])
        den_row = sb("den_row", [P, 2, BLK])
        out_t = [sb(f"out_t{a}", [P, T]) for a in range(2)]
        factor_b = sb("factor_b", [P, T])
        den_r = sb("den_r", [P, 2 * T // P])
        gate_r = sb("gate_r", [P, 2 * T // P])
        rden = sb("rden", [P, 2 * T // P])
        factor = sb("factor", [P, 2 * T // P])
        scores = psum("scores", [P, 2, 2, BLK])
        o_ps = psum("o_ps", [P, 2, BLK])
        proj_ps = psum("proj_ps", [P, BLK])
        den_ps = psum("den_ps", [P, BLK])

        init_ready = sem("init_ready")
        proj_computed, proj_hi_ready, proj_ready, q_doubled = pairs.computed, pairs.hi_ready, pairs.ready, pairs.q_doubled
        v_loaded = sem("v_loaded")
        scores_ready, tanh_done, exp_done, masked = sem("scores_ready"), sem("tanh_done"), sem("exp_done"), sem("masked")
        pv_done, summed, out_copied = sem("pv_done"), sem("summed"), sem("out_copied")
        den_computed, den_copied = sem("den_computed"), sem("den_copied")
        den_stored = [sem(f"den_stored{i}") for i in range(2)]
        den_loaded, rden_ready, factor_ready = sem("den_loaded"), sem("rden_ready"), sem("factor_ready")
        factor_stored, factor_loaded, normed, y_computed = sem("factor_stored"), sem("factor_loaded"), sem("normed"), sem("y_computed")
        w_y_loaded, y_added = sem("w_y_loaded"), sem("y_added")
        gate_loaded, gated, divided = sem("gate_loaded"), sem("gated"), sem("divided")
        gate_b = v[0].rearrange("p t d -> p (t d)")
        block = ctx.enter_context(nc.Block())

        def run_pairs(eng, pair):
            pair(0, 0, False)
            pair(1, 1, False)
            with eng.Fori(1, PAIRS // 2 - 1) as i:
                pair(i * 2, 0, False)
                pair(i * 2 + 1, 1, False)
            pair(PAIRS - 2, 0, False)
            pair(PAIRS - 1, 1, True)

        def is_first(p):
            return isinstance(p, int) and p == 0

        def blocks_in_place():
            return sorted(range(NB), key=lambda qb: PLACE[qb])

        def due(p, a, n, lag):
            for qb in blocks_in_place():
                if LAST[qb] + lag == n and not (isinstance(p, int) and p == PAIRS):
                    yield p, a, qb
                if LAST[qb] + lag - NS == n and not is_first(p):
                    yield p - 1, 1 - a, qb

        def queries(n):
            qb, j = STEPS[n]
            first = max(qb * BLK, j * P)
            return first, (qb + 1) * BLK - first, first - qb * BLK

        @block.sync
        def _(sp):
            def load_values(p, a):
                sp.dma_start(v[a], v_dram[bass.ds(p, 1)].rearrange("a p t d -> (a p) t d")).then_inc(v_loaded, 16)

            def factors(p, a, before):
                for stored in den_stored:
                    sp.wait_ge(stored, p * (16 * NB // 2))
                shape = dict(c=2 * T // P)
                sp.dma_start(den_r[:], den_dram[bass.ds(before, 1), 1:3].rearrange("a h (p c) -> (a h p) c", **shape)).then_inc(den_loaded, 16)
                sp.dma_start(gate_r[:], gate_dram[bass.ds(before, 1)].rearrange("a h (p c) -> (a h p) c", **shape)).then_inc(den_loaded, 16)
                wait(sp, y_computed, (p - 1) * NB)
                sp.dma_start(w_y[1 - a][:], w_out[bass.ds(before * P, P)]).then_inc(w_y_loaded, 16)
                sp.wait_ge(factor_ready, p)
                sp.dma_start(factor_dram.rearrange("h (p c) -> (h p) c", **shape), factor[:]).then_inc(factor_stored, 16)
                sp.wait_ge(factor_stored, p * 16)
                for h in range(2):
                    sp.dma_start(factor_b[h * DH:(h + 1) * DH, :], factor_dram[h:h + 1].broadcast_to([DH, T])).then_inc(factor_loaded, 16)

            def store_denominators(p, qb):
                sp.wait_ge(den_copied, p * NB + PLACE[qb] + 1)
                buffer = PLACE[qb] % 2
                sp.dma_start(den_dram[bass.ds(p, 1), 1:3, blk(qb)].rearrange("a h t -> (a h) t"),
                             den_row[0:DH + 1:DH, buffer]).then_inc(den_stored[buffer], 16)

            def pair(p, a, last):
                before = p - 1
                if not last:
                    sp.wait_ge(weights.split, p + 1)
                    weights.load_pair(sp, p + 1)
                    if not is_first(p):
                        sp.wait_ge(pv_done, p * NS)
                        wait(sp, v_loaded, (p - 1) * 16)
                        load_values(p + 1, 1 - a)
                if not is_first(p):
                    store_denominators(before, 0)
                    if last:
                        sp.wait_ge(pv_done, p * NS)
                        for h in range(2):
                            sp.dma_start(gate_b[rows_of(h), :], gate_dram[p, h:h + 1].broadcast_to([DH, T])).then_inc(gate_loaded, 16)
                    factors(p, a, before)
                if last:
                    sp.wait_ge(w_y_loaded, p * 16)
                    sp.dma_start(w_y[a][:], w_out[p * P:(p + 1) * P]).then_inc(w_y_loaded, 16)
                    return
                sp.wait_ge(proj_ready, p * UNITS + UNITS + NB)
                pairs.double_queries(sp, 1 - a)
                for qb in range(1, NB):
                    store_denominators(p, qb)

            run_pairs(sp, pair)
            sp.wait_ge(factor_stored, 16 * (PAIRS - 1))
            for stored in den_stored:
                sp.wait_ge(stored, 16 * NB // 2 * (PAIRS - 1))

        @block.tensor
        def _(pe):
            def scores_of(g, a, n):
                first, width, _ = queries(n)
                wait(pe, tanh_done, g - 1)
                for h in range(2):
                    keys = k_hl[a][h][:, blk(STEPS[n][1], P)]
                    out = scores[:, n % 2, h, 0:width]
                    nc.tensor.matmul(out, keys, q_hi[a][h][:, first:first + width], start=True, stop=False)
                    last = nc.tensor.matmul(out, keys, q_lo[a][h][:, first:first + width], start=False, stop=True)
                last.then_inc(scores_ready, 1)

            def outputs_of(p, g, a, n):
                qb, j = STEPS[n]
                _, width, at = queries(n)
                if DIAG[n]:
                    pe.wait_ge(masked, p * ND + sum(DIAG[:n]) + 1)
                else:
                    pe.wait_ge(exp_done, g + 1)
                bank = PLACE[qb] % 2
                if j == 0:
                    wait(pe, out_copied, p * NB + PLACE[qb] - 1)
                for h in range(2):
                    last = nc.tensor.matmul(o_ps[h * DH:(h + 1) * DH, bank, at:BLK], v[a][:, j, h * DH:(h + 1) * DH],
                                            probs[:, n % RING, h, 0:width], start=(j == 0), stop=(n == LAST[qb]),
                                            skip_group_check=True)
                last.then_inc(pv_done, 1)

            def denominators(p, a, qb):
                pe.wait_ge(summed, p * NS + LAST[qb] + 1)
                wait(pe, den_copied, p * NB + PLACE[qb])
                for h in range(2):
                    last = nc.tensor.matmul(den_ps[rows_of(h)], ones[:], psums[PLACE[qb] % 2][:, h], start=True, stop=True)
                last.then_inc(den_computed, 1)

            def output_projection(p, a, b, last):
                if not last:
                    pe.wait_ge(proj_ready, (p + 1) * UNITS + sum(at <= n_of_y[b] for at in PROJ_AT))
                wait(pe, y_added, (p - 1) * NB + b)
                if b == 0:
                    pe.wait_ge(w_y_loaded, p * 16)
                pe.wait_ge(normed, (p - 1) * NB + b + 1)
                nc.tensor.matmul(proj_ps[:], w_y[1 - a][:], factor_b[:, blk(b)], start=True, stop=True).then_inc(y_computed, 1)

            n_of_y = {b: n for n, b in Y_AT.items()}

            def pair(p, a, last):
                for n in range(NS):
                    g = p * NS + n
                    if n + 2 < NS:
                        scores_of(g + 2, a, n + 2)
                    elif not last:
                        if n + 2 == NS:
                            pe.wait_ge(proj_ready, (p + 2) * UNITS)
                            pe.wait_ge(q_doubled, (p + 2) * 64)
                            wait(pe, v_loaded, p * 16)
                        scores_of(g + 2, 1 - a, n + 2 - NS)
                    if n in PROJ_AT and not last:
                        if n == min(PROJ_AT):
                            pe.wait_ge(weights.split, p + 2)
                        wait(pe, proj_ready, (p + 1) * UNITS + PROJ_AT[n])
                        wait(pe, y_added, (p - 1) * NB + sum(at < n for at in Y_AT))
                        pairs.project(PROJ_AT[n], weights, x_hi, x_lo, proj_ps[:])
                    if n in Y_AT and not is_first(p):
                        output_projection(p, a, Y_AT[n], last)
                    for block_done in due(p, a, n, DEN_LAG):
                        denominators(*block_done)
                    if n > 0:
                        outputs_of(p, g - 1, a, n - 1)
                    elif not is_first(p):
                        outputs_of(p - 1, g - 1, 1 - a, NS - 1)

            pe.wait_ge(q_doubled, 64)
            scores_of(0, 0, 0)
            scores_of(1, 0, 1)
            pe.wait_ge(init_ready, 2)
            run_pairs(pe, pair)
            outputs_of(PAIRS - 1, PAIRS * NS - 1, 1, NS - 1)
            for n in range(NS):
                for block_done in due(PAIRS, 0, n, DEN_LAG):
                    denominators(*block_done)
            pe.wait_ge(w_y_loaded, PAIRS * 16)
            for place, qb in enumerate(blocks_in_place()):
                pe.wait_ge(divided, place + 1)
                nc.tensor.matmul(scores[:, place // 2, place % 2], w_y[1][:], out_t[1][:, blk(qb)], start=True, stop=True).then_inc(y_computed, 1)

        @block.scalar
        def _(act):
            def tanh(g, n):
                width = queries(n)[1]
                act.wait_ge(scores_ready, g + 1)
                wait(act, exp_done, g - 1)
                nc.scalar.activation(capped[:, n % 2, :, 0:width], scores[:, n % 2, :, 0:width], ACT.Tanh,
                                     scale=DH ** -0.5 / SOFTCAP).then_inc(tanh_done, 1)

            def exp(g, n):
                width = queries(n)[1]
                act.wait_ge(tanh_done, g + 1)
                wait(act, pv_done, g + 1 - RING)
                wait(act, summed, g + 1 - RING)
                nc.scalar.activation(probs[:, n % RING, :, 0:width], capped[:, n % 2, :, 0:width], ACT.Exp,
                                     scale=SOFTCAP).then_inc(exp_done, 1)

            def pair(p, a, last):
                for n in range(NS):
                    g = p * NS + n
                    if not (last and n == NS - 1):
                        tanh(g + 1, (n + 1) % NS)
                    exp(g, n)

            act.wait_ge(scores_ready, 1)
            width = queries(0)[1]
            nc.scalar.activation(capped[:, 0, :, 0:width], scores[:, 0, :, 0:width], ACT.Tanh,
                                 scale=DH ** -0.5 / SOFTCAP).then_inc(tanh_done, 1)
            run_pairs(act, pair)

        @block.gpsimd
        def _(pool):
            def mask(p, g, n):
                pool.wait_ge(exp_done, g + 1)
                tile = probs[:, n % RING, :, 0:P]
                nc.gpsimd.tensor_tensor(tile, tile, causal[:], ALU.mult).then_inc(masked, 1)

            def normalise(p, a, b):
                if b == 0:
                    pool.wait_ge(factor_loaded, p * 32)
                    pool.wait_ge(out_copied, p * NB)
                part = factor_b[:, blk(b)]
                nc.gpsimd.tensor_tensor(part, out_t[1 - a][:, blk(b)], part, ALU.mult).then_inc(normed, 1)

            def pair(p, a, last):
                for n in range(NS):
                    if DIAG[n]:
                        mask(p, p * NS + n, n)
                    if n in NORM_AT and not is_first(p):
                        normalise(p, a, NORM_AT[n])

            nc.gpsimd.memset(ones[:], 1.0).then_inc(init_ready, 1)
            nc.gpsimd.memset(causal[:], 1.0).then_inc(init_ready, 1)
            pool.wait_ge(init_ready, 2)
            nc.gpsimd.affine_select(out=causal[:], in_=causal[:], pattern=[[0, 2], [1, P]], compare_op=ALU.is_ge, fill=0.0,
                                    base=0, channel_multiplier=-1).then_inc(init_ready, 1)
            pool.wait_ge(init_ready, 3)
            sems.clear(pool, "ln0")
            run_pairs(pool, pair)

        @block.vector
        def _(dve):
            def sum_probs(p, g, n):
                qb, j = STEPS[n]
                _, width, at = queries(n)
                if DIAG[n]:
                    dve.wait_ge(masked, p * ND + sum(DIAG[:n]) + 1)
                else:
                    dve.wait_ge(exp_done, g + 1)
                new, total = probs[:, n % RING, :, 0:width], psums[PLACE[qb] % 2][:, :, at:BLK]
                if j == 0:
                    wait(dve, den_computed, p * NB + PLACE[qb] - 1)
                    nc.vector.tensor_copy(total, new).then_inc(summed, 1)
                else:
                    dve.wait_ge(summed, g)
                    nc.vector.tensor_tensor(total, total, new, ALU.add).then_inc(summed, 1)

            def split_weights(p):
                wait(dve, proj_computed, p * UNITS)
                weights.split_pair(dve, p)

            def split_projection(count, a, u):
                dve.wait_ge(proj_computed, count + 1)
                for h, hi in enumerate(pairs.leading(a, u)):
                    leading = nc.vector.tensor_copy(hi, proj_ps[rows_of(h)])
                leading.then_inc(proj_hi_ready, 1)
                dve.wait_ge(proj_hi_ready, count + 1)
                pairs.subtract_leading(a, u, proj_ps)

            def copy_outputs(p, a, qb):
                dve.wait_ge(pv_done, p * NS + LAST[qb] + 1)
                if PLACE[qb] == 0:
                    wait(dve, normed, (p - 1) * NB)
                nc.vector.tensor_copy(out_t[a][:, blk(qb)], o_ps[:, PLACE[qb] % 2]).then_inc(out_copied, 1)

            def copy_denominators(p, a, qb):
                place = PLACE[qb]
                dve.wait_ge(den_computed, p * NB + place + 1)
                wait(dve, den_stored[place % 2], (p * (NB // 2) + place // 2) * 16)
                nc.vector.tensor_copy(den_row[:, place % 2], den_ps[:]).then_inc(den_copied, 1)

            def add_outputs(p, b):
                dve.wait_ge(y_computed, (p - 1) * NB + b + 1)
                nc.vector.tensor_tensor(x[:, blk(b)], x[:, blk(b)], proj_ps[:], ALU.add).then_inc(y_added, 1)

            def factors(p):
                dve.wait_ge(den_loaded, p * 32)
                nc.vector.reciprocal(rden[:], den_r[:]).then_inc(rden_ready, 1)
                dve.wait_ge(rden_ready, p)
                wait(dve, factor_stored, (p - 1) * 16)
                nc.vector.tensor_tensor(factor[:], rden[:], gate_r[:], ALU.mult).then_inc(factor_ready, 1)

            def pair(p, a, last):
                for n in range(NS):
                    sum_probs(p, p * NS + n, n)
                    if not last:
                        if n == SPLIT_AT:
                            split_weights(p + 1)
                        if n in PROJ_AT:
                            if n == min(PROJ_AT):
                                wait(dve, scores_ready, p * NS)
                            split_projection((p + 1) * UNITS + PROJ_AT[n], 1 - a, PROJ_AT[n])
                    if n == FACTOR_AT and not is_first(p):
                        factors(p)
                    if n in Y_AT and not is_first(p):
                        add_outputs(p, Y_AT[n])
                    finish(p, a, n)

            def divide(qb):
                place, done = PLACE[qb], (PAIRS - 1) * NB + PLACE[qb] + 1
                rden, outputs = den_row[:, place % 2], out_t[1][:, blk(qb)]
                dve.wait_ge(den_computed, done)
                dve.wait_ge(den_stored[place % 2], 16 * NB // 2 * (PAIRS - 1))
                nc.vector.reciprocal(rden, den_ps[:]).then_inc(den_copied, 1)
                dve.wait_ge(gate_loaded, 32)
                dve.wait_ge(den_copied, done)
                nc.vector.tensor_tensor(rden, rden, gate_b[:, blk(qb)], ALU.mult).then_inc(gated, 1)
                dve.wait_ge(gated, place + 1)
                dve.wait_ge(out_copied, done)
                nc.vector.tensor_tensor(outputs, outputs, rden, ALU.mult).then_inc(divided, 1)

            def finish(p, a, n):
                for block_done in due(p, a, n, OUT_LAG):
                    copy_outputs(*block_done)
                for of, parity, qb in due(p, a, n, DEN_COPY_LAG):
                    if isinstance(of, int) and of == PAIRS - 1:
                        divide(qb)
                    else:
                        copy_denominators(of, parity, qb)

            run_pairs(dve, pair)
            for n in range(NS):
                finish(PAIRS, 0, n)
            for place, qb in enumerate(blocks_in_place()):
                dve.wait_ge(y_computed, (PAIRS - 1) * NB + place + 1)
                nc.vector.tensor_tensor(x[:, blk(qb)], x[:, blk(qb)], scores[:, place // 2, place % 2], ALU.add)


ROUTED = 8
EXPERTS = 1 + ROUTED
TOP_K = 2
HID = 256
CHUNKS = HID // P
UPB = EXPERTS * CHUNKS
RH = 6
RG = 3
LEAD = 3


SPLIT_LEAD = 3


class MixtureWeights:

    def __init__(self, ctx, nc, sems):
        sb = lambda n, s, d=F32: ctx.enter_context(nc.sbuf_tensor(f"mw_{n}", s, d))
        self.nc = nc
        self.gu_hi, self.gu_lo = sb("gu_hi", [P, EXPERTS, 2, HID], F32R), sb("gu_lo", [P, EXPERTS, 2, HID], F32R)
        self.d_hi, self.d_lo = sb("d_hi", [P, EXPERTS, CHUNKS, P], F32R), sb("d_lo", [P, EXPERTS, CHUNKS, P], F32R)
        self.router = sb("router", [P, ROUTED])
        self.bias = sb("bias", [P, ROUTED])
        self.ident = sb("ident", [P, P])
        self.before = sb("before", [P, ROUTED, ROUTED])
        self.router_loaded, self.ones_ready = sems("mw", "router_loaded"), sems("mw", "ones_ready")
        self.ident_ready, self.before_ready = sems("mw", "ident_ready"), sems("mw", "before_ready")
        self.loaded = [sems("mw", f"loaded{e}") for e in range(EXPERTS)]
        self.hi_ready, self.split = sems("mw", "hi_ready"), sems("mw", "split")

    def allocate_raw(self, ctx):
        self.gu = ctx.enter_context(self.nc.sbuf_tensor("mw_gu", [P, EXPERTS, 2, HID], F32))
        self.d = ctx.enter_context(self.nc.sbuf_tensor("mw_d", [P, EXPERTS, CHUNKS, P], F32))

    def load(self, sp, wg_t, wu_t, wd_t, wr_t, rb):
        sp.dma_start(self.router[:], wr_t).then_inc(self.router_loaded, 16)
        sp.dma_start(self.bias[:], rb.unsqueeze(0).broadcast_to([P, ROUTED])).then_inc(self.router_loaded, 16)
        for e in range(EXPERTS):
            sp.dma_start(self.gu[:, e, 0], wg_t[e]).then_inc(self.loaded[e], 16)
            sp.dma_start(self.gu[:, e, 1], wu_t[e]).then_inc(self.loaded[e], 16)
            sp.dma_start(self.d[:, e], wd_t[e].rearrange("(c i) h -> i c h", c=CHUNKS)).then_inc(self.loaded[e], 16)

    def lead(self, act, e):
        act.wait_ge(self.loaded[e], 48)
        self.nc.scalar.copy(self.gu_hi[:, e], self.gu[:, e]).then_inc(self.hi_ready, 1)
        self.nc.scalar.copy(self.d_hi[:, e], self.d[:, e]).then_inc(self.hi_ready, 1)

    def rest(self, dve, e):
        dve.wait_ge(self.hi_ready, 2 * e + 2)
        self.nc.vector.tensor_tensor(self.gu_lo[:, e], self.gu[:, e], self.gu_hi[:, e].bitcast(F32), ALU.subtract).then_inc(self.split, 1)
        self.nc.vector.tensor_tensor(self.d_lo[:, e], self.d[:, e], self.d_hi[:, e].bitcast(F32), ALU.subtract).then_inc(self.split, 1)

    def make_constants(self, pool):
        self.nc.gpsimd.memset(self.before[:], 1.0).then_inc(self.ones_ready, 1)
        self.nc.gpsimd.memset(self.ident[:], 1.0).then_inc(self.ones_ready, 1)
        pool.wait_ge(self.ones_ready, 2)
        self.nc.gpsimd.affine_select(out=self.before[:], in_=self.before[:], pattern=[[1, ROUTED], [-1, ROUTED]], compare_op=ALU.is_gt,
                                     fill=0.0, base=0, channel_multiplier=0).then_inc(self.before_ready, 1)
        self.nc.gpsimd.affine_select(out=self.ident[:], in_=self.ident[:], pattern=[[1, P]], compare_op=ALU.is_equal, fill=0.0,
                                     base=0, channel_multiplier=-1).then_inc(self.ident_ready, 1)


def experts(nc, sems, x, x_hi, x_lo, weights, probs, cw_dram, name, split, out):
    with ExitStack() as ctx:
        sb = lambda n, s, d=F32: ctx.enter_context(nc.sbuf_tensor(f"{name}_{n}", s, d))
        sem = lambda n: sems("ex", n)
        E = ROUTED
        above = sb("above", [P, NT, E, E])
        equal = sb("equal", [P, NT, E, E])
        rank = sb("rank", [P, NT, E])
        cw_n = sb("cw_n", [P, E, NT])
        cw_t = sb("cw_t", [E * NT, P])
        silu = sb("silu", [P, RG, BLK])
        hid = sb("hid", [P, RG, BLK])
        hid_hi = sb("hid_hi", [P, RH, BLK], F32R)
        hid_lo = sb("hid_lo", [P, RH, BLK], F32R)
        weighted = sb("weighted", [P, RG, BLK])
        cw = sb("cw", [P, E, BLK])
        gate_ps = ctx.enter_context(nc.psum_tensor(f"{name}_gate_ps", [P, RG, BLK], F32))
        up_ps = ctx.enter_context(nc.psum_tensor(f"{name}_up_ps", [P, RG, BLK], F32))
        down_ps = ctx.enter_context(nc.psum_tensor(f"{name}_down_ps", [P, 1, BLK], F32))
        route_ps = ctx.enter_context(nc.psum_tensor(f"{name}_route_ps", [E * NT, P], F32))
        compared, step, cw_ready, cw_turned, cw_copied, stored = sem("compared"), sem("step"), sem("cw_ready"), sem("cw_turned"), sem("cw_copied"), sem("stored")
        cw_loaded = [sem(f"cw_loaded{e}") for e in range(1, EXPERTS)]
        gate_ready, up_ready, silu_ready, hid_ready = sem("gate_ready"), sem("up_ready"), sem("silu_ready"), sem("hid_ready")
        hi_ready, lo_ready, down_ready, scaled, added = sem("hi_ready"), sem("lo_ready"), sem("down_ready"), sem("scaled"), sem("added")
        block = ctx.enter_context(nc.Block())

        def run_blocks(eng, body):
            body(0, True, False)
            with eng.Fori(1, NB - 1) as b:
                body(b, False, False)
            body(NB - 1, False, True)

        @block.sync
        def _(sp):
            def load(b, e):
                sp.dma_start(cw[:, e - 1], cw_dram[e - 1:e, bass.ds(b * BLK, BLK)].broadcast_to([P, BLK])).then_inc(cw_loaded[e - 1], 16)

            def store(b):
                sp.wait_ge(added, (b + 1) * EXPERTS)
                sp.dma_start(out[0][:, bass.ds(b * BLK, BLK)], x[:, bass.ds(b * BLK, BLK)]).then_inc(out[1], 16)

            sp.wait_ge(cw_copied, 1)
            sp.dma_start(cw_dram.rearrange("e (t k) -> (e t) k", k=P), cw_t[:]).then_inc(stored, 16)
            sp.wait_ge(stored, 16)
            for e in range(1, EXPERTS):
                load(0, e)
            with sp.Fori(0, NB - 1) as b:
                for e in range(1, EXPERTS):
                    sp.wait_ge(scaled, b * EXPERTS + e + 1)
                    load(b + 1, e)
                if out:
                    store(b)
            if out:
                store(NB - 1)
                sp.wait_ge(out[1], 16 * NB)

        @block.tensor
        def _(pe):
            def gate_up(b, i):
                e, c = i // CHUNKS, i % CHUNKS
                wait(pe, hid_ready, b * UPB + i - RG + 1)
                if split and isinstance(b, int) and b == 0:
                    pe.wait_ge(weights.split, 2 * e + 2)
                xs_hi, xs_lo = x_hi[:, bass.ds(b * BLK, BLK)], x_lo[:, bass.ds(b * BLK, BLK)]
                for which, out, ready in ((0, gate_ps, gate_ready), (1, up_ps, up_ready)):
                    out = out[:, i % RG]
                    hi, lo = weights.gu_hi[:, e, which, blk(c, P)], weights.gu_lo[:, e, which, blk(c, P)]
                    nc.tensor.matmul(out, hi, xs_hi, start=True, stop=False)
                    nc.tensor.matmul(out, hi, xs_lo, start=False, stop=False)
                    nc.tensor.matmul(out, lo, xs_hi, start=False, stop=True).then_inc(ready, 1)

            def down(b, e):
                wait(pe, scaled, b * EXPERTS + e)
                for c in range(CHUNKS):
                    i = e * CHUNKS + c
                    hi, lo = weights.d_hi[:, e, c], weights.d_lo[:, e, c]
                    wait(pe, hi_ready, b * UPB + i + 1)
                    nc.tensor.matmul(down_ps[:, 0], hi, hid_hi[:, i % RH], start=(c == 0), stop=False)
                    nc.tensor.matmul(down_ps[:, 0], lo, hid_hi[:, i % RH], start=False, stop=False)
                    wait(pe, lo_ready, b * UPB + i + 1)
                    mm = nc.tensor.matmul(down_ps[:, 0], hi, hid_lo[:, i % RH], start=False, stop=(c == CHUNKS - 1))
                mm.then_inc(down_ready, 1)

            def body(b, first, last):
                for i in range(UPB):
                    if i + LEAD < UPB:
                        gate_up(b, i + LEAD)
                    elif not last:
                        gate_up(b + 1, i + LEAD - UPB)
                    if i % CHUNKS == CHUNKS - 1:
                        down(b, i // CHUNKS)

            for i in range(LEAD):
                gate_up(0, i)
            pe.wait_ge(weights.ident_ready, 1)
            pe.wait_ge(cw_ready, 1)
            nc.tensor.transpose(route_ps[:], cw_n[:].rearrange("p e t -> p (e t)"), weights.ident[:]).then_inc(cw_turned, 1)
            run_blocks(pe, body)

        @block.scalar
        def _(act):
            def silu_of(b, i):
                wait(act, gate_ready, b * UPB + i + 1)
                wait(act, hid_ready, b * UPB + i - RG + 1)
                nc.scalar.activation(silu[:, i % RG], gate_ps[:, i % RG], ACT.Silu).then_inc(silu_ready, 1)

            def body(b, first, last):
                for i in range(UPB):
                    if i + 1 < UPB:
                        silu_of(b, i + 1)
                    elif not last:
                        silu_of(b + 1, 0)
                    wait(act, hid_ready, b * UPB + i + 1)
                    wait(act, down_ready, b * EXPERTS + (i - RH) // CHUNKS + 1)
                    nc.scalar.copy(hid_hi[:, i % RH], hid[:, i % RG]).then_inc(hi_ready, 1)
                    if split and first and i % CHUNKS == 0 and i // CHUNKS + SPLIT_LEAD < EXPERTS:
                        weights.lead(act, i // CHUNKS + SPLIT_LEAD)

            silu_of(0, 0)
            run_blocks(act, body)

        @block.vector
        def _(dve):
            def hidden(b, i):
                wait(dve, up_ready, b * UPB + i + 1)
                wait(dve, silu_ready, b * UPB + i + 1)
                wait(dve, hi_ready, b * UPB + i - RG + 1)
                wait(dve, lo_ready, b * UPB + i - RG + 1)
                nc.vector.tensor_tensor(hid[:, i % RG], silu[:, i % RG], up_ps[:, i % RG], ALU.mult).then_inc(hid_ready, 1)

            def scale(b, e):
                wait(dve, down_ready, b * EXPERTS + e + 1)
                wait(dve, added, b * EXPERTS + e - RG + 1)
                if e == 0:
                    nc.vector.tensor_copy(weighted[:, e % RG], down_ps[:, 0]).then_inc(scaled, 1)
                else:
                    wait(dve, cw_loaded[e - 1], b * 16 + 16)
                    nc.vector.tensor_tensor(weighted[:, e % RG], cw[:, e - 1], down_ps[:, 0], ALU.mult).then_inc(scaled, 1)

            def body(b, first, last):
                for i in range(UPB):
                    if i + 1 < UPB:
                        hidden(b, i + 1)
                    elif not last:
                        hidden(b + 1, 0)
                    wait(dve, hi_ready, b * UPB + i + 1)
                    wait(dve, down_ready, b * EXPERTS + (i - RH) // CHUNKS + 1)
                    nc.vector.tensor_tensor(hid_lo[:, i % RH], hid[:, i % RG], hid_hi[:, i % RH].bitcast(F32), ALU.subtract).then_inc(lo_ready, 1)
                    if i % CHUNKS == 0 and i:
                        scale(b, i // CHUNKS - 1)
                    elif i == 0 and not first:
                        scale(b - 1, EXPERTS - 1)
                    if split and first and i % CHUNKS == 0 and i // CHUNKS + SPLIT_LEAD < EXPERTS:
                        weights.rest(dve, i // CHUNKS + SPLIT_LEAD)
                if last:
                    scale(b, EXPERTS - 1)

            this = probs[:].unsqueeze(3).broadcast_to([P, NT, E, E])
            other = probs[:].unsqueeze(2).broadcast_to([P, NT, E, E])
            nc.vector.tensor_tensor(above[:], other, this, ALU.is_gt).then_inc(compared, 1)
            nc.vector.tensor_tensor(equal[:], other, this, ALU.is_equal).then_inc(compared, 1)
            dve.wait_ge(weights.before_ready, 1)
            dve.wait_ge(compared, 2)
            nc.vector.tensor_tensor(equal[:], equal[:], weights.before[:].unsqueeze(1).broadcast_to([P, NT, E, E]), ALU.mult).then_inc(step, 1)
            dve.wait_ge(step, 1)
            nc.vector.tensor_tensor(above[:], above[:], equal[:], ALU.add).then_inc(step, 1)
            dve.wait_ge(step, 2)
            nc.vector.tensor_reduce(rank[:], above[:], AX.X, ALU.add).then_inc(step, 1)
            dve.wait_ge(step, 3)
            nc.vector.scalar_tensor_tensor(out=cw_n[:].rearrange("p e t -> p t e"), in0=rank[:], scalar=float(TOP_K), in1=probs[:],
                                           op0=ALU.is_lt, op1=ALU.mult).then_inc(cw_ready, 1)
            dve.wait_ge(cw_turned, 1)
            nc.vector.tensor_copy(cw_t[:], route_ps[:]).then_inc(cw_copied, 1)
            hidden(0, 0)
            run_blocks(dve, body)

        @block.gpsimd
        def _(pool):
            for b in range(NB):
                for e in range(EXPERTS):
                    xs = x[:, blk(b)]
                    pool.wait_ge(scaled, b * EXPERTS + e + 1)
                    wait(pool, added, b * EXPERTS + e)
                    nc.gpsimd.tensor_tensor(xs, xs, weighted[:, e % RG], ALU.add).then_inc(added, 1)


HB = 16
DB = P // HB
PAD = 32
GROUPS = HB * PAD // P
PER_G = HB // GROUPS
STACK = 4


class LinearWeights:

    def __init__(self, ctx, nc, sems):
        sb = lambda n, s: ctx.enter_context(nc.sbuf_tensor(f"lw_{n}", s, F32))
        self.nat = sb("nat", [P, 3, P])
        self.bias_c = sb("bias_c", [P, 2])
        self.bo_c = sb("bo_c", [P, 1])
        self.bkv_r = sb("bkv_r", [P, 2, P])
        self.loaded = sems("lw", "loaded")

    def load(self, sp, wq_t, wk_t, wv_t, bq, bk, bv, bo):
        for i, src in enumerate((wq_t, wk_t, wv_t)):
            sp.dma_start(self.nat[:, i], src).then_inc(self.loaded, 16)
        for i, src in enumerate((bq, bk)):
            sp.dma_start(self.bias_c[:, i:i + 1], src.unsqueeze(1)).then_inc(self.loaded, 16)
        sp.dma_start(self.bo_c[:], bo.unsqueeze(1)).then_inc(self.loaded, 16)
        for i, src in enumerate((bk, bv)):
            sp.dma_start(self.bkv_r[:, i], src.unsqueeze(0).broadcast_to([P, P])).then_inc(self.loaded, 16)
        sp.wait_ge(self.loaded, 16 * 8)


def linear_attention(nc, sems, x, xn, w, wo_t):
    with ExitStack() as ctx:
        sb_in = lambda c, n, s, d=F32: c.enter_context(nc.sbuf_tensor(f"la_{n}", s, d))
        sb = lambda n, s, d=F32: sb_in(ctx, n, s, d)
        psum = lambda c, n, s: c.enter_context(nc.psum_tensor(f"la_{n}", s, F32))
        sem = lambda n: sems("la", n)
        wo = sb("wo", [P, P])
        q_t = sb("q_t", [P, T])
        q_st = sb("q_st", [P, GROUPS, T], F32R)
        k_st = sb("k_st", [P, GROUPS, T], F32R)
        kv_n = sb("kv_n", [P, NT, 2, P])
        ones = sb("ones", [P, HB])
        own_lo, own = sb("own_lo", [P, HB]), sb("own", [P, HB])
        own_st = sb("own_st", [P, PER_G])
        out_t = sb("out_t", [P, 2, BLK])

        const_ready, wo_loaded, own_lo_ready = sem("const_ready"), sem("wo_loaded"), sem("own_lo_ready")
        own_ready, own_st_ready, pick_ready, picks_ready = sem("own_ready"), sem("own_st_ready"), sem("pick_ready"), sem("picks_ready")
        nat_computed, nat_ready, nat_hi_ready, nat_split = sem("nat_computed"), sem("nat_ready"), sem("nat_hi_ready"), sem("nat_split")
        st_computed, st_copied_act, st_copied_dve = sem("st_computed"), sem("st_copied_act"), sem("st_copied_dve")
        kv_computed, kv_ready = sem("kv_computed"), sem("kv_ready")

        BANKS = 4
        stacks = [(i, g) for g in range(GROUPS) for i in range(2)]
        NST = len(stacks)
        KV_AFTER = {2 * i + 1: i for i in range(BLK // P)}
        by_dve = lambda n: n % BANKS == BANKS - 1

        with ExitStack() as c:
            nat = sb_in(c, "nat_k", [P, 2, BLK])
            nat_hi, nat_lo = sb_in(c, "nat_hi", [P, 2, 2, BLK], F32R), sb_in(c, "nat_lo", [P, 2, 2, BLK], F32R)
            pick = sb_in(c, "pick", [P, GROUPS, STACK, PAD])
            which = sb_in(c, "which", [P, 2, 2, STACK])
            picks = sb_in(c, "picks", [P, 2, 2, GROUPS, STACK, PAD], F32R)
            nat_ps = psum(c, "nat_ps", [P, 2, BLK])
            st_ps = psum(c, "st_ps", [P, BANKS, BLK])
            kv_ps = psum(c, "kv_ps", [P, 2, BLK])
            block = c.enter_context(nc.Block())

            def natural(b, i):
                return (q_t[:, blk(b)], nat[:, b % 2])[i]

            @block.gpsimd
            def _(pool):
                nc.gpsimd.memset(ones[:], 1.0).then_inc(const_ready, 1)
                nc.gpsimd.memset(pick[:], 1.0).then_inc(const_ready, 1)
                nc.gpsimd.memset(which[:], 0.0).then_inc(const_ready, 1)
                pool.wait_ge(const_ready, 3)
                nc.gpsimd.affine_select(out=pick[:], in_=pick[:], pattern=[[-PAD, GROUPS], [0, STACK], [-1, PAD]], compare_op=ALU.is_equal,
                                        fill=0.0, base=0, channel_multiplier=1).then_inc(pick_ready, 1)
                nc.gpsimd.memset(which[:, 0, 0, 0:2], 1.0).then_inc(pick_ready, 1)
                nc.gpsimd.memset(which[:, 0, 1, 2:4], 1.0).then_inc(pick_ready, 1)
                nc.gpsimd.memset(which[:, 1, 0, 0:4:2], 1.0).then_inc(pick_ready, 1)
                nc.gpsimd.memset(which[:, 1, 1, 1:4:2], 1.0).then_inc(pick_ready, 1)
                nc.gpsimd.affine_select(out=own_lo[:], in_=ones[:], pattern=[[-DB, HB]], compare_op=ALU.is_ge, fill=0.0,
                                        base=0, channel_multiplier=1).then_inc(own_lo_ready, 1)
                pool.wait_ge(own_lo_ready, 1)
                nc.gpsimd.affine_select(out=own[:], in_=own_lo[:], pattern=[[DB, HB]], compare_op=ALU.is_gt, fill=0.0,
                                        base=DB, channel_multiplier=-1).then_inc(own_ready, 1)
                sems.clear(pool, "ln1", "ex")

            @block.sync
            def _(sp):
                for j in range(PER_G):
                    for g in range(GROUPS):
                        at, head = j * PAD + g * DB, g * PER_G + j
                        sp.dma_start(wo[at:at + DB], wo_t[head * DB:(head + 1) * DB]).then_inc(wo_loaded, 16)
                sp.wait_ge(wo_loaded, 16 * HB)

            @block.tensor
            def _(pe):
                def project(b):
                    for i in range(2):
                        if b > 0:
                            pe.wait_ge(nat_ready, 2 * (b - 1) + i + 1)
                        nc.tensor.matmul(nat_ps[:, i], w.nat[:, i], xn[:, blk(b)], start=True, stop=True).then_inc(nat_computed, 1)

                def keys_and_values(t):
                    if t >= 2:
                        pe.wait_ge(kv_ready, t - 1)
                    nc.tensor.matmul(kv_ps[:, t % 2, 0:2 * P], xn[:, blk(t, P)], w.nat[:, 1:3].rearrange("p w d -> p (w d)"),
                                     start=True, stop=True).then_inc(kv_computed, 1)

                project(0)
                for b in range(NB):
                    if b + 1 < NB:
                        project(b + 1)
                    for s, (i, g) in enumerate(stacks):
                        n = b * NST + s
                        if n == 0:
                            pe.wait_ge(picks_ready, 4)
                        if s < 2:
                            pe.wait_ge(nat_split, 2 * b + i + 1)
                        before = n - BANKS
                        if before >= 0 and by_dve(before):
                            pe.wait_ge(st_copied_dve, before // BANKS + 1)
                        elif before >= 0:
                            pe.wait_ge(st_copied_act, before // BANKS * (BANKS - 1) + before % BANKS + 1)
                        for part, values in enumerate((nat_hi, nat_lo)):
                            mm = nc.tensor.matmul(st_ps[:, n % BANKS], picks[:, i, part, g].rearrange("p r d -> p (r d)"), values[:, b % 2, i],
                                                  start=(part == 0), stop=(part == 1))
                        mm.then_inc(st_computed, 1)
                        if s in KV_AFTER:
                            keys_and_values(b * BLK // P + KV_AFTER[s])

            def copy_stack(b, s, engine_copy):
                i, g = stacks[s]
                return engine_copy((q_st, k_st)[i][:, g, blk(b)], st_ps[:, (b * NST + s) % BANKS])

            @block.scalar
            def _(act):
                def add_bias(b):
                    for i in range(2):
                        act.wait_ge(nat_computed, 2 * b + i + 1)
                        if i == 1 and b >= 2:
                            act.wait_ge(nat_split, 2 * (b - 2) + 2)
                        nc.scalar.activation(natural(b, i), nat_ps[:, i], ACT.Identity, bias=w.bias_c[:, i:i + 1]).then_inc(nat_ready, 1)

                add_bias(0)
                for b in range(NB):
                    if b + 1 < NB:
                        add_bias(b + 1)
                    for s in range(NST):
                        n = b * NST + s
                        if not by_dve(n):
                            act.wait_ge(st_computed, n + 1)
                            copy_stack(b, s, nc.scalar.copy).then_inc(st_copied_act, 1)

            @block.vector
            def _(dve):
                def split(b):
                    for i in range(2):
                        dve.wait_ge(nat_ready, 2 * b + i + 1)
                        if b >= 2:
                            dve.wait_ge(st_computed, (b - 1) * NST)
                        nc.vector.tensor_copy(nat_hi[:, b % 2, i], natural(b, i)).then_inc(nat_hi_ready, 1)
                        dve.wait_ge(nat_hi_ready, 2 * b + i + 1)
                        nc.vector.tensor_tensor(nat_lo[:, b % 2, i], natural(b, i), nat_hi[:, b % 2, i].bitcast(F32), ALU.subtract).then_inc(nat_split, 1)

                def add_bias(t):
                    dve.wait_ge(kv_computed, t + 1)
                    nc.vector.tensor_tensor(kv_n[:, t], w.bkv_r[:], kv_ps[:, t % 2, 0:2 * P].rearrange("p (w d) -> p w d", w=2), ALU.add).then_inc(kv_ready, 1)

                dve.wait_ge(pick_ready, 5)
                shape = [P, GROUPS, STACK, PAD]
                for i in range(2):
                    for part in range(2):
                        nc.vector.tensor_tensor(picks[:, i, part], pick[:], which[:, i, part].unsqueeze(1).unsqueeze(3).broadcast_to(shape),
                                                ALU.mult).then_inc(picks_ready, 1)
                split(0)
                for b in range(NB):
                    if b + 1 < NB:
                        split(b + 1)
                    for s in range(NST):
                        n = b * NST + s
                        if by_dve(n):
                            dve.wait_ge(st_computed, n + 1)
                            copy_stack(b, s, nc.vector.tensor_copy).then_inc(st_copied_dve, 1)
                        if s in KV_AFTER:
                            add_bias(b * BLK // P + KV_AFTER[s])
                dve.wait_ge(own_ready, 1)
                nc.vector.tensor_reduce(own_st[:], own[:].rearrange("p (r j) -> p j r", j=PER_G), AX.X, ALU.add).then_inc(own_st_ready, 1)

        SB = HB * P // BLK
        scores_ready, scores_copied, q_x_ready, masked_ready = sem("scores_ready"), sem("scores_copied"), sem("q_x_ready"), sem("masked_ready")
        sums_ready, state_ready, out_ready, out_copied, y_ready, y_added = sem("sums_ready"), sem("state_ready"), sem("out_ready"), sem("out_copied"), sem("y_ready"), sem("y_added")
        state_zeroed, v_wide_ready = sem("state_zeroed"), sem("v_wide_ready")
        PER_Y = BLK // P
        with ExitStack() as c:
            q_x = sb_in(c, "q_x", [P, 2, GROUPS, PER_G, P], F32R)
            masked = sb_in(c, "masked", [P, 2, HB, P])
            state = sb_in(c, "state", [P, 2, P])
            v_wide = sb_in(c, "v_wide", [P, 2, GROUPS * (P + DB)])
            scores = psum(c, "scores", [P, HB, P])
            out_ps = psum(c, "out_ps", [P, 2, BLK])
            sums = psum(c, "sums", [P, HB, DB])
            y_ps = psum(c, "y_ps", [P, BLK])
            block = c.enter_context(nc.Block())

            @block.tensor
            def _(pe):
                def scores_of(t):
                    pe.wait_ge(q_x_ready, (t + 1) * PER_G)
                    for g in range(GROUPS):
                        if t > 0:
                            pe.wait_ge(scores_copied, (t - 1) * SB + g + 1)
                        nc.tensor.matmul(scores[:, g * PER_G:(g + 1) * PER_G], k_st[:, g, blk(t, P)], q_x[:, t % 2, g],
                                         start=True, stop=True).then_inc(scores_ready, 1)

                def outputs_of(t):
                    if t >= 2:
                        pe.wait_ge(out_copied, t - 1)
                    if t > 0:
                        pe.wait_ge(state_ready, t)
                    nc.tensor.matmul(out_ps[:, t % 2, 0:P], state[:, t % 2], q_t[:, blk(t, P)], start=True, stop=False, skip_group_check=True)
                    pe.wait_ge(v_wide_ready, t + 1)
                    for g in range(GROUPS):
                        pe.wait_ge(masked_ready, t * SB + g + 1)
                        for j in range(PER_G):
                            h = g * PER_G + j
                            mm = nc.tensor.matmul(out_ps[j * PAD:(j + 1) * PAD, t % 2, 0:P], v_wide[:, t % 2, blk(h, PAD)], masked[:, t % 2, h],
                                                  start=False, stop=(g == GROUPS - 1), skip_group_check=True)
                    mm.then_inc(out_ready, 1)

                def project(b):
                    pe.wait_ge(out_copied, (b + 1) * PER_Y)
                    if b > 0:
                        pe.wait_ge(y_added, b)
                    nc.tensor.matmul(y_ps[:], wo[:], out_t[:, b % 2], start=True, stop=True).then_inc(y_ready, 1)

                scores_of(0)
                pe.wait_ge(state_zeroed, 2)
                for t in range(NT):
                    if t + 1 < NT:
                        if t > 0:
                            pe.wait_ge(state_ready, t)
                        nc.tensor.matmul(sums[:].rearrange("p h d -> p (h d)"), kv_n[:, t, 0], kv_n[:, t, 1], start=(t == 0),
                                         stop=True, skip_group_check=True).then_inc(sums_ready, 1)
                        scores_of(t + 1)
                    outputs_of(t)
                    if t % PER_Y == 0 and t > 0:
                        project(t // PER_Y - 1)
                project(NB - 1)

            @block.scalar
            def _(act):
                act.wait_ge(state_zeroed, 2)
                for t in range(NT):
                    if t >= 2:
                        act.wait_ge(out_ready, t - 1)
                    wide = v_wide[:, t % 2].rearrange("p (g x) -> p g x", g=GROUPS)[:, :, 0:P].rearrange("p g (j m) -> p g j m", j=PER_G)
                    nc.scalar.copy(wide[:, :, :, 0:DB], kv_n[:, t, 1].rearrange("p (g j d) -> p g j d", g=GROUPS, j=PER_G)).then_inc(v_wide_ready, 1)
                    for g in range(GROUPS):
                        act.wait_ge(scores_ready, t * SB + g + 1)
                        if t >= 2 and g == 0:
                            act.wait_ge(out_ready, t - 1)
                        heads = slice(g * PER_G, (g + 1) * PER_G)
                        nc.scalar.copy(masked[:, t % 2, heads], scores[:, heads]).then_inc(scores_copied, 1)

            @block.gpsimd
            def _(pool):
                nc.gpsimd.memset(v_wide[:], 0.0).then_inc(state_zeroed, 1)
                nc.gpsimd.memset(state[:], 0.0).then_inc(state_zeroed, 1)
                for t in range(NT):
                    for g in range(GROUPS):
                        pool.wait_ge(scores_copied, t * SB + g + 1)
                        m = masked[:, t % 2, g * PER_G:(g + 1) * PER_G]
                        nc.gpsimd.affine_select(out=m, in_=m, pattern=[[0, PER_G], [1, P]], compare_op=ALU.is_ge, fill=0.0, base=0,
                                                channel_multiplier=-1).then_inc(masked_ready, 1)

            @block.vector
            def _(dve):
                def spread(t):
                    if t >= 2:
                        dve.wait_ge(scores_ready, (t - 1) * SB)
                    for j in range(PER_G):
                        nc.vector.tensor_scalar(out=q_x[:, t % 2, :, j], in0=q_st[:, :, blk(t, P)].bitcast(F32), scalar1=own_st[:, j:j + 1],
                                                scalar2=None, op0=ALU.mult).then_inc(q_x_ready, 1)

                def add(b):
                    dve.wait_ge(y_ready, b + 1)
                    nc.vector.scalar_tensor_tensor(out=x[:, blk(b)], in0=y_ps[:], scalar=w.bo_c[:, 0:1], in1=x[:, blk(b)],
                                                   op0=ALU.add, op1=ALU.add).then_inc(y_added, 1)

                spread(0)
                spread(1)
                dve.wait_ge(state_zeroed, 2)
                for t in range(NT):
                    if t + 1 < NT:
                        dve.wait_ge(sums_ready, t + 1)
                        if t > 0:
                            dve.wait_ge(out_ready, t)
                        nc.vector.tensor_tensor(state[:, (t + 1) % 2].rearrange("p (j g d) -> p g j d", g=GROUPS, j=PER_G),
                                                sums[:].rearrange("p (g j) d -> p g j d", g=GROUPS),
                                                own[:].rearrange("p (g j) -> p g j", g=GROUPS).unsqueeze(3).broadcast_to([P, GROUPS, PER_G, DB]),
                                                ALU.mult).then_inc(state_ready, 1)
                    if t + 2 < NT:
                        spread(t + 2)
                    dve.wait_ge(out_ready, t + 1)
                    b = t // PER_Y
                    if b >= 2:
                        dve.wait_ge(y_ready, b - 1)
                    nc.vector.tensor_copy(out_t[:, b % 2, blk(t % PER_Y, P)], out_ps[:, t % 2, 0:P]).then_inc(out_copied, 1)
                    if t % PER_Y == 0 and t > 0:
                        add(t // PER_Y - 1)
                add(NB - 1)


def program(nc, x_t, w_qkv, w_gates, w_out, wq_t, bq, wk_t, bk, wv_t, bv, wo_t, bo, wg_t, wu_t, wd_t, wr_t, rb, out_t):
    dram = lambda n, s: nc.dram_tensor(n, s, F32).ap()
    v_dram = dram("v_dram", [PAIRS, P, NT, P])
    gate_dram = dram("gate_dram", [PAIRS, 2, T])
    den_dram = dram("den_dram", [PAIRS, 3, T])
    factor_dram = dram("factor_dram", [2, T])
    cw_dram = [dram(f"cw_dram{i}", [ROUTED, T]) for i in range(2)]
    with ExitStack() as ctx:
        sb_in = lambda c, n, s, d=F32: c.enter_context(nc.sbuf_tensor(n, s, d))
        parts_in = lambda c, n: (sb_in(c, f"{n}_hi", [P, T], F32R), sb_in(c, f"{n}_lo", [P, T], F32R))
        x = sb_in(ctx, "x", [P, T])
        sems = Semaphores(nc, ctx)
        x_loaded, out_stored = [sems("io", f"x_loaded{b}") for b in range(NB)], sems("io", "out_stored")
        with ExitStack() as c:
            x_hi, x_lo = parts_in(c, "a")
            aw = AttentionWeights(c, nc, sems, w_qkv)

            def load(sp):
                for b in range(NB):
                    sp.dma_start(x[:, blk(b)], x_t[:, blk(b)]).then_inc(x_loaded[b], 16)
                aw.load_v(sp)
                aw.load_pair(sp, 0)

            def split(dve):
                aw.split_v(dve)
                aw.split_pair(dve, 0)

            pairs = Pairs(c, nc, sems)
            with ExitStack() as cv:
                xn = sb_in(cv, "xn_a", [P, T])
                aw.allocate_v(cv)
                layer_norm(nc, sems, "ln0", x, xn, x_hi, x_lo, "ln_a", x_loaded=x_loaded, beside={"sync": load, "vector": split})
                values_and_gates(nc, sems, xn, x_hi, x_lo, aw, pairs, w_gates, v_dram, gate_dram)
            softcap_attention(nc, sems, x, x_hi, x_lo, aw, pairs, w_out, v_dram, gate_dram, den_dram, factor_dram)
        sb = lambda n, s, d: sb_in(ctx, n, s, d)
        xn = sb("xn", [P, T], F32)
        weights = MixtureWeights(ctx, nc, sems)

        def mixture(i, split, out=None):
            with ExitStack() as c:
                x_hi, x_lo = parts_in(c, f"f{i}")
                probs = sb_in(c, f"probs{i}", [P, NT, ROUTED])
                beside = None
                if split:
                    weights.allocate_raw(c)
                    beside = {"sync": lambda sp: weights.load(sp, wg_t, wu_t, wd_t, wr_t, rb), "gpsimd": weights.make_constants,
                              "scalar": lambda act: [weights.lead(act, e) for e in range(SPLIT_LEAD)],
                              "vector_end": lambda dve: [weights.rest(dve, e) for e in range(SPLIT_LEAD)]}
                layer_norm(nc, sems, "ln1", x, xn, x_hi, x_lo, f"ln_f{i}", beside=beside, router=(weights, probs))
                experts(nc, sems, x, x_hi, x_lo, weights, probs, cw_dram[i], f"ex{i}", split, out)

        mixture(0, True)
        with ExitStack() as c:
            lw = LinearWeights(c, nc, sems)
            layer_norm(nc, sems, "ln0", x, xn, None, None, "ln_b",
                       beside={"sync": lambda sp: lw.load(sp, wq_t, wk_t, wv_t, bq, bk, bv, bo)})
            linear_attention(nc, sems, x, xn, lw, wo_t)
        mixture(1, False, (out_t, out_stored))


def kernel(**inputs):
    import numpy as np
    import concourse.bacc as bacc
    from concourse.bass_utils import run_bass_kernel_spmd

    a = {n.removeprefix("L0_"): np.asarray(v) for n, v in inputs.items()}
    turn = lambda v: np.ascontiguousarray(np.swapaxes(v, -1, -2))
    both = lambda n: turn(np.concatenate([a[f"ffn_{n}_s"][None], a[f"ffn_{n}"]]))
    arrays = {"x_t": turn(a["attn_a_x"][0]), "w_qkv": a["attn_a_w_qkv"], "w_gates": a["attn_a_w_gates"], "w_out": a["attn_a_w_out"]}
    for n in "qkvo":
        arrays[f"w{n}_t"] = turn(a[f"attn_b_w{n}_w"])
        arrays[f"b{n}"] = a[f"attn_b_w{n}_b"]
    arrays |= {"wg_t": both("Wg"), "wu_t": both("Wu"), "wd_t": both("Wd"), "wr_t": turn(a["ffn_Wr"]), "rb": a["ffn_rb"]}
    arrays = {f"in_{n}": np.ascontiguousarray(v) for n, v in arrays.items()}

    nc = bacc.Bacc("TRN2", target_bir_lowering=False, num_devices=1)
    args = [nc.dram_tensor(n, v.shape, mybir.dt.from_np(v.dtype), kind="ExternalInput").ap() for n, v in arrays.items()]
    out = nc.dram_tensor("out_0", (P, T), F32, kind="ExternalOutput").ap()
    program(nc, *args, out)
    r = run_bass_kernel_spmd(nc, [arrays], core_ids=[0])
    return np.ascontiguousarray(r.results[0]["out_0"].T)[None]
```
